# Optimizing a Trainium2 kernel written in Bass

```python
import numpy as np
import jax
import jax.numpy as jnp

def _softmax(x, axis=-1):
    return jax.nn.softmax(x, axis=axis)

def _gelu(x):
    return jax.nn.gelu(x, approximate=True)

def _silu(x):
    return jax.nn.silu(x)

def _sigmoid(x):
    return jax.nn.sigmoid(x)

def _layernorm(x, axis=-1, eps=1e-05):
    m = jnp.mean(x, axis=axis, keepdims=True)
    v = jnp.var(x, axis=axis, keepdims=True)
    return (x - m) / jnp.sqrt(v + eps)

def _scatter_add(tgt, idx, src, axis=0):
    return tgt.at[idx].add(src)

def _segment_sum(src, seg, n):
    return jax.ops.segment_sum(src, seg, n)
kernel_name = 'mk_decoder_postln_d1_seqx_r2_c7537d'

def setup_inputs(seed: int=0):
    np.random.seed(seed)
    _w = jnp.asarray

    def _rec_inputs():
        import jax
        import jax.numpy as jnp
        _rk = jax.random.key(seed)
        x = -0.0002928 + 1 * jax.random.normal(jax.random.fold_in(_rk, 1), (2, 2048, 512), jnp.float32)
        _lenS = 2048 - jax.random.randint(jax.random.fold_in(_rk, 7), (2,), 0, max(1, 2048 // 4) + 1, jnp.int32)
        _lenS2 = 77 - jax.random.randint(jax.random.fold_in(_rk, 8), (2,), 0, max(1, 77 // 4) + 1, jnp.int32)
        _ctx_1024P = jax.random.normal(jax.random.fold_in(_rk, 11), (2, 16, 512), jnp.float32)
        _ctx_1024c = jax.random.dirichlet(jax.random.fold_in(_rk, 511), 0.3 * jnp.ones((16,), jnp.float32), (2, 77))
        _ctx_1024t = jnp.einsum('bsk,bkd->bsd', _ctx_1024c, _ctx_1024P)
        _ctx_1024t = _ctx_1024t * jax.lax.rsqrt(jnp.mean(jnp.square(_ctx_1024t)) + 1e-12) * 0.953939
        ctx_1024 = -1.39393e-06 + 0.999914 * (_ctx_1024t + 0.3 * jax.random.normal(jax.random.fold_in(_rk, 611), (2, 77, 512), jnp.float32))
        return (x, ctx_1024)
    x, ctx_1024 = _rec_inputs()

    def _L0_attn_setup():
        import jax, jax.numpy as jnp
        import numpy as np
        D_CONV = 4
        CHUNK = 64

        def segsum(x):
            T = x.shape[-1]
            strict = jnp.tril(jnp.ones((T, T), dtype=bool), -1)
            xr = jnp.where(strict, x[..., :, None], 0.0)
            x_segsum = jnp.cumsum(xr, axis=-2)
            return jnp.where(jnp.tril(jnp.ones((T, T), dtype=bool)), x_segsum, -jnp.inf)

        def ssd(x, A, B, C, chunk):
            b, s, h, p = x.shape
            c = s // chunk
            x = x.reshape(b, c, chunk, h, p)
            B = B.reshape(b, c, chunk, h, -1)
            C = C.reshape(b, c, chunk, h, -1)
            A = A.reshape(b, c, chunk, h).transpose(0, 3, 1, 2)
            A_cumsum = jnp.cumsum(A, axis=-1)
            L = jnp.exp(segsum(A))
            Y_diag = jnp.einsum('bclhn,bcshn,bhcls,bcshp->bclhp', C, B, L, x)
            decay_states = jnp.exp(A_cumsum[..., -1:] - A_cumsum)
            states = jnp.einsum('bclhn,bhcl,bclhp->bchpn', B, decay_states, x)
            states = jnp.concatenate([jnp.zeros_like(states[:, :1]), states], axis=1)
            A_last = jnp.pad(A_cumsum[..., -1], ((0, 0), (0, 0), (1, 0)))
            decay_chunk = jnp.exp(segsum(A_last))
            states = jnp.einsum('bhzc,bchpn->bzhpn', decay_chunk, states)[:, :-1]
            Y_off = jnp.einsum('bclhn,bchpn,bhcl->bclhp', C, states, jnp.exp(A_cumsum))
            return (Y_diag + Y_off).reshape(b, s, h, p)
        key = jax.random.key(seed)
        ks = jax.random.split(key, 6)
        d_model, d_state, d_inner, n_heads = (512, 512, 512, 16)
        d_in_proj = 2 * d_state + d_inner + n_heads
        d_conv_c = 2 * d_state + d_inner
        b, s = (4, 2048)

        def xavier(k, shape):
            bnd = float(np.sqrt(6.0 / (shape[0] + shape[1])))
            return jax.random.uniform(k, shape, minval=-bnd, maxval=bnd, dtype=jnp.float32)
        return {'x': jax.random.normal(ks[0], (b, s, d_model), dtype=jnp.float32), 'W_in': xavier(ks[1], (d_in_proj, d_model)), 'conv_w': jax.random.uniform(ks[2], (d_conv_c, D_CONV), minval=-0.8, maxval=0.8, dtype=jnp.float32), 'conv_b': jnp.zeros((d_conv_c,), dtype=jnp.float32), 'A_param': jax.random.uniform(ks[3], (16,), minval=-0.01, maxval=0.01, dtype=jnp.float32), 'dt_bias': jax.random.uniform(ks[4], (16,), minval=-0.1, maxval=0.1, dtype=jnp.float32), 'W_out': xavier(ks[5], (d_model, d_inner))}
    _L0_attn_all = _L0_attn_setup()
    _L0_attn_in = {k: v for k, v in _L0_attn_all.items() if k in ('W_in', 'conv_w', 'conv_b', 'A_param', 'dt_bias', 'W_out')}
    del _L0_attn_all

    def _L0_xattn_setup():
        import jax, jax.numpy as jnp
        import numpy as np
        N_EMBD = 512
        N_HEADS = 16
        HEAD_DIM = N_EMBD // N_HEADS
        key = jax.random.key(seed)
        ks = jax.random.split(key, 12)
        B, T, S, C = (2, 1024, 1024, N_EMBD)
        std = 1.0 / np.sqrt(C)
        inp = {'x': jax.random.normal(ks[0], (B, T, C), dtype=jnp.float32), 'context': jax.random.normal(ks[1], (B, S, C), dtype=jnp.float32), 'q_w': jax.random.uniform(ks[2], (C, C), minval=-std, maxval=std, dtype=jnp.float32), 'q_b': jax.random.uniform(ks[3], (C,), minval=-std, maxval=std, dtype=jnp.float32), 'k_w': jax.random.uniform(ks[4], (C, C), minval=-std, maxval=std, dtype=jnp.float32), 'k_b': jax.random.uniform(ks[5], (C,), minval=-std, maxval=std, dtype=jnp.float32), 'v_w': jax.random.uniform(ks[6], (C, C), minval=-std, maxval=std, dtype=jnp.float32), 'v_b': jax.random.uniform(ks[7], (C,), minval=-std, maxval=std, dtype=jnp.float32), 'o_w': jax.random.uniform(ks[8], (C, C), minval=-std, maxval=std, dtype=jnp.float32), 'o_b': jax.random.uniform(ks[9], (C,), minval=-std, maxval=std, dtype=jnp.float32)}
        return inp
    _L0_xattn_all = _L0_xattn_setup()
    _L0_xattn_in = {k: v for k, v in _L0_xattn_all.items() if k in ('q_w', 'q_b', 'k_w', 'k_b', 'v_w', 'v_b', 'o_w', 'o_b')}
    del _L0_xattn_all

    def _L0_ffn_setup():
        import jax, jax.numpy as jnp
        import numpy as np
        B, L, D = (4, 1024, 512)
        H = 16
        E = 16
        NS = 16
        S = NS // E
        F = 2048
        EPS = 1e-05

        def _layernorm(x, g, b):
            mu = jnp.mean(x, axis=-1, keepdims=True)
            var = jnp.mean(jnp.square(x - mu), axis=-1, keepdims=True)
            return (x - mu) * jax.lax.rsqrt(var + EPS) * g + b

        def _mha(q, k, v, Wq, bq, Wk, bk, Wv, bv, Wo, bo):
            Bq, Lq, Dm = q.shape
            dh = Dm // H
            qh = (q @ Wq + bq).reshape(Bq, Lq, H, dh)
            kh = (k @ Wk + bk).reshape(Bq, -1, H, dh)
            vh = (v @ Wv + bv).reshape(Bq, -1, H, dh)
            scores = jnp.einsum('bqhd,bkhd->bhqk', qh, kh) / jnp.asarray(np.sqrt(dh), q.dtype)
            attn = jax.nn.softmax(scores, axis=-1)
            out = jnp.einsum('bhqk,bkhd->bqhd', attn, vh).reshape(Bq, Lq, Dm)
            return out @ Wo + bo
        key = jax.random.key(seed)
        ks = jax.random.split(key, 32)
        s = 0.02
        d = {}
        d['x'] = jax.random.normal(ks[0], (B, L, D), jnp.float32)
        d['slot_query'] = jax.random.normal(ks[1], (1, NS, D), jnp.float32) * 0.01
        for i, nm in enumerate(['d_Wq', 'd_Wk', 'd_Wv', 'd_Wo']):
            d[nm] = jax.random.normal(ks[2 + i], (D, D), jnp.float32) * s
        for nm in ['d_bq', 'd_bk', 'd_bv', 'd_bo']:
            d[nm] = jnp.zeros((D,), jnp.float32)
        for i, nm in enumerate(['c_Wq', 'c_Wk', 'c_Wv', 'c_Wo']):
            d[nm] = jax.random.normal(ks[6 + i], (D, D), jnp.float32) * s
        for nm in ['c_bq', 'c_bk', 'c_bv', 'c_bo']:
            d[nm] = jnp.zeros((D,), jnp.float32)
        d['e_ln_g'] = jnp.ones((E, D), jnp.float32)
        d['e_ln_b'] = jnp.zeros((E, D), jnp.float32)
        d['e_W1'] = jax.random.normal(ks[10], (E, D, F), jnp.float32) * s
        d['e_b1'] = jnp.zeros((E, F), jnp.float32)
        d['e_Wg'] = jax.random.normal(ks[11], (E, D, F), jnp.float32) * s
        d['e_bg'] = jnp.zeros((E, F), jnp.float32)
        d['e_W2'] = jax.random.normal(ks[12], (E, F, D), jnp.float32) * s
        d['e_b2'] = jnp.zeros((E, D), jnp.float32)
        return d
    _L0_ffn_all = _L0_ffn_setup()
    _L0_ffn_in = {k: v for k, v in _L0_ffn_all.items() if k in ('slot_query', 'd_Wq', 'd_Wk', 'd_Wv', 'd_Wo', 'd_bq', 'd_bk', 'd_bv', 'd_bo', 'c_Wq', 'c_Wk', 'c_Wv', 'c_Wo', 'c_bq', 'c_bk', 'c_bv', 'c_bo', 'e_ln_g', 'e_ln_b', 'e_W1', 'e_b1', 'e_Wg', 'e_bg', 'e_W2', 'e_b2')}
    del _L0_ffn_all
    return {'x': x, 'ctx_1024': ctx_1024, 'L0_attn_W_in': _L0_attn_in['W_in'], 'L0_attn_conv_w': _L0_attn_in['conv_w'], 'L0_attn_conv_b': _L0_attn_in['conv_b'], 'L0_attn_A_param': _L0_attn_in['A_param'], 'L0_attn_dt_bias': _L0_attn_in['dt_bias'], 'L0_attn_W_out': _L0_attn_in['W_out'], 'L0_xattn_q_w': _L0_xattn_in['q_w'], 'L0_xattn_q_b': _L0_xattn_in['q_b'], 'L0_xattn_k_w': _L0_xattn_in['k_w'], 'L0_xattn_k_b': _L0_xattn_in['k_b'], 'L0_xattn_v_w': _L0_xattn_in['v_w'], 'L0_xattn_v_b': _L0_xattn_in['v_b'], 'L0_xattn_o_w': _L0_xattn_in['o_w'], 'L0_xattn_o_b': _L0_xattn_in['o_b'], 'L0_ffn_slot_query': _L0_ffn_in['slot_query'], 'L0_ffn_d_Wq': _L0_ffn_in['d_Wq'], 'L0_ffn_d_Wk': _L0_ffn_in['d_Wk'], 'L0_ffn_d_Wv': _L0_ffn_in['d_Wv'], 'L0_ffn_d_Wo': _L0_ffn_in['d_Wo'], 'L0_ffn_d_bq': _L0_ffn_in['d_bq'], 'L0_ffn_d_bk': _L0_ffn_in['d_bk'], 'L0_ffn_d_bv': _L0_ffn_in['d_bv'], 'L0_ffn_d_bo': _L0_ffn_in['d_bo'], 'L0_ffn_c_Wq': _L0_ffn_in['c_Wq'], 'L0_ffn_c_Wk': _L0_ffn_in['c_Wk'], 'L0_ffn_c_Wv': _L0_ffn_in['c_Wv'], 'L0_ffn_c_Wo': _L0_ffn_in['c_Wo'], 'L0_ffn_c_bq': _L0_ffn_in['c_bq'], 'L0_ffn_c_bk': _L0_ffn_in['c_bk'], 'L0_ffn_c_bv': _L0_ffn_in['c_bv'], 'L0_ffn_c_bo': _L0_ffn_in['c_bo'], 'L0_ffn_e_ln_g': _L0_ffn_in['e_ln_g'], 'L0_ffn_e_ln_b': _L0_ffn_in['e_ln_b'], 'L0_ffn_e_W1': _L0_ffn_in['e_W1'], 'L0_ffn_e_b1': _L0_ffn_in['e_b1'], 'L0_ffn_e_Wg': _L0_ffn_in['e_Wg'], 'L0_ffn_e_bg': _L0_ffn_in['e_bg'], 'L0_ffn_e_W2': _L0_ffn_in['e_W2'], 'L0_ffn_e_b2': _L0_ffn_in['e_b2']}

def reference(x, ctx_1024, L0_attn_W_in, L0_attn_conv_w, L0_attn_conv_b, L0_attn_A_param, L0_attn_dt_bias, L0_attn_W_out, L0_xattn_q_w, L0_xattn_q_b, L0_xattn_k_w, L0_xattn_k_b, L0_xattn_v_w, L0_xattn_v_b, L0_xattn_o_w, L0_xattn_o_b, L0_ffn_slot_query, L0_ffn_d_Wq, L0_ffn_d_Wk, L0_ffn_d_Wv, L0_ffn_d_Wo, L0_ffn_d_bq, L0_ffn_d_bk, L0_ffn_d_bv, L0_ffn_d_bo, L0_ffn_c_Wq, L0_ffn_c_Wk, L0_ffn_c_Wv, L0_ffn_c_Wo, L0_ffn_c_bq, L0_ffn_c_bk, L0_ffn_c_bv, L0_ffn_c_bo, L0_ffn_e_ln_g, L0_ffn_e_ln_b, L0_ffn_e_W1, L0_ffn_e_b1, L0_ffn_e_Wg, L0_ffn_e_bg, L0_ffn_e_W2, L0_ffn_e_b2):
    import jax
    import jax.numpy as jnp

    def _L0_attn_ref(x, W_in, conv_w, conv_b, A_param, dt_bias, W_out):
        import jax, jax.numpy as jnp
        import numpy as np
        D_CONV = 4
        CHUNK = 64

        def segsum(x):
            T = x.shape[-1]
            strict = jnp.tril(jnp.ones((T, T), dtype=bool), -1)
            xr = jnp.where(strict, x[..., :, None], 0.0)
            x_segsum = jnp.cumsum(xr, axis=-2)
            return jnp.where(jnp.tril(jnp.ones((T, T), dtype=bool)), x_segsum, -jnp.inf)

        def ssd(x, A, B, C, chunk):
            b, s, h, p = x.shape
            c = s // chunk
            x = x.reshape(b, c, chunk, h, p)
            B = B.reshape(b, c, chunk, h, -1)
            C = C.reshape(b, c, chunk, h, -1)
            A = A.reshape(b, c, chunk, h).transpose(0, 3, 1, 2)
            A_cumsum = jnp.cumsum(A, axis=-1)
            L = jnp.exp(segsum(A))
            Y_diag = jnp.einsum('bclhn,bcshn,bhcls,bcshp->bclhp', C, B, L, x)
            decay_states = jnp.exp(A_cumsum[..., -1:] - A_cumsum)
            states = jnp.einsum('bclhn,bhcl,bclhp->bchpn', B, decay_states, x)
            states = jnp.concatenate([jnp.zeros_like(states[:, :1]), states], axis=1)
            A_last = jnp.pad(A_cumsum[..., -1], ((0, 0), (0, 0), (1, 0)))
            decay_chunk = jnp.exp(segsum(A_last))
            states = jnp.einsum('bhzc,bchpn->bzhpn', decay_chunk, states)[:, :-1]
            Y_off = jnp.einsum('bclhn,bchpn,bhcl->bclhp', C, states, jnp.exp(A_cumsum))
            return (Y_diag + Y_off).reshape(b, s, h, p)
        b, src_len, d_model = x.shape
        n_heads = A_param.shape[0]
        d_conv_c = conv_w.shape[0]
        d_inner = W_out.shape[1]
        d_state = (d_conv_c - d_inner) // 2
        pad = -src_len % CHUNK
        xs = jnp.pad(x, ((0, 0), (0, pad), (0, 0)))
        s = xs.shape[1]
        proj = xs @ W_in.T
        xBC, dt = (proj[..., :d_conv_c], proj[..., d_conv_c:])
        xp = jnp.pad(xBC, ((0, 0), (D_CONV - 1, 0), (0, 0)))
        conv_out = sum((xp[:, k:k + s, :] * conv_w[:, k] for k in range(D_CONV))) + conv_b
        C_ = conv_out[..., :d_state]
        B_ = conv_out[..., d_state:2 * d_state]
        xin = conv_out[..., 2 * d_state:]
        dt = jax.nn.softplus(dt + dt_bias)
        Ch = C_.reshape(b, s, n_heads, -1)
        Bh = B_.reshape(b, s, n_heads, -1)
        xh = xin.reshape(b, s, n_heads, -1)
        A = A_param * dt
        cumA = jnp.cumsum(A, axis=1)
        norm = (jnp.exp(cumA) * jnp.cumsum(jnp.exp(-cumA), axis=1))[..., None]
        Y = ssd(xh, A, Bh, Ch, CHUNK)
        out = Y[0] / norm
        out = out.reshape(b, s, -1) @ W_out.T
        return out[:, :src_len]

    def _L0_xattn_ref(x, context, q_w, q_b, k_w, k_b, v_w, v_b, o_w, o_b):
        import jax, jax.numpy as jnp
        import numpy as np
        N_EMBD = 512
        N_HEADS = 16
        HEAD_DIM = N_EMBD // N_HEADS
        B, T, C = x.shape
        S = context.shape[1]
        H, D = (N_HEADS, HEAD_DIM)
        q = (x @ q_w + q_b).reshape(B, T, H, D).transpose(0, 2, 1, 3)
        k = (context @ k_w + k_b).reshape(B, S, H, D).transpose(0, 2, 1, 3)
        v = (context @ v_w + v_b).reshape(B, S, H, D).transpose(0, 2, 1, 3)
        att = jnp.einsum('bhtd,bhsd->bhts', q, k) / jnp.sqrt(jnp.float32(D))
        causal = jnp.tril(jnp.ones((T, S), dtype=bool))
        att = jnp.where(causal[None, None, :, :], att, -jnp.inf)
        att = jax.nn.softmax(att, axis=-1)
        y = jnp.einsum('bhts,bhsd->bhtd', att, v)
        y = y.transpose(0, 2, 1, 3).reshape(B, T, C)
        return y @ o_w + o_b

    def _L0_ffn_ref(x, slot_query, d_Wq, d_Wk, d_Wv, d_Wo, d_bq, d_bk, d_bv, d_bo, c_Wq, c_Wk, c_Wv, c_Wo, c_bq, c_bk, c_bv, c_bo, e_ln_g, e_ln_b, e_W1, e_b1, e_Wg, e_bg, e_W2, e_b2):
        import jax, jax.numpy as jnp
        import numpy as np
        B, L, D = (4, 1024, 512)
        H = 16
        E = 16
        NS = 16
        S = NS // E
        F = 2048
        EPS = 1e-05

        def _layernorm(x, g, b):
            mu = jnp.mean(x, axis=-1, keepdims=True)
            var = jnp.mean(jnp.square(x - mu), axis=-1, keepdims=True)
            return (x - mu) * jax.lax.rsqrt(var + EPS) * g + b

        def _mha(q, k, v, Wq, bq, Wk, bk, Wv, bv, Wo, bo):
            Bq, Lq, Dm = q.shape
            dh = Dm // H
            qh = (q @ Wq + bq).reshape(Bq, Lq, H, dh)
            kh = (k @ Wk + bk).reshape(Bq, -1, H, dh)
            vh = (v @ Wv + bv).reshape(Bq, -1, H, dh)
            scores = jnp.einsum('bqhd,bkhd->bhqk', qh, kh) / jnp.asarray(np.sqrt(dh), q.dtype)
            attn = jax.nn.softmax(scores, axis=-1)
            out = jnp.einsum('bhqk,bkhd->bqhd', attn, vh).reshape(Bq, Lq, Dm)
            return out @ Wo + bo
        Bx = x.shape[0]
        q = jnp.broadcast_to(slot_query, (Bx, NS, D))
        o = q + _mha(q, x, x, d_Wq, d_bq, d_Wk, d_bk, d_Wv, d_bv, d_Wo, d_bo)
        os = o.reshape(Bx, E, S, D)
        h = _layernorm(os, e_ln_g[None, :, None, :], e_ln_b[None, :, None, :])
        u = jax.nn.silu(jnp.einsum('besd,edf->besf', h, e_W1) + e_b1[None, :, None, :])
        g = jax.nn.silu(jnp.einsum('besd,edf->besf', h, e_Wg) + e_bg[None, :, None, :])
        y = jnp.einsum('besf,efd->besd', u * g, e_W2) + e_b2[None, :, None, :]
        o = o + y.reshape(Bx, NS, D)
        out = _mha(x, o, o, c_Wq, c_bq, c_Wk, c_bk, c_Wv, c_bv, c_Wo, c_bo)
        return out
    x = _layernorm(x + _L0_attn_ref(x, L0_attn_W_in, L0_attn_conv_w, L0_attn_conv_b, L0_attn_A_param, L0_attn_dt_bias, L0_attn_W_out), axis=-1)
    x = _layernorm(x + _L0_xattn_ref(x, ctx_1024, L0_xattn_q_w, L0_xattn_q_b, L0_xattn_k_w, L0_xattn_k_b, L0_xattn_v_w, L0_xattn_v_b, L0_xattn_o_w, L0_xattn_o_b), axis=-1)
    x = _layernorm(x + _L0_ffn_ref(x, L0_ffn_slot_query, L0_ffn_d_Wq, L0_ffn_d_Wk, L0_ffn_d_Wv, L0_ffn_d_Wo, L0_ffn_d_bq, L0_ffn_d_bk, L0_ffn_d_bv, L0_ffn_d_bo, L0_ffn_c_Wq, L0_ffn_c_Wk, L0_ffn_c_Wv, L0_ffn_c_Wo, L0_ffn_c_bq, L0_ffn_c_bk, L0_ffn_c_bv, L0_ffn_c_bo, L0_ffn_e_ln_g, L0_ffn_e_ln_b, L0_ffn_e_W1, L0_ffn_e_b1, L0_ffn_e_Wg, L0_ffn_e_bg, L0_ffn_e_W2, L0_ffn_e_b2), axis=-1)
    return x

_drawn_inputs = setup_inputs


def setup_inputs(seed=0):
    import zlib

    import numpy as np

    out = dict(_drawn_inputs(seed))
    spreads = {'L0_attn_conv_b': (0.0, 0.1),
     'L0_ffn_d_bq': (0.0, 0.8),
     'L0_ffn_d_bk': (0.0, 2.0),
     'L0_ffn_d_bv': (0.0, 0.726),
     'L0_ffn_d_bo': (0.0, 0.356),
     'L0_ffn_c_bq': (0.0, 0.8),
     'L0_ffn_c_bk': (0.0, 2.0),
     'L0_ffn_c_bv': (0.0, 2.0),
     'L0_ffn_c_bo': (0.0, 2.0),
     'L0_ffn_e_ln_g': (1.0, 0.6),
     'L0_ffn_e_ln_b': (0.0, 0.8),
     'L0_ffn_e_b1': (0.0, 0.8),
     'L0_ffn_e_bg': (0.0, 0.8),
     'L0_ffn_e_b2': (0.0, 0.8)}
    factors = {'L0_attn_dt_bias': 8.0,
     'L0_xattn_q_b': 8.0,
     'L0_xattn_k_b': 200.0,
     'L0_xattn_v_b': 4.127,
     'L0_ffn_slot_query': 8.0,
     'L0_ffn_d_Wq': 8.0,
     'L0_ffn_d_Wk': 8.0,
     'L0_ffn_d_Wv': 8.0,
     'L0_ffn_d_Wo': 4.817,
     'L0_ffn_c_Wq': 8.0,
     'L0_ffn_c_Wk': 8.0,
     'L0_ffn_e_W1': 8.0,
     'L0_ffn_e_Wg': 8.0,
     'L0_ffn_e_W2': 8.0}
    for name, (base, spread) in spreads.items():
        noise = np.random.default_rng([zlib.crc32(name.encode()), seed]).standard_normal(out[name].shape)
        drawn = base * np.exp(spread * noise) if base else spread * noise
        out[name] = jnp.asarray(drawn.astype(out[name].dtype))
    for name, factor in factors.items():
        out[name] = (out[name] * factor).astype(out[name].dtype)
    return out
```

```python
from contextlib import ExitStack

import concourse.bass as bass
import concourse.mybir as mybir

F32 = mybir.dt.float32
ALU = mybir.AluOpType
ACT = mybir.ActivationFunctionType
AX = mybir.AxisListType

P = 128
BATCH, SEQ, D = 2, 2048, 512
TOKENS = BATCH * SEQ
TILES = TOKENS // P
CHUNKS = SEQ // P
KC = D // P
HEADS = 16
HD = D // HEADS
HG = P // HD
GROUPS = HEADS // HG
TAPS = 4
HALO = TAPS - 1
CONV = 3 * D
CT = CONV // P
CTX = 77
SLOTS = 16
SROWS = HEADS * SLOTS
SM = SROWS // P
EXPERTS = 16
F = 2048
EPS = 1e-5
SCALE = float(HD) ** -0.5
NEG = -3.0e38
KROWS = HG * CTX
PIECE = -(-KROWS // 3)
PIECES = [min(PIECE, KROWS - i * PIECE) for i in range(3)]
UNIT = 4096
UNITS = 6
FQ = F // 4


def broadcast(ap, shape):
    return ap.broadcast_to(shape)


class Stage:

    def __init__(self, nc, tag, arena=None):
        self.nc, self.tag, self.stack, self.arena, self.used, self.taken = nc, tag, ExitStack(), arena, 0, []

    def __enter__(self):
        return self

    def __exit__(self, *a):
        if self.taken and a[0] is None:
            self.nc.clear_and_free_semaphores(self.taken)
            self.nc.all_engine_barrier()
        return self.stack.__exit__(*a)

    def sb(self, name, shape):
        size = 1
        for n in shape[1:]:
            size *= n
        if self.arena is not None and self.used + size <= UNITS * UNIT:
            flat = self.arena[0:shape[0], self.used:self.used + size]
            self.used += size
            return shaped(flat, shape)
        return self.stack.enter_context(self.nc.sbuf_tensor(f"{self.tag}_{name}", shape, F32))

    def banks(self, n=8):
        return [self.stack.enter_context(self.nc.psum_tensor(f"{self.tag}_bank{i}", [P, 512], F32)) for i in range(n)]

    def sem(self, name):
        self.taken.append(self.nc.alloc_semaphore(f"{self.tag}_{name}"))
        return self.taken[-1]

    def sems(self, *names):
        return {n: self.sem(n) for n in names}

    def pair(self, name):
        return [self.sem(f"{name}{i}") for i in range(2)]


def shaped(flat, shape):
    names = "abcd"[:len(shape) - 1]
    dims = dict(zip(names, shape[1:]))
    return flat.rearrange(f"p ({' '.join(names)}) -> p {' '.join(names)}", **dims)


def wait_later(eng, sem, value):
    if not isinstance(value, int) or value > 0:
        eng.wait_ge(sem, value)


def tables_stage(nc, io, hold):
    with Stage(nc, "tab", hold["arena"]) as st:
        wdt = st.sb("wdt", [P, KC, HD])
        xblk = [st.sb(f"xblk{i}", [P, KC, 512]) for i in range(3)]
        bias = st.sb("bias", [P, 1])
        apar = st.sb("apar", [P, 1])
        zabs = st.sb("zabs", [P, BATCH, 512])
        zexp = st.sb("zexp", [P, BATCH, 512])
        zln = st.sb("zln", [P, BATCH, 512])
        zrelu = st.sb("zrelu", [P, BATCH, 512])
        arow = st.sb("arow", [P, BATCH, 512])
        atok = st.sb("atok", [P, BATCH, CHUNKS, HEADS])
        carry = st.sb("carry", [P, BATCH, CHUNKS, HEADS])
        carry2 = st.sb("carry2", [P, BATCH, CHUNKS, HEADS])
        cum = st.sb("cum", [P, BATCH, CHUNKS, HEADS])
        neg = st.sb("neg", [P, BATCH, CHUNKS, HEADS])
        pos = st.sb("pos", [P, BATCH, CHUNKS, HEADS])
        cume = st.sb("cume", [P, BATCH, CHUNKS, HEADS])
        norm = st.sb("norm", [P, BATCH, CHUNKS, HEADS])
        rnorm = st.sb("rnorm", [P, BATCH, CHUNKS, HEADS])
        tri = st.sb("tri", [P, P])
        ones = st.sb("ones", [P, P])
        wk = st.sb("wk", [P, KC, D])
        wv = st.sb("wv", [P, KC, D])
        wq = st.sb("wq", [P, KC, D])
        wkT = st.sb("wkT", [P, KC, D])
        ctxT = st.sb("ctxT", [P, KC, BATCH * CTX])
        kb = st.sb("kb", [P, GROUPS])
        qb = st.sb("qb", [P, GROUPS])
        bk = st.sb("bk", [P, GROUPS])
        vb = st.sb("vb", [CTX, D])
        vtok = st.sb("vtok", [CTX, BATCH, D])
        slotT = st.sb("slotT", [P, KC, SLOTS])
        sqbd = st.sb("sqbd", [P, GROUPS, HG, SLOTS])
        bank = st.banks()
        s = st.sems("consts", "zeros", "small", "wdt_in", "ctx_in", "kw_in", "vw_in", "qw_in", "kT_in", "blk_used",
                    "dt_ready", "softplus", "dt_steps", "a_ready", "a_turned", "atok_ready", "cum_ready", "exp_ready",
                    "sums1", "sums2", "carry_steps", "norm_steps", "tables_ready", "k_ready", "v_ready", "vtok_ready",
                    "vbd_in", "q_ready", "sq_ready", "m1_ready", "kbias_ready", "kbd_done", "m1_done")
        blk_in = [st.sem(f"blk_in{i}") for i in range(3)]
        QB = SEQ // 512

        def small_loads(sp):
            for q in range(QB):
                sp.dma_start(bias[HD * q:HD * q + HEADS, :], io["dt_bias"].rearrange("(h o) -> h o", o=1)).then_inc(s["small"], 16)
                sp.dma_start(apar[HD * q:HD * q + HEADS, :], io["A_param"].rearrange("(h o) -> h o", o=1)).then_inc(s["small"], 16)
        SMALL_AP = 2 * QB * 16

        with nc.Block() as block:
            @block.sync
            def _(sp):
                sp.wait_ge(s["zeros"], 3)
                sp.dma_start(wdt[:, :, 0:HEADS], io["WinT"][:, CONV:].rearrange("(k p) n -> p k n", p=P)).then_inc(s["wdt_in"], 16)
                small_loads(sp)
                for i in range(BATCH * QB):
                    if i >= 3:
                        sp.wait_ge(s["blk_used"], i - 2)
                    sp.dma_start(xblk[i % 3][:], io["xT"][:, i * 512:(i + 1) * 512].rearrange("(k p) n -> p k n", p=P)).then_inc(blk_in[i % 3], 16)
                    if i == 2:
                        sp.dma_start(ctxT[:], io["ctxT"].rearrange("(k p) n -> p k n", p=P)).then_inc(s["ctx_in"], 16)
                        sp.dma_start(slotT[:], io["slotT"].rearrange("(k p) n -> p k n", p=P)).then_inc(s["ctx_in"], 16)
                        sp.dma_start(vb[:], broadcast(io["v_b"].rearrange("(o n) -> o n", o=1), [CTX, D])).then_inc(s["ctx_in"], 16)
                        for dst, src in ((kb, io["k_b"]), (qb, io["d_bq"]), (bk, io["d_bk"])):
                            sp.dma_start(dst[:], src).then_inc(s["ctx_in"], 16)
                CTX_IN = 6 * 16
                for dst, src, sem in ((wk, io["k_w"], s["kw_in"]), (wv, io["v_w"], s["vw_in"]), (wq, io["d_Wq"], s["qw_in"]), (wkT, io["d_WkT"], s["kT_in"])):
                    sp.dma_start(dst[:], src.rearrange("(k p) n -> p k n", p=P)).then_inc(sem, 16)
                sp.wait_ge(s["vtok_ready"], BATCH)
                n = 0
                for b in range(BATCH):
                    for h in range(HG):
                        r = h * CTX
                        while r < (h + 1) * CTX:
                            piece = r // PIECE
                            end = min((h + 1) * CTX, (piece + 1) * PIECE)
                            src = vtok[r - h * CTX:end - h * CTX, b, :].rearrange("s (g h p) -> s g h p", g=GROUPS, h=HG)[:, :, h, :]
                            sp.dma_start(hold["vbd"][r - piece * PIECE:end - piece * PIECE, b, piece, :, h * HD:(h + 1) * HD], src).then_inc(s["vbd_in"], 16)
                            n += 1
                            r = end
                sp.wait_ge(s["vbd_in"], 16 * n)

            @block.gpsimd
            def _(pool):
                nc.gpsimd.memset(wdt[:], 0.0).then_inc(s["zeros"], 1)
                nc.gpsimd.memset(bias[:], 0.0).then_inc(s["zeros"], 1)
                nc.gpsimd.memset(apar[:], 0.0).then_inc(s["zeros"], 1)
                nc.gpsimd.memset(hold["ident"][:], 0.0).then_inc(s["zeros"], 1)
                nc.gpsimd.memset(tri[:], 1.0).then_inc(s["zeros"], 1)
                nc.gpsimd.memset(ones[:], 1.0).then_inc(s["zeros"], 1)
                nc.gpsimd.memset(hold["mask"][:], 0.0).then_inc(s["zeros"], 1)
                pool.wait_ge(s["zeros"], 7)
                nc.gpsimd.affine_select(out=hold["ident"][:], in_=hold["ident"][:], compare_op=ALU.not_equal, fill=1.0, base=0,
                                        pattern=[[-1, P]], channel_multiplier=1).then_inc(s["consts"], 1)
                nc.gpsimd.affine_select(out=tri[:], in_=tri[:], compare_op=ALU.is_ge, fill=0.0, base=0,
                                        pattern=[[1, P]], channel_multiplier=-1).then_inc(s["consts"], 1)
                for t in range(0, TILES, CHUNKS):
                    m = hold["mask"][:, t * CTX:(t + 1) * CTX]
                    nc.gpsimd.affine_select(out=m, in_=m, compare_op=ALU.is_ge, fill=NEG, base=0,
                                            pattern=[[-1, CTX]], channel_multiplier=1).then_inc(s["consts"], 1)
                nc.gpsimd.memset(hold["vbd"][:], 0.0).then_inc(s["zeros"], 1)
                nc.gpsimd.memset(hold["kbd"][:], 0.0).then_inc(s["zeros"], 1)
                nc.gpsimd.memset(sqbd[:], 0.0).then_inc(s["zeros"], 1)
                pool.wait_ge(s["consts"], 2)
                nc.gpsimd.tensor_copy(hold["tri"][:], tri[:]).then_inc(s["consts"], 1)

            @block.tensor
            def _(pe):
                pe.wait_ge(s["wdt_in"], 16)
                for b in range(BATCH):
                    for q in range(QB):
                        i = b * QB + q
                        pe.wait_ge(blk_in[i % 3], 16 * (i // 3 + 1))
                        for k in range(KC):
                            last = nc.tensor.matmul(bank[b][HD * q:HD * (q + 1), :], wdt[:, k, :], xblk[i % 3][:, k, :],
                                                    start=(k == 0), stop=(k == KC - 1))
                        last.then_inc(s["blk_used"], 1)
                pe.wait_ge(s["ctx_in"], 6 * 16)
                pe.wait_ge(s["kw_in"], 16)
                for g in range(GROUPS):
                    for k in range(KC):
                        last = nc.tensor.matmul(bank[2 + g // 2][:, (g % 2) * 256:(g % 2) * 256 + BATCH * CTX], wk[:, k, g * P:(g + 1) * P],
                                                ctxT[:, k, :], start=(k == 0), stop=(k == KC - 1))
                last.then_inc(s["k_ready"], 1)
                pe.wait_ge(s["vw_in"], 16)
                for b in range(BATCH):
                    for k in range(KC):
                        last = nc.tensor.matmul(bank[4 + b][0:CTX, :], ctxT[:, k, b * CTX:(b + 1) * CTX], wv[:, k, :],
                                                start=(k == 0), stop=(k == KC - 1))
                    last.then_inc(s["v_ready"], 1)
                pe.wait_ge(s["consts"], 2)
                for b in range(BATCH):
                    pe.wait_ge(s["a_ready"], b + 1)
                    for sub in range(4):
                        last = nc.tensor.transpose(bank[6 + b][:, sub * P:(sub + 1) * P], arow[:, b, sub * P:(sub + 1) * P], hold["ident"][:])
                    last.then_inc(s["a_turned"], 1)
                pe.wait_ge(s["atok_ready"], BATCH)
                nc.tensor.matmul(bank[0][:], tri[:], atok[:], start=True, stop=True)
                nc.tensor.matmul(bank[1][:], ones[:], atok[:], start=True, stop=True).then_inc(s["sums1"], 1)
                pe.wait_ge(s["qw_in"], 16)
                pe.wait_ge(s["atok_ready"], BATCH)
                for g in range(GROUPS):
                    for k in range(KC):
                        last = nc.tensor.matmul(bank[6][:, g * SLOTS:(g + 1) * SLOTS], wq[:, k, g * P:(g + 1) * P], slotT[:, k, :],
                                                start=(k == 0), stop=(k == KC - 1))
                last.then_inc(s["q_ready"], 1)
                pe.wait_ge(s["exp_ready"], 1)
                pe.wait_ge(s["cum_ready"], 1)
                nc.tensor.matmul(bank[0][:], tri[:], neg[:], start=True, stop=True)
                nc.tensor.matmul(bank[1][:], ones[:], neg[:], start=True, stop=True).then_inc(s["sums2"], 1)
                pe.wait_ge(s["kT_in"], 16)
                pe.wait_ge(s["sq_ready"], GROUPS)
                pe.wait_ge(s["kbd_done"], 1)
                pe.wait_ge(s["vtok_ready"], BATCH)
                for k in range(KC):
                    for g in range(GROUPS):
                        last = nc.tensor.matmul(bank[2 + k][:, g * HG * SLOTS:(g + 1) * HG * SLOTS], wkT[:, g, k * P:(k + 1) * P],
                                                sqbd[:, g, :, :], start=True, stop=True)
                last.then_inc(s["m1_ready"], 1)
                for g in range(GROUPS):
                    half = (g % 2) * HG * SLOTS
                    last = nc.tensor.matmul(bank[7][half:half + HG * SLOTS, g // 2:g // 2 + 1], sqbd[:, g, :, :], bk[:, g:g + 1],
                                            start=True, stop=True)
                last.then_inc(s["kbias_ready"], 1)

            @block.scalar
            def _(act):
                act.wait_ge(s["small"], SMALL_AP)
                for b in range(BATCH):
                    act.wait_ge(s["blk_used"], QB * (b + 1))
                    nc.scalar.activation(zabs[:, b, :], bank[b][:], ACT.Abs, bias=bias[:]).then_inc(s["softplus"], 1)
                    nc.scalar.activation(zrelu[:, b, :], bank[b][:], ACT.Relu, bias=bias[:]).then_inc(s["softplus"], 1)
                    act.wait_ge(s["softplus"], 4 * b + 2)
                    nc.scalar.activation(zexp[:, b, :], zabs[:, b, :], ACT.Exp, scale=-1.0).then_inc(s["softplus"], 1)
                    act.wait_ge(s["softplus"], 4 * b + 3)
                    nc.scalar.activation(zln[:, b, :], zexp[:, b, :], ACT.Ln, bias=1.0).then_inc(s["softplus"], 1)
                act.wait_ge(s["cum_ready"], 1)
                nc.scalar.activation(neg[:], cum[:], ACT.Exp, scale=-1.0).then_inc(s["exp_ready"], 1)
                nc.scalar.activation(pos[:], cum[:], ACT.Exp).then_inc(s["exp_ready"], 1)
                act.wait_ge(s["exp_ready"], 1)
                nc.scalar.activation(hold["decay"][:], neg[:, 0, :, :], ACT.Copy).then_inc(s["tables_ready"], 1)

            def running_sums(dve, sums, carry, out, first, before):
                step = first
                for c in range(1, CHUNKS):
                    dve.wait_ge(s["carry_steps"], step)
                    nc.vector.tensor_tensor(carry[:, :, c, :], carry[:, :, c - 1, :],
                                            before.rearrange("p (b c h) -> p b c h", b=BATCH, c=CHUNKS)[:, :, c - 1, :],
                                            ALU.add).then_inc(s["carry_steps"], 1)
                    step += 1
                dve.wait_ge(s["carry_steps"], step)
                return nc.vector.tensor_tensor(out[:], sums.rearrange("p (b c h) -> p b c h", b=BATCH, c=CHUNKS), carry[:], ALU.add)

            @block.vector
            def _(dve):
                nc.vector.memset(carry[:, :, 0, :], 0.0)
                nc.vector.memset(carry2[:, :, 0, :], 0.0).then_inc(s["carry_steps"], 1)
                dve.wait_ge(s["small"], SMALL_AP)
                for b in range(BATCH):
                    dve.wait_ge(s["softplus"], 4 * (b + 1))
                    nc.vector.tensor_tensor(arow[:, b, :], zrelu[:, b, :], zln[:, b, :], ALU.add).then_inc(s["dt_steps"], 1)
                    dve.wait_ge(s["dt_steps"], b + 1)
                    nc.vector.tensor_scalar(arow[:, b, :], arow[:, b, :], apar[:], None, ALU.mult).then_inc(s["a_ready"], 1)
                for b in range(BATCH):
                    dve.wait_ge(s["a_turned"], b + 1)
                    nc.vector.tensor_copy(atok[:, b, :, :].rearrange("p (q i) h -> p i q h", q=QB),
                                          bank[6 + b][:].rearrange("p (i q h) -> p i q h", i=4, q=QB)[:, :, :, 0:HEADS]).then_inc(s["atok_ready"], 1)
                dve.wait_ge(s["k_ready"], 1)
                dve.wait_ge(s["zeros"], 10)
                for g in range(GROUPS):
                    for h in range(HG):
                        r = slice(h * HD, (h + 1) * HD)
                        last = nc.vector.tensor_scalar(hold["kbd"][r, :, g, h, :],
                                                       bank[2 + g // 2][r, (g % 2) * 256:(g % 2) * 256 + BATCH * CTX].rearrange("p (b s) -> p b s", b=BATCH),
                                                       kb[r, g:g + 1], None, ALU.add)
                last.then_inc(s["kbd_done"], 1)
                for b in range(BATCH):
                    dve.wait_ge(s["v_ready"], b + 1)
                    nc.vector.tensor_tensor(vtok[:, b, :], bank[4 + b][0:CTX, :], vb[:], ALU.add).then_inc(s["vtok_ready"], 1)
                dve.wait_ge(s["sums1"], 1)
                running_sums(dve, bank[0][:], carry, cum, 1, bank[1][:]).then_inc(s["cum_ready"], 1)
                dve.wait_ge(s["q_ready"], 1)
                for g in range(GROUPS):
                    for h in range(HG):
                        r = slice(h * HD, (h + 1) * HD)
                        last = nc.vector.tensor_scalar(sqbd[r, g, h, :], bank[6][r, g * SLOTS:(g + 1) * SLOTS], qb[r, g:g + 1], None, ALU.add)
                    last.then_inc(s["sq_ready"], 1)
                dve.wait_ge(s["sums2"], 1)
                running_sums(dve, bank[0][:], carry2, cume, CHUNKS, bank[1][:]).then_inc(s["norm_steps"], 1)
                dve.wait_ge(s["exp_ready"], 2)
                dve.wait_ge(s["norm_steps"], 1)
                nc.vector.tensor_tensor(norm[:], pos[:], cume[:], ALU.mult).then_inc(s["norm_steps"], 1)
                dve.wait_ge(s["norm_steps"], 2)
                nc.vector.reciprocal(rnorm[:], norm[:]).then_inc(s["norm_steps"], 1)
                dve.wait_ge(s["norm_steps"], 3)
                for b in range(BATCH):
                    nc.vector.tensor_tensor(hold["rate"][:, b, :, :], pos[:, 0, :, :], rnorm[:, b, :, :], ALU.mult).then_inc(s["tables_ready"], 1)
                dve.wait_ge(s["m1_ready"], 1)
                for k in range(KC):
                    nc.vector.tensor_copy(hold["m1"][:, k, :], bank[2 + k][:, 0:SROWS]).then_inc(s["m1_done"], 1)
                dve.wait_ge(s["kbias_ready"], 1)
                nc.vector.tensor_scalar(hold["kbias"][:], bank[7][:, 0:SM], SCALE, None, ALU.mult).then_inc(s["m1_done"], 1)


LN_STEPS = 14
MAGIC = 0x5F3759DF


def layernorm(nc, dve, sem, first, x, stats, out):
    n = len(x)
    var, y, t = stats[:, 0:n, 8:9], stats[:, 0:n, 9:10], stats[:, 0:n, 10:11]
    INT = mybir.dt.int32
    for i in range(n):
        last = nc.vector.bn_stats(stats[:, i, 0:6], x[i])
    last.then_inc(sem, 1)
    dve.wait_ge(sem, first + 1)
    nc.vector.memset(var, EPS)
    for i in range(n):
        last = nc.vector.bn_aggr(stats[:, i, 6:8], stats[:, i, 0:6])
    last.then_inc(sem, 1)
    dve.wait_ge(sem, first + 2)
    nc.vector.tensor_tensor(var, var, stats[:, 0:n, 7:8], ALU.add).then_inc(sem, 1)
    dve.wait_ge(sem, first + 3)
    nc.vector.tensor_scalar(y.bitcast(INT), var.bitcast(INT), 1, None, ALU.logical_shift_right).then_inc(sem, 1)
    dve.wait_ge(sem, first + 4)
    nc.vector.tensor_scalar(y.bitcast(INT), y.bitcast(INT), -1.0, float(MAGIC), ALU.mult, ALU.add).then_inc(sem, 1)
    for i in range(3):
        dve.wait_ge(sem, first + 5 + 3 * i)
        nc.vector.tensor_tensor(t, y, y, ALU.mult).then_inc(sem, 1)
        dve.wait_ge(sem, first + 6 + 3 * i)
        nc.vector.scalar_tensor_tensor(t, t, -0.5, var, ALU.mult, ALU.mult).then_inc(sem, 1)
        dve.wait_ge(sem, first + 7 + 3 * i)
        last = nc.vector.scalar_tensor_tensor(y, t, 1.5, y, ALU.add, ALU.mult)
        last.then_inc(sem, 1)
    dve.wait_ge(sem, first + LN_STEPS)
    for i in range(n):
        last = nc.vector.tensor_scalar(out[i], x[i], stats[:, i, 6:7], stats[:, i, 9:10], ALU.subtract, ALU.mult)
    return last


def mixer_stage(nc, io, hold):
    with Stage(nc, "mix", hold["arena"]) as st:
        win = st.sb("win", [P, KC, CONV])
        wout = st.sb("wout", [P, KC, D])
        taps = st.sb("taps", [P, CT, TAPS])
        convb = st.sb("convb", [P, CT])
        xT = [st.sb(f"xT{i}", [P, KC, P]) for i in range(2)]
        x_in = [st.sb(f"x_in{i}", [P, BATCH, D]) for i in range(2)]
        proj = [st.sb(f"proj{i}", [P, CT, HALO + P]) for i in range(2)]
        conv = st.sb("conv", [P, CT, P])
        product = [st.sb(f"product{i}", [P, 4, P]) for i in range(2)]
        cbd = st.sb("cbd", [P, GROUPS, HG, P])
        btok = st.sb("btok", [P, D])
        xs = st.sb("xs", [P, D])
        scores = st.sb("scores", [P, HEADS, P])
        state = st.sb("state", [P, GROUPS, P])
        rate = st.sb("rate", [P, BATCH, HEADS, HD])
        rateT = st.sb("rateT", [P, BATCH, D])
        yT = st.sb("yT", [P, BATCH, D])
        xr = st.sb("xr", [P, BATCH, D])
        stats = st.sb("stats", [P, BATCH, 12])
        x1 = [st.sb(f"x1_{i}", [P, BATCH, D]) for i in range(2)]
        bank = st.banks()
        s = st.sems("weights_in", "zeros", "proj_done", "proj_out", "halo_done", "convC", "convB", "convX", "conv_tap", "conv_tapX",
                    "cbd_done", "b_turned", "btok_done", "x_turned", "xs_done", "scores_done", "scores_masked", "state_done",
                    "state_added", "y_done", "rate_done", "rate_turned", "rateT_done", "yT_done", "out_done", "res_done",
                    "ln_step", "x1_done")
        xT_in, x_arrived, x1_stored = st.pair("xT_in"), st.pair("x_arrived"), st.pair("x1_stored")
        x_v = io["x"].rearrange("(b n) d -> n b d", b=BATCH)
        x1_v = io["x1"].rearrange("(b n) d -> n b d", b=BATCH)
        LAST = CHUNKS - 1

        def load(sp, c, u):
            wait_later(sp, s["proj_done"], 3 * (c - 1))
            sp.dma_start(xT[u][:], io["xT"].rearrange("(k p) n -> p k n", p=P)[:, :, bass.ds(c * P, P)]).then_inc(xT_in[u], 16)
            wait_later(sp, s["res_done"], 2 * (c - 1))
            sp.dma_start(x_in[u][:], x_v[bass.ds(c * P, P), :, :]).then_inc(x_arrived[u], 16)

        def store(sp, c, u):
            sp.wait_ge(s["x1_done"], c + 1)
            sp.dma_start(x1_v[bass.ds(c * P, P), :, :], x1[u][:]).then_inc(x1_stored[u], 16)

        def project(pe, c, u, half):
            pe.wait_ge(xT_in[u], 16 * (half + 1))
            wait_later(pe, s["proj_out"], 3 * c)
            for grp in range(3):
                for m in range(4):
                    for k in range(KC):
                        last = nc.tensor.matmul(bank[grp][:, m * P:(m + 1) * P], win[:, k, (grp * 4 + m) * P:(grp * 4 + m + 1) * P],
                                                xT[u][:, k, :], start=(k == 0), stop=(k == KC - 1))
                last.then_inc(s["proj_done"], 1)

        def attend(pe, c):
            pe.wait_ge(s["convB"], c + 1)
            wait_later(pe, s["rateT_done"], 2 * c)
            for g in range(GROUPS):
                last = nc.tensor.transpose(bank[3][:, g * P:(g + 1) * P], conv[:, 4 + g, :], hold["ident"][:])
            last.then_inc(s["b_turned"], 1)
            pe.wait_ge(s["convX"], c + 1)
            for g in range(GROUPS):
                last = nc.tensor.transpose(bank[4][:, g * P:(g + 1) * P], conv[:, 8 + g, :], hold["ident"][:])
            last.then_inc(s["x_turned"], 1)
            pe.wait_ge(s["cbd_done"], c + 1)
            for g in range(GROUPS):
                if g == 0:
                    pe.wait_ge(s["btok_done"], c + 1)
                elif g == 1:
                    pe.wait_ge(s["xs_done"], c + 1)
                else:
                    pe.wait_ge(s["scores_masked"], 4 * c + g - 1)
                nc.tensor.matmul(bank[3 + g % 2][:], conv[:, 4 + g, :], cbd[:, g, :, :], start=True, stop=True).then_inc(s["scores_done"], 1)
                if g == 1:
                    wait_later(pe, s["res_done"], 2 * c - 1)
                    for gg in range(GROUPS):
                        last = nc.tensor.matmul(bank[6][:, gg * P:(gg + 1) * P], btok[:, gg * P:(gg + 1) * P], xs[:, gg * P:(gg + 1) * P],
                                                start=True, stop=True)
                    last.then_inc(s["state_done"], 1)
            wait_later(pe, s["yT_done"], 2 * c)
            wait_later(pe, s["state_added"], c)
            for g in range(GROUPS):
                nc.tensor.matmul(bank[5][:, g * P:(g + 1) * P], state[:, g, :], conv[:, g, :], start=True, stop=False, skip_group_check=True)
                pe.wait_ge(s["scores_masked"], 4 * c + g + 1)
                for h in range(HG):
                    hh = g * HG + h
                    last = nc.tensor.matmul(bank[5][h * HD:(h + 1) * HD, g * P:(g + 1) * P], xs[:, hh * HD:(hh + 1) * HD], scores[:, hh, :],
                                            start=False, stop=True, skip_group_check=True)
            last.then_inc(s["y_done"], 1)
            pe.wait_ge(s["rate_done"], c + 1)
            for b in range(BATCH):
                for g in range(GROUPS):
                    last = nc.tensor.transpose(bank[3 + b][:, g * P:(g + 1) * P], rate[:, b, g * HG:(g + 1) * HG, :], hold["ident"][:])
                last.then_inc(s["rate_turned"], 1)
            for b in range(BATCH):
                pe.wait_ge(s["yT_done"], 2 * c + b + 1)
                if b == 0:
                    pe.wait_ge(s["state_added"], c + 1)
                else:
                    wait_later(pe, s["res_done"], 2 * c)
                for g in range(GROUPS):
                    last = nc.tensor.matmul(bank[6 + b][:], yT[:, b, g * P:(g + 1) * P], wout[:, g, :], start=(g == 0), stop=(g == GROUPS - 1))
                last.then_inc(s["out_done"], 1)

        def take_projection(act, c, u, grp):
            act.wait_ge(s["proj_done"], 3 * c + grp + 1)
            if grp == 0:
                wait_later(act, s["halo_done"], c - 1)
                wait_later(act, s["convB"], c - 1)
                wait_later(act, s["convX"], c - 1)
            nc.scalar.activation(proj[u][:, grp * 4:grp * 4 + 4, HALO:], bank[grp][:].rearrange("p (m t) -> p m t", m=4), ACT.Copy).then_inc(s["proj_out"], 1)

        def spread_c(act, c):
            act.wait_ge(s["convC"], c + 1)
            wait_later(act, s["scores_done"], 4 * c)
            for h in range(HG):
                r = slice(h * HD, (h + 1) * HD)
                last = nc.scalar.activation(cbd[r, :, h, :], conv[r, 0:GROUPS, :], ACT.Copy)
            last.then_inc(s["cbd_done"], 1)

        def take_turned(act, c):
            act.wait_ge(s["b_turned"], c + 1)
            wait_later(act, s["state_done"], c)
            nc.scalar.activation(btok[:], bank[3][:], ACT.Copy).then_inc(s["btok_done"], 1)
            for b in range(BATCH):
                act.wait_ge(s["rate_turned"], 2 * c + b + 1)
                wait_later(act, s["yT_done"], 2 * c - 1 + b)
                nc.scalar.activation(rateT[:, b, :], bank[3 + b][:], ACT.Copy).then_inc(s["rateT_done"], 1)

        def convolve(dve, c, u, m0, done, first):
            for k in range(TAPS):
                if k:
                    dve.wait_ge(s["conv_tap"], 6 * c + first + k)
                for m in range(m0, m0 + 4):
                    src = proj[u][:, m, k:k + P]
                    if k == 0:
                        last = nc.vector.tensor_scalar(conv[:, m, :], src, taps[:, m, 0:1], convb[:, m:m + 1], ALU.mult, ALU.add)
                    else:
                        last = nc.vector.scalar_tensor_tensor(conv[:, m, :], src, taps[:, m, k:k + 1], conv[:, m, :], ALU.mult, ALU.add)
                last.then_inc(s["conv_tap"] if k < TAPS - 1 else done, 1)

        def convolve_x(pool, c, u):
            for k in range(TAPS):
                nc.gpsimd.tensor_tensor(product[k % 2][:], proj[u][:, 8:12, k:k + P], broadcast(taps[:, 8:12, k:k + 1], [P, 4, P]),
                                        ALU.mult).then_inc(s["conv_tapX"], 1)
                pool.wait_ge(s["conv_tapX"], 7 * c + 2 * k + 1)
                so_far = conv[:, 8:12, :] if k else broadcast(convb[:, 8:12].unsqueeze(2), [P, 4, P])
                last = nc.gpsimd.tensor_tensor(conv[:, 8:12, :], so_far, product[k % 2][:], ALU.add)
                if k < TAPS - 1:
                    last.then_inc(s["conv_tapX"], 1)
                else:
                    last.then_inc(s["convX"], 1)

        def vector_chunk(dve, c, u, half):
            dve.wait_ge(s["proj_out"], 3 * c + 3)
            wait_later(dve, s["halo_done"], c)
            wait_later(dve, s["y_done"], c)
            convolve(dve, c, u, 0, s["convC"], 0)
            convolve(dve, c, u, 4, s["convB"], 3)
            dve.wait_ge(s["x_turned"], c + 1)
            nc.vector.tensor_tensor(xs[:].rearrange("p (h d) -> p h d", h=HEADS), bank[4][:].rearrange("p (h d) -> p h d", h=HEADS),
                                    broadcast(hold["decay"][:, bass.ds(c, 1), :].rearrange("p o h -> p (o h)").unsqueeze(2), [P, HEADS, HD]),
                                    ALU.mult).then_inc(s["xs_done"], 1)
            for g in range(GROUPS):
                dve.wait_ge(s["scores_done"], 4 * c + g + 1)
                nc.vector.tensor_tensor(scores[:, g * HG:(g + 1) * HG, :], bank[3 + g % 2][:].rearrange("p (h l) -> p h l", h=HG),
                                        broadcast(hold["tri"][:].unsqueeze(1), [P, HG, P]), ALU.mult).then_inc(s["scores_masked"], 1)
            dve.wait_ge(s["y_done"], c + 1)
            dve.wait_ge(s["state_done"], c + 1)
            for h in range(HG):
                r = slice(h * HD, (h + 1) * HD)
                last = nc.vector.tensor_tensor(state[r, :, r], bank[6][r, :].rearrange("p (g q) -> p g q", g=GROUPS)[:, :, r], state[r, :, r], ALU.add)
            last.then_inc(s["state_added"], 1)
            for b in range(BATCH):
                dve.wait_ge(s["rateT_done"], 2 * c + b + 1)
                wait_later(dve, s["out_done"], 2 * c - 1 + b)
                nc.vector.tensor_tensor(yT[:, b, :], bank[5][:], rateT[:, b, :], ALU.mult).then_inc(s["yT_done"], 1)
            dve.wait_ge(x_arrived[u], 16 * (half + 1))
            wait_later(dve, x1_stored[u], 16 * half)
            for b in range(BATCH):
                dve.wait_ge(s["out_done"], 2 * c + b + 1)
                nc.vector.tensor_tensor(xr[:, b, :], bank[6 + b][:], x_in[u][:, b, :], ALU.add).then_inc(s["res_done"], 1)
            dve.wait_ge(s["res_done"], 2 * c + 2)
            layernorm(nc, dve, s["ln_step"], LN_STEPS * c, [xr[:, b, :] for b in range(BATCH)], stats,
                      [x1[u][:, b, :] for b in range(BATCH)]).then_inc(s["x1_done"], 1)

        def pool_chunk(pool, c, u):
            pool.wait_ge(s["proj_out"], 3 * c + 3)
            wait_later(pool, s["halo_done"], c)
            wait_later(pool, s["x_turned"], c)
            convolve_x(pool, c, u)

        def pass_halo(act, c, u):
            act.wait_ge(s["proj_out"], 3 * c + 3)
            wait_later(act, s["convB"], c)
            wait_later(act, s["convX"], c)
            nc.scalar.activation(proj[1 - u][:, :, 0:HALO], proj[u][:, :, P:P + HALO], ACT.Copy).then_inc(s["halo_done"], 1)

        def spread_rates(act, c):
            wait_later(act, s["rate_turned"], 2 * c)
            for b in range(BATCH):
                last = nc.scalar.activation(rate[:, b, :, :], broadcast(hold["rate"][:, b, bass.ds(c, 1), :].rearrange("p o h -> p (o h)").unsqueeze(2), [P, HEADS, HD]), ACT.Copy)
            last.then_inc(s["rate_done"], 1)

        def pairs(eng, body):
            for c in (0, 1):
                body(c, c, 0)
            with eng.Fori(1, CHUNKS // 2 - 1) as i:
                for u in (0, 1):
                    body(2 * i + u, u, i)
            for c in (LAST - 1, LAST):
                body(c, c % 2, c // 2)

        with nc.Block() as block:
            @block.sync
            def _(sp):
                for k in range(KC):
                    sp.dma_start(win[:, k, :], io["WinT"][k * P:(k + 1) * P, 0:CONV]).then_inc(s["weights_in"], 16)
                load(sp, 0, 0)
                sp.dma_start(taps[:], io["conv_w"]).then_inc(s["weights_in"], 16)
                sp.dma_start(convb[:], io["conv_b"]).then_inc(s["weights_in"], 16)
                sp.dma_start(wout[:], io["WoutT"].rearrange("(k p) n -> p k n", p=P)).then_inc(s["weights_in"], 16)
                load(sp, 1, 1)

                def step(c, u, half):
                    if not (isinstance(c, int) and c < 2):
                        load(sp, c, u)
                        store(sp, c - 2, u)
                pairs(sp, step)
                store(sp, LAST - 1, 0)
                store(sp, LAST, 1)
                for u in range(2):
                    sp.wait_ge(x1_stored[u], 16 * CHUNKS // 2)

            @block.tensor
            def _(pe):
                pe.wait_ge(s["weights_in"], 7 * 16)
                pe.wait_ge(s["zeros"], 3)
                project(pe, 0, 0, 0)

                def step(c, u, half):
                    if not (isinstance(c, int) and c == LAST):
                        project(pe, c + 1, 1 - u, half + u)
                    attend(pe, c)
                pairs(pe, step)

            @block.scalar
            def _(act):
                for grp in range(3):
                    take_projection(act, 0, 0, grp)
                pass_halo(act, 0, 0)

                def step(c, u, half):
                    more = not (isinstance(c, int) and c == LAST)
                    act.wait_ge(s["zeros"], 3)
                    if more:
                        take_projection(act, c + 1, 1 - u, 0)
                    spread_c(act, c)
                    if more:
                        take_projection(act, c + 1, 1 - u, 1)
                        take_projection(act, c + 1, 1 - u, 2)
                        pass_halo(act, c + 1, 1 - u)
                    spread_rates(act, c)
                    take_turned(act, c)
                pairs(act, step)

            @block.gpsimd
            def _(pool):
                nc.gpsimd.memset(cbd[:], 0.0).then_inc(s["zeros"], 1)
                nc.gpsimd.memset(proj[0][:, :, 0:HALO], 0.0).then_inc(s["zeros"], 1)
                nc.gpsimd.memset(state[:], 0.0).then_inc(s["zeros"], 1)
                pool.wait_ge(s["weights_in"], 7 * 16)
                pool.wait_ge(s["zeros"], 3)
                pairs(pool, lambda c, u, half: pool_chunk(pool, c, u))

            @block.vector
            def _(dve):
                dve.wait_ge(s["weights_in"], 7 * 16)
                dve.wait_ge(s["zeros"], 3)
                pairs(dve, lambda c, u, half: vector_chunk(dve, c, u, half))


def prefetch(sp, io, ring, ring_in, e, unit):
    kind, half = unit // 2, unit % 2
    if kind < 2:
        src = (io["e_W1"], io["e_Wg"])[kind].rearrange("e (p k) f -> e p (k f)", p=P)[bass.ds(e, 1), :, half * UNIT:(half + 1) * UNIT]
        dst = ring[:, unit, :]
        sp.dma_start(dst, src.rearrange("o p f -> (o p) f")).then_inc(ring_in[unit], 16)
    else:
        src = io["e_W2"].rearrange("e (q p s) n -> e p q (s n)", q=4, p=P)[bass.ds(e, 1), :, 2 * half:2 * half + 2, :]
        dst = ring[:, unit, :].rearrange("p (q n) -> p q n", q=2)
        sp.dma_start(dst, src.rearrange("o p q n -> (o p) q n")).then_inc(ring_in[unit], 16)


def cross_stage(nc, io, hold, ring, ring_in):
    with Stage(nc, "crs") as st:
        wq = st.sb("wq", [P, KC, D])
        wo = st.sb("wo", [P, KC, D])
        qbias = st.sb("qbias", [P, GROUPS])
        ob = st.sb("ob", [P, D])
        x1 = [st.sb(f"x1_{i}", [P, D]) for i in range(2)]
        x1b = st.sb("x1b", [P, D])
        x1T = st.sb("x1T", [P, KC, P])
        qT = st.sb("qT", [P, GROUPS, P])
        sc = st.sb("sc", [P, GROUPS, HG, CTX])
        pr = st.sb("pr", [P, GROUPS, KROWS])
        top = st.sb("top", [P, HEADS])
        den = st.sb("den", [P, HEADS])
        rden = st.sb("rden", [P, HEADS])
        prT = st.sb("prT", [PIECE, 3, GROUPS * P])
        y = st.sb("y", [P, D])
        yT = st.sb("yT", [P, KC, P])
        xr = st.sb("xr", [P, D])
        stats = st.sb("stats", [P, 1, 12])
        x2 = [st.sb(f"x2_{i}", [P, D]) for i in range(2)]
        x2T = [st.sb(f"x2T{i}", [P, KC, P]) for i in range(2)]
        tile_top = st.sb("tile_top", [P, SM])
        new_top = st.sb("new_top", [P, SM])
        drop = st.sb("drop", [P, SM])
        shift = st.sb("shift", [P, SM])
        alpha = st.sb("alpha", [P, SM])
        tile_sum = st.sb("tile_sum", [P, SM])
        sp_pr = st.sb("sp_pr", [P, SM, P])
        sp_prT = st.sb("sp_prT", [P, SROWS])
        bank = st.banks()
        s = st.sems("weights_in", "zeros", "mix_turned", "x1T_done", "q_done", "qT_done", "sc_done", "sc_out", "top_done", "shifted", "exp_done",
                    "den_done", "rden_done", "pr_turned", "prT_done", "av_done", "y_done", "y_turned", "yT_done", "o_done", "x1b_done",
                    "res_done", "ln_step", "x2_done", "x2_turned", "x2T_done", "slot_sc", "slot_step", "slot_shift", "slot_alpha", "slot_exp", "slot_sum",
                    "slot_turned", "sp_prT_done", "z_done", "z_added")
        x1_in, x2_stored, x2T_stored = st.pair("x1_in"), st.pair("x2_stored"), st.pair("x2T_stored")
        LAST = TILES - 1

        def load(sp, t, u, half):
            wait_later(sp, s["mix_turned"], t - 1)
            wait_later(sp, s["x1b_done"], t - 1)
            sp.dma_start(x1[u][:], io["x1"][bass.ds(t * P, P), :]).then_inc(x1_in[u], 16)

        def store_x2(sp, t, u):
            sp.wait_ge(s["x2_done"], t + 1)
            sp.dma_start(io["x2"][bass.ds(t * P, P), :], x2[u][:]).then_inc(x2_stored[u], 16)

        def store_x2T(sp, t, u):
            sp.wait_ge(s["x2T_done"], t + 1)
            sp.dma_start(io["x2T"][bass.ds(t * P, P), :], x2T[u][:].rearrange("p k t -> p (k t)")).then_inc(x2T_stored[u], 16)

        def turn_x1(pe, t, u, half):
            pe.wait_ge(x1_in[u], 16 * (half + 1))
            wait_later(pe, s["yT_done"], t - 1)
            for k in range(KC):
                last = nc.tensor.transpose(bank[4][:, k * P:(k + 1) * P], x1[u][:, k * P:(k + 1) * P], hold["ident"][:])
            last.then_inc(s["mix_turned"], 1)

        def queries(pe, t):
            pe.wait_ge(s["x1T_done"], t + 1)
            wait_later(pe, s["res_done"], t - 1)
            for g in range(GROUPS):
                for k in range(KC):
                    last = nc.tensor.matmul(bank[5][:, g * P:(g + 1) * P], wq[:, k, g * P:(g + 1) * P], x1T[:, k, :],
                                            start=(k == 0), stop=(k == KC - 1))
            last.then_inc(s["q_done"], 1)

        def score(pe, t, b):
            pe.wait_ge(s["qT_done"], t + 1)
            wait_later(pe, s["prT_done"], 3 * t)
            wait_later(pe, s["y_done"], t)
            for g in range(GROUPS):
                nc.tensor.matmul(bank[g][:, 0:KROWS], qT[:, g, :], hold["kbd"][:, bass.ds(b, 1), g, :, :], start=True, stop=True).then_inc(s["sc_done"], 1)

        def turn_probs(pe, t):
            pe.wait_ge(s["exp_done"], t + 1)
            for i, w in enumerate(PIECES):
                for g in range(GROUPS):
                    last = nc.tensor.transpose(bank[i][0:w, g * P:(g + 1) * P], pr[:, g, i * PIECE:i * PIECE + w], hold["ident"][:])
                last.then_inc(s["pr_turned"], 1)

        def weigh_values(pe, t, b):
            pe.wait_ge(s["prT_done"], 3 * t + 3)
            for g in range(GROUPS):
                for i, w in enumerate(PIECES):
                    last = nc.tensor.matmul(bank[3][:, g * P:(g + 1) * P], prT[0:w, i, g * P:(g + 1) * P], hold["vbd"][0:w, bass.ds(b, 1), i, g, :],
                                            start=(i == 0), stop=(i == 2))
            last.then_inc(s["av_done"], 1)

        def turn_y(pe, t):
            pe.wait_ge(s["y_done"], t + 1)
            wait_later(pe, s["x2T_done"], t)
            for k in range(KC):
                last = nc.tensor.transpose(bank[4][:, k * P:(k + 1) * P], y[:, k * P:(k + 1) * P], hold["ident"][:])
            last.then_inc(s["y_turned"], 1)

        def project_out(pe, t, last_tile):
            pe.wait_ge(s["yT_done"], t + 1)
            if not last_tile:
                pe.wait_ge(s["qT_done"], t + 2)
            for k in range(KC):
                last = nc.tensor.matmul(bank[5][:], yT[:, k, :], wo[:, k, :], start=(k == 0), stop=(k == KC - 1))
            last.then_inc(s["o_done"], 1)

        def turn_x2(pe, t, u):
            pe.wait_ge(s["x2_done"], t + 1)
            for k in range(KC):
                last = nc.tensor.transpose(bank[4][:, k * P:(k + 1) * P], x2[u][:, k * P:(k + 1) * P], hold["ident"][:])
            last.then_inc(s["x2_turned"], 1)

        def slot_scores(pe, t, u):
            pe.wait_ge(s["x2T_done"], t + 1)
            wait_later(pe, s["z_added"], 2 * t - 1)
            for m in range(SM):
                for k in range(KC):
                    last = nc.tensor.matmul(bank[6][:, m * P:(m + 1) * P], hold["m1"][:, k, m * P:(m + 1) * P], x2T[u][:, k, :],
                                            start=(k == 0), stop=(k == KC - 1))
            last.then_inc(s["slot_sc"], 1)

        def turn_slots(pe, t):
            pe.wait_ge(s["slot_exp"], t + 1)
            wait_later(pe, s["z_added"], 2 * t)
            for m in range(SM):
                last = nc.tensor.transpose(bank[7][:, m * P:(m + 1) * P], sp_pr[:, m, :], hold["ident"][:])
            last.then_inc(s["slot_turned"], 1)

        def weigh_tokens(pe, t, u, m):
            pe.wait_ge(s["sp_prT_done"], t + 1)
            nc.tensor.matmul(bank[6 + m][:], sp_prT[:, m * P:(m + 1) * P], x2[u][:], start=True, stop=True).then_inc(s["z_done"], 1)

        def take_x1T(act, t):
            act.wait_ge(s["mix_turned"], t + 1)
            wait_later(act, s["q_done"], t)
            nc.scalar.activation(x1T[:].rearrange("p k t -> p (k t)"), bank[4][:], ACT.Copy).then_inc(s["x1T_done"], 1)

        def exponents(act, t):
            act.wait_ge(s["shifted"], t + 1)
            nc.scalar.activation(pr[:], pr[:], ACT.Exp).then_inc(s["exp_done"], 1)

        def take_x2T(act, t, u, half):
            act.wait_ge(s["x2_turned"], t + 1)
            wait_later(act, s["slot_sc"], t - 1)
            wait_later(act, x2T_stored[u], 16 * half)
            nc.scalar.activation(x2T[u][:].rearrange("p k t -> p (k t)"), bank[4][:], ACT.Copy).then_inc(s["x2T_done"], 1)

        def slot_exponents(act, t):
            act.wait_ge(s["slot_shift"], t + 1)
            wait_later(act, s["z_added"], 2 * t)
            wait_later(act, s["slot_sum"], 2 * t)
            nc.scalar.activation(alpha[:], drop[:], ACT.Exp).then_inc(s["slot_alpha"], 1)
            wait_later(act, s["slot_turned"], t)
            for m in range(SM):
                last = nc.scalar.activation(sp_pr[:, m, :], bank[6][:, m * P:(m + 1) * P], ACT.Exp, bias=shift[:, m:m + 1], scale=SCALE,
                                            accum_out=tile_sum[:, m:m + 1])
            last.then_inc(s["slot_exp"], 1)

        def take_probsT(act, t):
            wait_later(act, s["av_done"], t)
            for i, w in enumerate(PIECES):
                act.wait_ge(s["pr_turned"], 3 * t + i + 1)
                nc.scalar.activation(prT[0:w, i, :], bank[i][0:w, :], ACT.Copy).then_inc(s["prT_done"], 1)

        def take_slotsT(act, t):
            act.wait_ge(s["slot_turned"], t + 1)
            wait_later(act, s["z_done"], 2 * t)
            nc.scalar.activation(sp_prT[:], bank[7][:, 0:SROWS], ACT.Copy).then_inc(s["sp_prT_done"], 1)

        def take_yT(act, t):
            act.wait_ge(s["y_turned"], t + 1)
            wait_later(act, s["o_done"], t)
            nc.scalar.activation(yT[:].rearrange("p k t -> p (k t)"), bank[4][:], ACT.Copy).then_inc(s["yT_done"], 1)

        def take_scores(dve, t):
            wait_later(dve, s["shifted"], t)
            for g in range(GROUPS):
                dve.wait_ge(s["sc_done"], 4 * t + g + 1)
                last = nc.vector.scalar_tensor_tensor(sc[:, g, :, :], bank[g][:, 0:KROWS].rearrange("p (h s) -> p h s", h=HG), SCALE,
                                                      broadcast(hold["mask"][:, bass.ds(t * CTX, CTX)].unsqueeze(1), [P, HG, CTX]), ALU.mult, ALU.add)
            last.then_inc(s["sc_out"], 1)
            dve.wait_ge(s["sc_out"], t + 1)
            nc.vector.tensor_reduce(top[:].rearrange("p (g h) -> p g h", g=GROUPS), sc[:], AX.X, ALU.max).then_inc(s["top_done"], 1)

        def take_queries(dve, t):
            dve.wait_ge(s["q_done"], t + 1)
            wait_later(dve, s["sc_done"], 4 * t)
            nc.vector.tensor_tensor(qT[:], bank[5][:].rearrange("p (g t) -> p g t", g=GROUPS), broadcast(qbias[:].unsqueeze(2), [P, GROUPS, P]),
                                    ALU.add).then_inc(s["qT_done"], 1)

        def slot_maxima(dve, t, b):
            st_top = hold["top"][:, bass.ds(b, 1), :].rearrange("p o m -> p (o m)")
            dve.wait_ge(s["slot_sc"], t + 1)
            wait_later(dve, s["slot_exp"], t)
            first = 3 * t
            nc.vector.tensor_reduce(tile_top[:], bank[6][:, 0:SROWS].rearrange("p (m t) -> p m t", m=SM), AX.X, ALU.max).then_inc(s["slot_step"], 1)
            dve.wait_ge(s["slot_step"], first + 1)
            nc.vector.scalar_tensor_tensor(tile_top[:], tile_top[:], SCALE, hold["kbias"][:], ALU.mult, ALU.add).then_inc(s["slot_step"], 1)
            dve.wait_ge(s["slot_step"], first + 2)
            nc.vector.tensor_tensor(new_top[:], st_top, tile_top[:], ALU.max).then_inc(s["slot_step"], 1)
            dve.wait_ge(s["slot_step"], first + 3)
            nc.vector.tensor_tensor(drop[:], st_top, new_top[:], ALU.subtract)
            nc.vector.tensor_tensor(shift[:], hold["kbias"][:], new_top[:], ALU.subtract).then_inc(s["slot_shift"], 1)
            dve.wait_ge(s["slot_shift"], t + 1)
            nc.vector.tensor_copy(st_top, new_top[:])

        def denominators(dve, t):
            dve.wait_ge(s["exp_done"], t + 1)
            nc.vector.tensor_reduce(den[:], pr[:].rearrange("p g (h s) -> p (g h) s", h=HG), AX.X, ALU.add).then_inc(s["den_done"], 1)
            dve.wait_ge(s["den_done"], t + 1)
            nc.vector.reciprocal(rden[:], den[:]).then_inc(s["rden_done"], 1)

        def slot_sums(dve, t, b):
            st_sum = hold["sum"][:, bass.ds(b, 1), :].rearrange("p o m -> p (o m)")
            dve.wait_ge(s["slot_exp"], t + 1)
            nc.vector.tensor_tensor(st_sum, st_sum, alpha[:], ALU.mult).then_inc(s["slot_sum"], 1)
            dve.wait_ge(s["slot_sum"], 2 * t + 1)
            nc.vector.tensor_tensor(st_sum, st_sum, tile_sum[:], ALU.add).then_inc(s["slot_sum"], 1)

        def normalise(dve, t):
            dve.wait_ge(s["rden_done"], t + 1)
            dve.wait_ge(s["av_done"], t + 1)
            wait_later(dve, s["y_turned"], t)
            nc.vector.tensor_tensor(y[:].rearrange("p (h d) -> p h d", h=HEADS), bank[3][:].rearrange("p (h d) -> p h d", h=HEADS),
                                    broadcast(rden[:].unsqueeze(2), [P, HEADS, HD]), ALU.mult).then_inc(s["y_done"], 1)

        def add_tokens(dve, t, b, m):
            z = hold["z"][:, bass.ds(b, 1), m, :].rearrange("p o d -> p (o d)")
            dve.wait_ge(s["z_done"], 2 * t + m + 1)
            nc.vector.scalar_tensor_tensor(z, z, alpha[:, m:m + 1], bank[6 + m][:], ALU.mult, ALU.add).then_inc(s["z_added"], 1)

        def residual(dve, t, u, half):
            dve.wait_ge(s["o_done"], t + 1)
            dve.wait_ge(s["x1b_done"], t + 1)
            nc.vector.tensor_tensor(xr[:], bank[5][:], x1b[:], ALU.add).then_inc(s["res_done"], 1)
            dve.wait_ge(s["res_done"], t + 1)
            wait_later(dve, x2_stored[u], 16 * half)
            wait_later(dve, s["z_done"], 2 * t - 2)
            layernorm(nc, dve, s["ln_step"], LN_STEPS * t, [xr[:]], stats, [x2[u][:]]).then_inc(s["x2_done"], 1)

        def pool_tile(pool, t, u, half):
            pool.wait_ge(x1_in[u], 16 * (half + 1))
            wait_later(pool, s["res_done"], t)
            nc.gpsimd.tensor_tensor(x1b[:], x1[u][:], ob[:], ALU.add).then_inc(s["x1b_done"], 1)
            pool.wait_ge(s["top_done"], t + 1)
            wait_later(pool, s["pr_turned"], 3 * t)
            wait_later(pool, s["den_done"], t)
            nc.gpsimd.tensor_tensor(pr[:].rearrange("p g (h s) -> p (g h) s", h=HG), sc[:].rearrange("p g h s -> p (g h) s"),
                                    broadcast(top[:].unsqueeze(2), [P, HEADS, CTX]), ALU.subtract).then_inc(s["shifted"], 1)

        def tiles(eng, body):
            for t in (0, 1):
                body(t, t, 0, 0, 0, False)
            with eng.Fori(1, CHUNKS // 2) as i:
                for u in (0, 1):
                    body(2 * i + u, u, i, 0, 0, False)
            t0 = CHUNKS
            for u in (0, 1):
                body(t0 + u, u, t0 // 2, 1, 1 if u else 0, False)
            with eng.Fori(CHUNKS // 2 + 1, TILES // 2 - 1) as i:
                for u in (0, 1):
                    body(2 * i + u, u, i, 1, 1, False)
            for u in (0, 1):
                body(LAST - 1 + u, u, TILES // 2 - 1, 1, 1, u == 1)

        def first(t):
            return isinstance(t, int) and t == 0

        with nc.Block() as block:
            @block.sync
            def _(sp):
                sp.dma_start(wq[:], io["q_w"].rearrange("(k p) n -> p k n", p=P)).then_inc(s["weights_in"], 16)
                sp.dma_start(wo[:], io["o_w"].rearrange("(k p) n -> p k n", p=P)).then_inc(s["weights_in"], 16)
                sp.dma_start(qbias[:], io["q_b"]).then_inc(s["weights_in"], 16)
                sp.dma_start(ob[:], broadcast(io["o_b"].rearrange("(o n) -> o n", o=1), [P, D])).then_inc(s["weights_in"], 16)
                load(sp, 0, 0, 0)

                def step(t, u, half, b, bp, last):
                    if not last:
                        load(sp, t + 1, 1 - u, half + u)
                    if not first(t):
                        store_x2(sp, t - 1, 1 - u)
                    if not (isinstance(t, int) and t < 2):
                        store_x2T(sp, t - 2, u)
                    if isinstance(t, int) and t == 1:
                        for unit in range(UNITS):
                            prefetch(sp, io, ring, ring_in, 0, unit)
                tiles(sp, step)
                store_x2(sp, LAST, 1)
                store_x2T(sp, LAST - 1, 0)
                store_x2T(sp, LAST, 1)
                for u in range(2):
                    sp.wait_ge(x2_stored[u], 16 * TILES // 2)
                    sp.wait_ge(x2T_stored[u], 16 * TILES // 2)

            @block.tensor
            def _(pe):
                pe.wait_ge(s["weights_in"], 4 * 16)
                turn_x1(pe, 0, 0, 0)
                queries(pe, 0)

                def step(t, u, half, b, bp, last):
                    if not last:
                        turn_x1(pe, t + 1, 1 - u, half + u)
                    score(pe, t, b)
                    if not last:
                        queries(pe, t + 1)
                    if not first(t):
                        turn_x2(pe, t - 1, 1 - u)
                        slot_scores(pe, t - 1, 1 - u)
                    turn_probs(pe, t)
                    if not first(t):
                        turn_slots(pe, t - 1)
                    weigh_values(pe, t, b)
                    if not first(t):
                        weigh_tokens(pe, t - 1, 1 - u, 0)
                    turn_y(pe, t)
                    if not first(t):
                        weigh_tokens(pe, t - 1, 1 - u, 1)
                    project_out(pe, t, last)
                tiles(pe, step)
                turn_x2(pe, LAST, 1)
                slot_scores(pe, LAST, 1)
                turn_slots(pe, LAST)
                for m in range(SM):
                    weigh_tokens(pe, LAST, 1, m)

            @block.scalar
            def _(act):
                take_x1T(act, 0)

                def step(t, u, half, b, bp, last):
                    if not last:
                        take_x1T(act, t + 1)
                    exponents(act, t)
                    if not first(t):
                        take_x2T(act, t - 1, 1 - u, half - 1 + u)
                        slot_exponents(act, t - 1)
                    take_probsT(act, t)
                    if not first(t):
                        take_slotsT(act, t - 1)
                    take_yT(act, t)
                tiles(act, step)
                take_x2T(act, LAST, 1, TILES // 2 - 1)
                slot_exponents(act, LAST)
                take_slotsT(act, LAST)

            @block.vector
            def _(dve):
                nc.vector.memset(hold["top"][:], NEG)
                nc.vector.memset(hold["sum"][:], 0.0)
                nc.vector.memset(hold["z"][:], 0.0).then_inc(s["zeros"], 1)
                dve.wait_ge(s["zeros"], 1)
                dve.wait_ge(s["weights_in"], 4 * 16)
                take_queries(dve, 0)

                def step(t, u, half, b, bp, last):
                    take_scores(dve, t)
                    if not last:
                        take_queries(dve, t + 1)
                    if not first(t):
                        slot_maxima(dve, t - 1, bp)
                    denominators(dve, t)
                    if not first(t):
                        slot_sums(dve, t - 1, bp)
                    normalise(dve, t)
                    if not first(t):
                        for m in range(SM):
                            add_tokens(dve, t - 1, bp, m)
                    residual(dve, t, u, half)
                tiles(dve, step)
                slot_maxima(dve, LAST, 1)
                slot_sums(dve, LAST, 1)
                for m in range(SM):
                    add_tokens(dve, LAST, 1, m)

            @block.gpsimd
            def _(pool):
                pool.wait_ge(s["weights_in"], 4 * 16)
                tiles(pool, lambda t, u, half, b, bp, last: pool_tile(pool, t, u, half))


ROWS = BATCH * SLOTS


def experts_stage(nc, io, hold, ring, ring_in):
    with Stage(nc, "exp") as st:
        dwv = st.sb("dwv", [P, KC, D])
        dwo = st.sb("dwo", [P, KC, D])
        dbv = st.sb("dbv", [P, GROUPS])
        dbo = st.sb("dbo", [ROWS, D])
        slot = st.sb("slot", [ROWS, D])
        ln_g = st.sb("ln_g", [ROWS, D])
        ln_b = st.sb("ln_b", [ROWS, D])
        b2 = st.sb("b2", [ROWS, D])
        rsum = st.sb("rsum", [P, BATCH, SM])
        znT = st.sb("znT", [P, KC, BATCH, SROWS])
        aoT = st.sb("aoT", [P, GROUPS, BATCH, SLOTS])
        o = st.sb("o", [ROWS, D])
        h = st.sb("h", [ROWS, D])
        stats = st.sb("stats", [ROWS, 1, 12])
        hT = st.sb("hT", [P, KC, ROWS])
        pick = st.sb("pick", [P, EXPERTS, ROWS])
        fold = st.sb("fold", [P, ROWS])
        hm = [st.sb(f"hm{i}", [P, KC, ROWS]) for i in range(2)]
        pm = [st.sb(f"pm{i}", [P, 4, ROWS]) for i in range(2)]
        quarter = st.sb("quarter", [P, 4, ROWS])
        bias = st.sb("bias", [P, 2, FQ])
        up = st.sb("up", [P, FQ])
        gate = st.sb("gate", [P, FQ])
        gu = st.sb("gu", [P, FQ])
        guT = st.sb("guT", [P, 4, P])
        y4 = st.sb("y4", [P, D])
        cwk, cwqT = dwv, dwo
        cwv = shaped(znT[:].rearrange("p k b r -> p (k b r)"), [P, KC, D])
        cwo = shaped(hold["z"][:].rearrange("p b m d -> p (b m d)"), [P, KC, D])
        cbk = st.sb("cbk", [P, GROUPS])
        cbv = st.sb("cbv", [P, GROUPS])
        cbq = st.sb("cbq", [P, GROUPS])
        cbqb = st.sb("cbqb", [P, GROUPS, P])
        oT = st.sb("oT", [P, KC, ROWS])
        kbd = st.sb("kbd", [P, GROUPS, BATCH, HG, SLOTS])
        vbd = st.sb("vbd", [P, GROUPS, BATCH, HG, SLOTS])
        bank = st.banks()
        s = st.sems("slot_w_in", "rows_in", "comb_w_in", "zeros", "consts", "rsum_done", "zn_done", "zn_turned", "znT_done", "ao_done", "aoT_done",
                    "wo_done", "o_step", "ln_step", "h_turned", "hT_done", "hm_done", "bias_in", "up_done", "silu_done", "gu_done",
                    "gu_turned", "guT_done", "y4_done", "fold_done", "o_done", "o_turned", "oT_done",
                    "k_done", "kbd_done", "v_done", "vbd_done", "qb_done", "m2_done", "m2_out", "kb_done", "vo_done", "vo_out")
        unit_used = [st.sem(f"unit_used{i}") for i in range(UNITS)]

        def expert(pe, e, u):
            pe.wait_ge(s["hm_done"], e + 1)
            wait_later(pe, s["silu_done"], 2 * e)
            pe.wait_ge(s["bias_in"], 32 * (e + 1))
            for w in range(2):
                for k in range(KC):
                    if k % 2 == 0:
                        pe.wait_ge(ring_in[2 * w + k // 2], 16 * (e + 1))
                    for q in range(4):
                        at = (k % 2) * F + q * FQ
                        last = nc.tensor.matmul(bank[w][q * ROWS:(q + 1) * ROWS, :], hm[u][:, k, :], ring[:, 2 * w + k // 2, at:at + FQ],
                                                start=(k == 0), stop=False)
                    if k % 2 == 1:
                        last.then_inc(unit_used[2 * w + k // 2], 1)
                for q in range(4):
                    last = nc.tensor.matmul(bank[w][q * ROWS:(q + 1) * ROWS, :], pm[u][:, q, :], bias[:, w, :], start=False, stop=True)
                last.then_inc(s["up_done"], 1)
            pe.wait_ge(s["gu_done"], e + 1)
            wait_later(pe, s["guT_done"], e)
            for i in range(4):
                last = nc.tensor.transpose(bank[2][:, i * P:(i + 1) * P], gu[:].rearrange("r (p i) -> r i p", i=4)[:, i, :], hold["ident"][:])
            last.then_inc(s["gu_turned"], 1)
            pe.wait_ge(s["guT_done"], e + 1)
            first = isinstance(e, int) and e == 0
            final = isinstance(e, int) and e == EXPERTS - 1
            for half in range(2):
                pe.wait_ge(ring_in[4 + half], 16 * (e + 1))
                for i in range(4):
                    for j in range(2):
                        q = 2 * half + j
                        last = nc.tensor.matmul(bank[3][q * ROWS:(q + 1) * ROWS, :], guT[:, i, q * ROWS:(q + 1) * ROWS],
                                                ring[:, 4 + half, (j * 4 + i) * D:(j * 4 + i + 1) * D],
                                                start=first and i == 0, stop=final and i == 3, skip_group_check=True)
                last.then_inc(unit_used[4 + half], 1)

        def masked(dve, e, u):
            wait_later(dve, s["up_done"], 2 * e - 2)
            nc.vector.tensor_tensor(hm[u][:], hT[:], broadcast(pick[:, bass.ds(e, 1), :], [P, KC, ROWS]), ALU.mult)
            nc.vector.tensor_tensor(pm[u][:], quarter[:], broadcast(pick[:, bass.ds(e, 1), :], [P, 4, ROWS]), ALU.mult).then_inc(s["hm_done"], 1)

        def combine_up(dve, e):
            dve.wait_ge(s["silu_done"], 2 * e + 2)
            wait_later(dve, s["gu_turned"], e)
            nc.vector.tensor_tensor(gu[:], up[:], gate[:], ALU.mult).then_inc(s["gu_done"], 1)
            dve.wait_ge(s["gu_turned"], e + 1)
            wait_later(dve, unit_used[5], e)
            nc.vector.tensor_copy(guT[:].rearrange("p i r -> p (i r)"), bank[2][:]).then_inc(s["guT_done"], 1)

        def activate(act, e):
            wait_later(act, s["gu_done"], e)
            for w, dst in ((0, up), (1, gate)):
                act.wait_ge(s["up_done"], 2 * e + w + 1)
                nc.scalar.activation(dst[:], bank[w][:], ACT.Silu).then_inc(s["silu_done"], 1)

        def experts(eng, body):
            for e in (0, 1):
                body(e, e)
            with eng.Fori(1, EXPERTS // 2 - 1) as i:
                for u in (0, 1):
                    body(2 * i + u, u)
            for e in (EXPERTS - 2, EXPERTS - 1):
                body(e, e % 2)

        with nc.Block() as block:
            @block.sync
            def _(sp):
                for dst, src in ((dwv, io["d_Wv"]), (dwo, io["d_Wo"])):
                    sp.dma_start(dst[:], src.rearrange("(k p) n -> p k n", p=P)).then_inc(s["slot_w_in"], 16)
                sp.dma_start(dbv[:], io["d_bv"]).then_inc(s["slot_w_in"], 16)
                sp.dma_start(dbo[:], broadcast(io["d_bo"].rearrange("(o n) -> o n", o=1), [ROWS, D])).then_inc(s["rows_in"], 16)
                for dst, src in ((slot, io["slot"]), (ln_g, io["e_ln_g"]), (ln_b, io["e_ln_b"]), (b2, io["e_b2"])):
                    for b in range(BATCH):
                        sp.dma_start(dst[b * SLOTS:(b + 1) * SLOTS, :], src).then_inc(s["rows_in"], 16)

                def step(e, u):
                    if isinstance(e, int) and e == 0:
                        return
                    for unit in range(UNITS):
                        sp.wait_ge(unit_used[unit], e)
                        prefetch(sp, io, ring, ring_in, e, unit)
                    if isinstance(e, int) and e == 1:
                        sp.wait_ge(s["wo_done"], 1)
                        for dst, src in ((cwk, io["c_Wk"]), (cwqT, io["c_WqT"]), (cwv, io["c_Wv"]), (cwo, io["c_Wo"])):
                            sp.dma_start(dst[:], src.rearrange("(k p) n -> p k n", p=P)).then_inc(s["comb_w_in"], 16)
                        for dst, src in ((cbk, io["c_bk"]), (cbv, io["c_bv"]), (cbq, io["c_bq"])):
                            sp.dma_start(dst[:], src).then_inc(s["comb_w_in"], 16)
                experts(sp, step)

            @block.gpsimd
            def _(pool):
                nc.gpsimd.memset(pick[:], 0.0).then_inc(s["zeros"], 1)
                nc.gpsimd.memset(fold[:], 0.0).then_inc(s["zeros"], 1)
                nc.gpsimd.memset(bias[:], 0.0).then_inc(s["zeros"], 1)
                nc.gpsimd.memset(quarter[:], 0.0).then_inc(s["zeros"], 1)
                pool.wait_ge(s["zeros"], 4)
                nc.gpsimd.affine_select(out=quarter[:], in_=quarter[:], compare_op=ALU.not_equal, fill=1.0, base=0,
                                        pattern=[[-1, 4], [0, ROWS]], channel_multiplier=1).then_inc(s["consts"], 1)
                p4 = pick[:].rearrange("p e (b r) -> p e b r", b=BATCH)
                nc.gpsimd.affine_select(out=p4, in_=p4, compare_op=ALU.not_equal, fill=1.0, base=0,
                                        pattern=[[1, EXPERTS], [0, BATCH], [-1, SLOTS]], channel_multiplier=0).then_inc(s["consts"], 1)
                for q in range(4):
                    nc.gpsimd.affine_select(out=fold[:], in_=fold[:], compare_op=ALU.not_equal, fill=1.0, base=-q * ROWS,
                                            pattern=[[-1, ROWS]], channel_multiplier=1).then_inc(s["consts"], 1)
                    pool.wait_ge(s["consts"], q + 3)
                nc.gpsimd.memset(kbd[:], 0.0).then_inc(s["zeros"], 1)
                nc.gpsimd.memset(vbd[:], 0.0).then_inc(s["zeros"], 1)

                def step(e, u):
                    wait_later(pool, s["up_done"], 2 * e)
                    for w, src in ((0, io["e_b1"]), (1, io["e_bg"])):
                        pool.dma_start(bias[0:4, w, :], src.rearrange("e (q f) -> e q f", q=4)[bass.ds(e, 1), :, :].rearrange("o q f -> (o q) f")).then_inc(s["bias_in"], 16)
                experts(pool, step)
                pool.wait_ge(s["comb_w_in"], 7 * 16)
                nc.gpsimd.tensor_copy(cbqb[:], broadcast(cbq[:].unsqueeze(2), [P, GROUPS, P])).then_inc(s["qb_done"], 1)

            @block.tensor
            def _(pe):
                for b in range(BATCH):
                    for m in range(SM):
                        i = b * SM + m
                        pe.wait_ge(s["zn_done"], i + 1)
                        for k in range(KC):
                            last = nc.tensor.transpose(bank[i][:, k * P:(k + 1) * P], hold["z"][:, b, m, k * P:(k + 1) * P], hold["ident"][:])
                        last.then_inc(s["zn_turned"], 1)
                pe.wait_ge(s["slot_w_in"], 3 * 16)
                pe.wait_ge(s["znT_done"], 4)
                for g in range(GROUPS):
                    for k in range(KC):
                        last = nc.tensor.matmul(bank[4][:, g * P:(g + 1) * P], dwv[:, k, g * P:(g + 1) * P],
                                                znT[:, k, :, g * HG * SLOTS:(g + 1) * HG * SLOTS], start=(k == 0), stop=(k == KC - 1))
                last.then_inc(s["ao_done"], 1)
                pe.wait_ge(s["aoT_done"], 1)
                for g in range(GROUPS):
                    last = nc.tensor.matmul(bank[5][0:ROWS, :], aoT[:, g, :, :], dwo[:, g, :], start=(g == 0), stop=(g == GROUPS - 1))
                last.then_inc(s["wo_done"], 1)
                pe.wait_ge(s["o_step"], 4)
                for k in range(KC):
                    last = nc.tensor.transpose(bank[6][:, k * ROWS:(k + 1) * ROWS], h[:].rearrange("r (p k) -> r k p", k=KC)[:, k, :],
                                               hold["ident"][0:ROWS, 0:ROWS])
                last.then_inc(s["h_turned"], 1)
                experts(pe, lambda e, u: expert(pe, e, u))
                pe.wait_ge(s["y4_done"], 1)
                nc.tensor.matmul(bank[4][0:ROWS, :], fold[:], y4[:], start=True, stop=True).then_inc(s["fold_done"], 1)
                pe.wait_ge(s["o_done"], 1)
                for k in range(KC):
                    last = nc.tensor.transpose(bank[5][:, k * ROWS:(k + 1) * ROWS], o[:, k * P:(k + 1) * P], hold["ident"][0:ROWS, 0:ROWS])
                last.then_inc(s["o_turned"], 1)
                pe.wait_ge(s["comb_w_in"], 7 * 16)
                pe.wait_ge(s["oT_done"], 1)
                for w, bk, sem in ((cwk, bank[6], s["k_done"]), (cwv, bank[7], s["v_done"])):
                    for g in range(GROUPS):
                        for k in range(KC):
                            last = nc.tensor.matmul(bk[:, g * ROWS:(g + 1) * ROWS], w[:, k, g * P:(g + 1) * P], oT[:, k, :],
                                                    start=(k == 0), stop=(k == KC - 1))
                    last.then_inc(sem, 1)
                pe.wait_ge(s["kbd_done"], 1)
                for k in range(KC):
                    for g in range(GROUPS):
                        last = nc.tensor.matmul(bank[k][:, g * P:(g + 1) * P], cwqT[:, g, k * P:(k + 1) * P], kbd[:, g, :, :, :], start=True, stop=True)
                    last.then_inc(s["m2_done"], 1)
                pe.wait_ge(s["qb_done"], 1)
                for g in range(GROUPS):
                    last = nc.tensor.matmul(bank[6][:, g * P:(g + 1) * P], cbqb[:, g, :], kbd[:, g, :, :, :], start=True, stop=True)
                last.then_inc(s["kb_done"], 1)
                pe.wait_ge(s["vbd_done"], 1)
                half = HG * SLOTS
                for b in range(BATCH):
                    for m in range(SM):
                        out = bank[(4, 5, 7, 0)[b * SM + m]]
                        if b * SM + m == 3:
                            pe.wait_ge(s["m2_out"], 1)
                        for j in range(2):
                            last = nc.tensor.matmul(out[j * half:(j + 1) * half, :], vbd[:, 2 * m + j, b, :, :], cwo[:, 2 * m + j, :], start=True, stop=True)
                        last.then_inc(s["vo_done"], 1)

            @block.scalar
            def _(act):
                for i in range(BATCH * SM):
                    act.wait_ge(s["zn_turned"], i + 1)
                    nc.scalar.activation(znT[:, :, i // SM, (i % SM) * P:(i % SM + 1) * P], bank[i][:].rearrange("p (k r) -> p k r", k=KC),
                                         ACT.Copy).then_inc(s["znT_done"], 1)
                experts(act, lambda e, u: activate(act, e))
                for k in range(KC):
                    act.wait_ge(s["m2_done"], k + 1)
                    nc.scalar.activation(hold["m2"][:, :, k, :, :].rearrange("p b g r -> p g b r"),
                                         bank[k][:].rearrange("p (g b r) -> p g b r", g=GROUPS, b=BATCH), ACT.Copy).then_inc(s["m2_out"], 1)
                act.wait_ge(s["kb_done"], 1)
                nc.scalar.activation(hold["kb2"][:].rearrange("p b g r -> p g b r"), bank[6][:].rearrange("p (g b r) -> p g b r", g=GROUPS, b=BATCH),
                                     ACT.Copy, scale=SCALE).then_inc(s["m2_out"], 1)

            @block.vector
            def _(dve):
                nc.vector.reciprocal(rsum[:], hold["sum"][:]).then_inc(s["rsum_done"], 1)
                dve.wait_ge(s["rsum_done"], 1)
                for b in range(BATCH):
                    for m in range(SM):
                        nc.vector.tensor_scalar(hold["z"][:, b, m, :], hold["z"][:, b, m, :], rsum[:, b, m:m + 1], None, ALU.mult).then_inc(s["zn_done"], 1)
                dve.wait_ge(s["slot_w_in"], 3 * 16)
                dve.wait_ge(s["ao_done"], 1)
                for g in range(GROUPS):
                    for hh in range(HG):
                        r = slice(hh * HD, (hh + 1) * HD)
                        src = bank[4][r, g * P:(g + 1) * P].rearrange("p (b h q) -> p b h q", b=BATCH, h=HG)[:, :, hh, :]
                        last = nc.vector.tensor_scalar(aoT[r, g, :, :], src, dbv[r, g:g + 1], None, ALU.add)
                last.then_inc(s["aoT_done"], 1)
                dve.wait_ge(s["rows_in"], 9 * 16)
                nc.vector.tensor_tensor(slot[:], slot[:], dbo[:], ALU.add).then_inc(s["o_step"], 1)
                dve.wait_ge(s["o_step"], 1)
                dve.wait_ge(s["wo_done"], 1)
                nc.vector.tensor_tensor(o[:], bank[5][0:ROWS, :], slot[:], ALU.add).then_inc(s["o_step"], 1)
                dve.wait_ge(s["o_step"], 2)
                layernorm(nc, dve, s["ln_step"], 0, [o[:]], stats, [h[:]]).then_inc(s["ln_step"], 1)
                dve.wait_ge(s["ln_step"], LN_STEPS + 1)
                nc.vector.tensor_tensor(h[:], h[:], ln_g[:], ALU.mult).then_inc(s["o_step"], 1)
                dve.wait_ge(s["o_step"], 3)
                nc.vector.tensor_tensor(h[:], h[:], ln_b[:], ALU.add).then_inc(s["o_step"], 1)
                nc.vector.tensor_tensor(o[:], o[:], b2[:], ALU.add).then_inc(s["o_step"], 1)
                dve.wait_ge(s["h_turned"], 1)
                nc.vector.tensor_copy(hT[:].rearrange("p k r -> p (k r)"), bank[6][:, 0:KC * ROWS]).then_inc(s["hT_done"], 1)
                dve.wait_ge(s["hT_done"], 1)
                dve.wait_ge(s["consts"], 6)
                masked(dve, 0, 0)

                def step(e, u):
                    if not (isinstance(e, int) and e == EXPERTS - 1):
                        masked(dve, e + 1, 1 - u)
                    combine_up(dve, e)
                experts(dve, step)
                dve.wait_ge(unit_used[5], EXPERTS)
                nc.vector.tensor_copy(y4[:], bank[3][:]).then_inc(s["y4_done"], 1)
                dve.wait_ge(s["fold_done"], 1)
                dve.wait_ge(s["o_step"], 5)
                nc.vector.tensor_tensor(o[:], bank[4][0:ROWS, :], o[:], ALU.add).then_inc(s["o_done"], 1)
                dve.wait_ge(s["o_turned"], 1)
                nc.vector.tensor_copy(oT[:].rearrange("p k r -> p (k r)"), bank[5][:, 0:KC * ROWS]).then_inc(s["oT_done"], 1)
                dve.wait_ge(s["comb_w_in"], 7 * 16)
                dve.wait_ge(s["zeros"], 6)
                for src, dst, bias_, ready, done in ((bank[6], kbd, cbk, s["k_done"], s["kbd_done"]), (bank[7], vbd, cbv, s["v_done"], s["vbd_done"])):
                    dve.wait_ge(ready, 1)
                    for g in range(GROUPS):
                        for hh in range(HG):
                            r = slice(hh * HD, (hh + 1) * HD)
                            last = nc.vector.tensor_scalar(dst[r, g, :, hh, :], src[r, g * ROWS:(g + 1) * ROWS].rearrange("p (b q) -> p b q", b=BATCH),
                                                           bias_[r, g:g + 1], None, ALU.add)
                    last.then_inc(done, 1)
                for i in range(BATCH * SM):
                    dve.wait_ge(s["vo_done"], i + 1)
                    nc.vector.tensor_copy(hold["vo"][:, i // SM, i % SM, :], bank[(4, 5, 7, 0)[i]][:]).then_inc(s["vo_out"], 1)


def combine_stage(nc, io, hold):
    with Stage(nc, "cmb") as st:
        ob = st.sb("ob", [P, D])
        x2T = [st.sb(f"x2T{i}", [P, KC, P]) for i in range(2)]
        x2 = [st.sb(f"x2_{i}", [P, D]) for i in range(2)]
        x2b = [st.sb(f"x2b{i}", [P, D]) for i in range(2)]
        sc = [st.sb(f"sc{i}", [P, HEADS, SLOTS]) for i in range(2)]
        pr = [st.sb(f"pr{i}", [P, HEADS, SLOTS]) for i in range(2)]
        top = [st.sb(f"top{i}", [P, HEADS]) for i in range(2)]
        den = st.sb("den", [P, HEADS])
        rden = [st.sb(f"rden{i}", [P, HEADS]) for i in range(2)]
        prT = [st.sb(f"prT{i}", [P, SM, P]) for i in range(2)]
        xr = st.sb("xr", [P, D])
        stats = st.sb("stats", [P, 1, 12])
        out = [st.sb(f"out{i}", [P, D]) for i in range(2)]
        bank = st.banks()
        s = st.sems("ob_in", "sc_done", "sc_out", "top_done", "shifted", "exp_done", "den_done", "rden_done", "normed", "pr_turned", "prT_done",
                    "o_done", "x2b_done", "res_done", "ln_step", "out_done")
        x2T_in, x2_in, stored = st.pair("x2T_in"), st.pair("x2_in"), st.pair("stored")
        LAST = TILES - 1

        def load(sp, t, u):
            wait_later(sp, s["sc_done"], t - 1)
            sp.dma_start(x2T[u][:].rearrange("p k t -> p (k t)"), io["x2T"][bass.ds(t * P, P), :]).then_inc(x2T_in[u], 16)
            wait_later(sp, s["x2b_done"], t - 1)
            sp.dma_start(x2[u][:], io["x2"][bass.ds(t * P, P), :]).then_inc(x2_in[u], 16)

        def store(eng, t, u):
            eng.wait_ge(s["out_done"], t + 1)
            eng.dma_start(io["out"][bass.ds(t * P, P), :], out[u][:]).then_inc(stored[u], 16)

        def score(pe, t, u, half, b):
            pe.wait_ge(x2T_in[u], 16 * (half + 1))
            wait_later(pe, s["sc_out"], t - 1)
            for k in range(KC):
                last = nc.tensor.matmul(bank[u][:, 0:SROWS], x2T[u][:, k, :], hold["m2"][:, b, k, :, :], start=(k == 0), stop=(k == KC - 1))
            last.then_inc(s["sc_done"], 1)

        def turn(pe, t, u):
            pe.wait_ge(s["normed"], t + 1)
            wait_later(pe, s["prT_done"], t - 1)
            for m in range(SM):
                last = nc.tensor.transpose(bank[2 + u][:, m * P:(m + 1) * P], pr[u][:].rearrange("p h q -> p (h q)")[:, m * P:(m + 1) * P], hold["ident"][:])
            last.then_inc(s["pr_turned"], 1)

        def project_out(pe, t, u, b):
            pe.wait_ge(s["prT_done"], t + 1)
            wait_later(pe, s["res_done"], t - 1)
            for m in range(SM):
                last = nc.tensor.matmul(bank[4 + u][:], prT[u][:, m, :], hold["vo"][:, b, m, :], start=(m == 0), stop=(m == SM - 1))
            last.then_inc(s["o_done"], 1)

        def take_scores(dve, t, u, b):
            dve.wait_ge(s["sc_done"], t + 1)
            wait_later(dve, s["shifted"], t - 1)
            nc.vector.scalar_tensor_tensor(sc[u][:].rearrange("p h q -> p (h q)"), bank[u][:, 0:SROWS], SCALE,
                                           hold["kb2"][:, b, :, :].rearrange("p g r -> p (g r)"), ALU.mult, ALU.add).then_inc(s["sc_out"], 1)
            dve.wait_ge(s["sc_out"], t + 1)
            nc.vector.tensor_reduce(top[u][:], sc[u][:], AX.X, ALU.max).then_inc(s["top_done"], 1)

        def denominators(dve, t, u):
            dve.wait_ge(s["exp_done"], t + 1)
            nc.vector.tensor_reduce(den[:], pr[u][:], AX.X, ALU.add).then_inc(s["den_done"], 1)
            dve.wait_ge(s["den_done"], t + 1)
            wait_later(dve, s["normed"], t - 1)
            nc.vector.reciprocal(rden[u][:], den[:]).then_inc(s["rden_done"], 1)

        def residual(dve, t, u, half):
            dve.wait_ge(s["o_done"], t + 1)
            dve.wait_ge(s["x2b_done"], t + 1)
            wait_later(dve, s["out_done"], t)
            nc.vector.tensor_tensor(xr[:], bank[4 + u][:], x2b[u][:], ALU.add).then_inc(s["res_done"], 1)
            dve.wait_ge(s["res_done"], t + 1)
            wait_later(dve, stored[u], 16 * half)
            layernorm(nc, dve, s["ln_step"], LN_STEPS * t, [xr[:]], stats, [out[u][:]]).then_inc(s["out_done"], 1)

        def tiles(eng, body):
            for t in (0, 1):
                body(t, t, 0, 0, 0)
            with eng.Fori(1, CHUNKS // 2 - 1) as i:
                for u in (0, 1):
                    body(2 * i + u, u, i, 0, 0)
            for u in (0, 1):
                body(CHUNKS - 2 + u, u, CHUNKS // 2 - 1, 0, 1)
            with eng.Fori(CHUNKS // 2, TILES // 2 - 1) as i:
                for u in (0, 1):
                    body(2 * i + u, u, i, 1, 1)
            for u in (0, 1):
                body(LAST - 1 + u, u, TILES // 2 - 1, 1, None)

        with nc.Block() as block:
            @block.sync
            def _(sp):
                load(sp, 0, 0)
                load(sp, 1, 1)
                sp.dma_start(ob[:], broadcast(io["c_bo"].rearrange("(o n) -> o n", o=1), [P, D])).then_inc(s["ob_in"], 16)

                def step(t, u, half, b, ahead):
                    if ahead is not None:
                        load(sp, t + 2, u)
                tiles(sp, step)

            @block.tensor
            def _(pe):
                score(pe, 0, 0, 0, 0)
                score(pe, 1, 1, 0, 0)
                turn(pe, 0, 0)

                def step(t, u, half, b, ahead):
                    if ahead is not None:
                        score(pe, t + 2, u, half + 1, ahead)
                    if not (isinstance(t, int) and t == LAST):
                        turn(pe, t + 1, 1 - u)
                    project_out(pe, t, u, b)
                tiles(pe, step)

            def exponents(act, t, u):
                act.wait_ge(s["shifted"], t + 1)
                nc.scalar.activation(pr[u][:], pr[u][:], ACT.Exp).then_inc(s["exp_done"], 1)

            def take_turned(act, t, u):
                act.wait_ge(s["pr_turned"], t + 1)
                wait_later(act, s["o_done"], t - 1)
                nc.scalar.activation(prT[u][:].rearrange("p m t -> p (m t)"), bank[2 + u][:, 0:SROWS], ACT.Copy).then_inc(s["prT_done"], 1)

            @block.scalar
            def _(act):
                exponents(act, 0, 0)
                exponents(act, 1, 1)
                take_turned(act, 0, 0)

                def step(t, u, half, b, ahead):
                    if not (isinstance(t, int) and t < 2):
                        store(act, t - 2, u)
                    if ahead is not None:
                        exponents(act, t + 2, u)
                    if not (isinstance(t, int) and t == LAST):
                        take_turned(act, t + 1, 1 - u)
                tiles(act, step)
                store(act, LAST - 1, 0)
                store(act, LAST, 1)
                for u in range(2):
                    act.wait_ge(stored[u], 16 * TILES // 2)

            @block.vector
            def _(dve):
                for t in (0, 1):
                    take_scores(dve, t, t, 0)
                    denominators(dve, t, t)

                def step(t, u, half, b, ahead):
                    if ahead is not None:
                        take_scores(dve, t + 2, u, ahead)
                    residual(dve, t, u, half)
                    if ahead is not None:
                        denominators(dve, t + 2, u)
                tiles(dve, step)

            def softmax_shift(pool, t, u):
                pool.wait_ge(s["top_done"], t + 1)
                wait_later(pool, s["pr_turned"], t - 1)
                nc.gpsimd.tensor_tensor(pr[u][:], sc[u][:], broadcast(top[u][:].unsqueeze(2), [P, HEADS, SLOTS]), ALU.subtract).then_inc(s["shifted"], 1)

            def softmax_norm(pool, t, u):
                pool.wait_ge(s["rden_done"], t + 1)
                nc.gpsimd.tensor_tensor(pr[u][:], pr[u][:], broadcast(rden[u][:].unsqueeze(2), [P, HEADS, SLOTS]), ALU.mult).then_inc(s["normed"], 1)

            def add_bias(pool, t, u, half):
                pool.wait_ge(x2_in[u], 16 * (half + 1))
                wait_later(pool, s["res_done"], t - 1)
                nc.gpsimd.tensor_tensor(x2b[u][:], x2[u][:], ob[:], ALU.add).then_inc(s["x2b_done"], 1)

            @block.gpsimd
            def _(pool):
                pool.wait_ge(s["ob_in"], 16)
                for t in (0, 1):
                    softmax_shift(pool, t, t)
                    softmax_norm(pool, t, t)

                def step(t, u, half, b, ahead):
                    add_bias(pool, t, u, half)
                    if ahead is not None:
                        softmax_shift(pool, t + 2, u)
                        softmax_norm(pool, t + 2, u)
                tiles(pool, step)


def decoder_layer(nc, io):
    with Stage(nc, "all") as keep:
        ring = keep.sb("ring", [P, UNITS, UNIT])
        ring_in = [nc.alloc_semaphore(f"ring_in{i}") for i in range(UNITS)]
        hold = dict(
            arena=ring[:].rearrange("p u n -> p (u n)"),
            ident=keep.sb("ident", [P, P]),
            tri=keep.sb("tri", [P, P]),
            decay=keep.sb("decay", [P, CHUNKS, HEADS]),
            rate=keep.sb("rate", [P, BATCH, CHUNKS, HEADS]),
            kbias=keep.sb("kbias", [P, SM]),
            top=keep.sb("top", [P, BATCH, SM]),
            sum=keep.sb("sum", [P, BATCH, SM]),
            z=keep.sb("z", [P, BATCH, SM, D]),
        )
        with Stage(nc, "att") as att:
            hold["mask"] = att.sb("mask", [P, TILES * CTX])
            hold["kbd"] = att.sb("kbd", [P, BATCH, GROUPS, HG, CTX])
            hold["vbd"] = att.sb("vbd", [PIECE, BATCH, 3, GROUPS, P])
            hold["m1"] = att.sb("m1", [P, KC, SROWS])
            tables_stage(nc, io, hold)
            mixer_stage(nc, io, hold)
            cross_stage(nc, io, hold, ring, ring_in)
        with Stage(nc, "slt") as slt:
            hold["m2"] = slt.sb("m2", [P, BATCH, KC, GROUPS, HG * SLOTS])
            hold["kb2"] = slt.sb("kb2", [P, BATCH, GROUPS, HG * SLOTS])
            hold["vo"] = slt.sb("vo", [P, BATCH, SM, D])
            experts_stage(nc, io, hold, ring, ring_in)
            combine_stage(nc, io, hold)


INPUTS = {"conv_w": "L0_attn_conv_w", "conv_b": "L0_attn_conv_b", "A_param": "L0_attn_A_param", "dt_bias": "L0_attn_dt_bias",
          "q_w": "L0_xattn_q_w", "q_b": "L0_xattn_q_b", "k_w": "L0_xattn_k_w", "k_b": "L0_xattn_k_b", "v_w": "L0_xattn_v_w",
          "v_b": "L0_xattn_v_b", "o_w": "L0_xattn_o_w", "o_b": "L0_xattn_o_b"}
for _n in ("d_Wq", "d_Wv", "d_Wo", "d_bq", "d_bk", "d_bv", "d_bo", "c_Wk", "c_Wv", "c_Wo", "c_bq", "c_bk", "c_bv", "c_bo",
           "e_ln_g", "e_ln_b", "e_W1", "e_b1", "e_Wg", "e_bg", "e_W2", "e_b2"):
    INPUTS[_n] = "L0_ffn_" + _n


def kernel(**inputs):
    import concourse.bacc as bacc
    import numpy as np
    from concourse.bass_utils import run_bass_kernel_spmd

    x = np.asarray(inputs["x"]).reshape(TOKENS, D)
    arrays = {name: np.ascontiguousarray(inputs[of]) for name, of in INPUTS.items()}
    arrays["x"] = np.ascontiguousarray(x)
    arrays["xT"] = np.ascontiguousarray(x.T)
    arrays["ctxT"] = np.ascontiguousarray(np.asarray(inputs["ctx_1024"]).reshape(BATCH * CTX, D).T)
    arrays["WinT"] = np.ascontiguousarray(np.asarray(inputs["L0_attn_W_in"]).T)
    arrays["WoutT"] = np.ascontiguousarray(np.asarray(inputs["L0_attn_W_out"]).T)
    slot = np.asarray(inputs["L0_ffn_slot_query"]).reshape(SLOTS, D)
    arrays["slot"] = np.ascontiguousarray(slot)
    arrays["slotT"] = np.ascontiguousarray(slot.T)
    arrays["d_WkT"] = np.ascontiguousarray(np.asarray(inputs["L0_ffn_d_Wk"]).T)
    arrays["c_WqT"] = np.ascontiguousarray(np.asarray(inputs["L0_ffn_c_Wq"]).T)

    arrays["conv_w"] = np.ascontiguousarray(arrays["conv_w"].reshape(CT, P, TAPS).transpose(1, 0, 2))
    for name in ("conv_b", "q_b", "k_b", "d_bq", "d_bk", "d_bv", "c_bq", "c_bk", "c_bv"):
        arrays[name] = np.ascontiguousarray(arrays[name].reshape(-1, P).T)

    nc = bacc.Bacc("TRN2", target_bir_lowering=False, num_devices=1)
    io = {name: nc.dram_tensor(f"in_{name}", a.shape, F32, kind="ExternalInput").ap() for name, a in arrays.items()}
    io["out"] = nc.dram_tensor("out", [TOKENS, D], F32, kind="ExternalOutput").ap()
    io["x1"] = nc.dram_tensor("scratch_x1", [TOKENS, D], F32).ap()
    io["x2"] = nc.dram_tensor("scratch_x2", [TOKENS, D], F32).ap()
    io["x2T"] = nc.dram_tensor("scratch_x2T", [TOKENS, D], F32).ap()
    decoder_layer(nc, io)
    got = run_bass_kernel_spmd(nc, [{f"in_{name}": a for name, a in arrays.items()}], core_ids=[0])
    return got.results[0]["out"].reshape(BATCH, SEQ, D)
```

```python
from contextlib import ExitStack

import concourse.bass as bass
import concourse.mybir as mybir

F32 = mybir.dt.float32
ALU = mybir.AluOpType
ACT = mybir.ActivationFunctionType
AX = mybir.AxisListType

P = 128
BATCH, SEQ, D = 2, 2048, 512
TOKENS = BATCH * SEQ
TILES = TOKENS // P
CHUNKS = SEQ // P
KC = D // P
HEADS = 16
HD = D // HEADS
HG = P // HD
GROUPS = HEADS // HG
TAPS = 4
HALO = TAPS - 1
CONV = 3 * D
CT = CONV // P
CTX = 77
SLOTS = 16
SROWS = HEADS * SLOTS
SM = SROWS // P
EXPERTS = 16
F = 2048
EPS = 1e-5
SCALE = float(HD) ** -0.5
NEG = -3.0e38
KROWS = HG * CTX
PIECE = -(-KROWS // 3)
PIECES = [min(PIECE, KROWS - i * PIECE) for i in range(3)]
UNIT = 4096
UNITS = 6
FQ = F // 4


def broadcast(ap, shape):
    return ap.broadcast_to(shape)


class Stage:

    def __init__(self, nc, tag, arena=None):
        self.nc, self.tag, self.stack, self.arena, self.used, self.taken = nc, tag, ExitStack(), arena, 0, []

    def __enter__(self):
        return self

    def __exit__(self, *a):
        if self.taken and a[0] is None:
            self.nc.clear_and_free_semaphores(self.taken)
            self.nc.all_engine_barrier()
        return self.stack.__exit__(*a)

    def sb(self, name, shape):
        size = 1
        for n in shape[1:]:
            size *= n
        if self.arena is not None and self.used + size <= UNITS * UNIT:
            flat = self.arena[0:shape[0], self.used:self.used + size]
            self.used += size
            return shaped(flat, shape)
        return self.stack.enter_context(self.nc.sbuf_tensor(f"{self.tag}_{name}", shape, F32))

    def banks(self, n=8):
        return [self.stack.enter_context(self.nc.psum_tensor(f"{self.tag}_bank{i}", [P, 512], F32)) for i in range(n)]

    def sem(self, name):
        self.taken.append(self.nc.alloc_semaphore(f"{self.tag}_{name}"))
        return self.taken[-1]

    def sems(self, *names):
        return {n: self.sem(n) for n in names}

    def pair(self, name):
        return [self.sem(f"{name}{i}") for i in range(2)]


def shaped(flat, shape):
    names = "abcd"[:len(shape) - 1]
    dims = dict(zip(names, shape[1:]))
    return flat.rearrange(f"p ({' '.join(names)}) -> p {' '.join(names)}", **dims)


def wait_later(eng, sem, value):
    if not isinstance(value, int) or value > 0:
        eng.wait_ge(sem, value)


def tables_stage(nc, io, hold):
    with Stage(nc, "tab", hold["arena"]) as st:
        wdt = st.sb("wdt", [P, KC, HD])
        xblk = [st.sb(f"xblk{i}", [P, KC, 512]) for i in range(3)]
        bias = st.sb("bias", [P, 1])
        apar = st.sb("apar", [P, 1])
        zabs = st.sb("zabs", [P, BATCH, 512])
        zexp = st.sb("zexp", [P, BATCH, 512])
        zln = st.sb("zln", [P, BATCH, 512])
        zrelu = st.sb("zrelu", [P, BATCH, 512])
        arow = st.sb("arow", [P, BATCH, 512])
        atok = st.sb("atok", [P, BATCH, CHUNKS, HEADS])
        carry = st.sb("carry", [P, BATCH, CHUNKS, HEADS])
        carry2 = st.sb("carry2", [P, BATCH, CHUNKS, HEADS])
        cum = st.sb("cum", [P, BATCH, CHUNKS, HEADS])
        neg = st.sb("neg", [P, BATCH, CHUNKS, HEADS])
        pos = st.sb("pos", [P, BATCH, CHUNKS, HEADS])
        cume = st.sb("cume", [P, BATCH, CHUNKS, HEADS])
        norm = st.sb("norm", [P, BATCH, CHUNKS, HEADS])
        rnorm = st.sb("rnorm", [P, BATCH, CHUNKS, HEADS])
        tri = st.sb("tri", [P, P])
        ones = st.sb("ones", [P, P])
        wk = st.sb("wk", [P, KC, D])
        wv = st.sb("wv", [P, KC, D])
        wq = st.sb("wq", [P, KC, D])
        wkT = st.sb("wkT", [P, KC, D])
        ctxT = st.sb("ctxT", [P, KC, BATCH * CTX])
        kb = st.sb("kb", [P, GROUPS])
        qb = st.sb("qb", [P, GROUPS])
        bk = st.sb("bk", [P, GROUPS])
        vb = st.sb("vb", [CTX, D])
        vtok = st.sb("vtok", [CTX, BATCH, D])
        slotT = st.sb("slotT", [P, KC, SLOTS])
        sqbd = st.sb("sqbd", [P, GROUPS, HG, SLOTS])
        bank = st.banks()
        s = st.sems("consts", "zeros", "small", "wdt_in", "ctx_in", "kw_in", "vw_in", "qw_in", "kT_in", "blk_used",
                    "dt_ready", "softplus", "dt_steps", "a_ready", "a_turned", "atok_ready", "cum_ready", "exp_ready",
                    "sums1", "sums2", "carry_steps", "norm_steps", "tables_ready", "k_ready", "v_ready", "vtok_ready",
                    "vbd_in", "q_ready", "sq_ready", "m1_ready", "kbias_ready", "kbd_done", "m1_done")
        blk_in = [st.sem(f"blk_in{i}") for i in range(3)]
        QB = SEQ // 512

        def small_loads(sp):
            for q in range(QB):
                sp.dma_start(bias[HD * q:HD * q + HEADS, :], io["dt_bias"].rearrange("(h o) -> h o", o=1)).then_inc(s["small"], 16)
                sp.dma_start(apar[HD * q:HD * q + HEADS, :], io["A_param"].rearrange("(h o) -> h o", o=1)).then_inc(s["small"], 16)
        SMALL_AP = 2 * QB * 16

        with nc.Block() as block:
            @block.sync
            def _(sp):
                sp.wait_ge(s["zeros"], 3)
                sp.dma_start(wdt[:, :, 0:HEADS], io["WinT"][:, CONV:].rearrange("(k p) n -> p k n", p=P)).then_inc(s["wdt_in"], 16)
                small_loads(sp)
                for i in range(BATCH * QB):
                    if i >= 3:
                        sp.wait_ge(s["blk_used"], i - 2)
                    sp.dma_start(xblk[i % 3][:], io["xT"][:, i * 512:(i + 1) * 512].rearrange("(k p) n -> p k n", p=P)).then_inc(blk_in[i % 3], 16)
                    if i == 2:
                        sp.dma_start(ctxT[:], io["ctxT"].rearrange("(k p) n -> p k n", p=P)).then_inc(s["ctx_in"], 16)
                        sp.dma_start(slotT[:], io["slotT"].rearrange("(k p) n -> p k n", p=P)).then_inc(s["ctx_in"], 16)
                        sp.dma_start(vb[:], broadcast(io["v_b"].rearrange("(o n) -> o n", o=1), [CTX, D])).then_inc(s["ctx_in"], 16)
                        for dst, src in ((kb, io["k_b"]), (qb, io["d_bq"]), (bk, io["d_bk"])):
                            sp.dma_start(dst[:], src).then_inc(s["ctx_in"], 16)
                CTX_IN = 6 * 16
                for dst, src, sem in ((wk, io["k_w"], s["kw_in"]), (wv, io["v_w"], s["vw_in"]), (wq, io["d_Wq"], s["qw_in"]), (wkT, io["d_WkT"], s["kT_in"])):
                    sp.dma_start(dst[:], src.rearrange("(k p) n -> p k n", p=P)).then_inc(sem, 16)
                mixer_weights(sp, io, hold, hold["mixer_in"])
                sp.wait_ge(s["vtok_ready"], BATCH)
                n = 0
                for b in range(BATCH):
                    for h in range(HG):
                        r = h * CTX
                        while r < (h + 1) * CTX:
                            piece = r // PIECE
                            end = min((h + 1) * CTX, (piece + 1) * PIECE)
                            src = vtok[r - h * CTX:end - h * CTX, b, :].rearrange("s (g h p) -> s g h p", g=GROUPS, h=HG)[:, :, h, :]
                            sp.dma_start(hold["vbd"][r - piece * PIECE:end - piece * PIECE, b, piece, :, h * HD:(h + 1) * HD], src).then_inc(s["vbd_in"], 16)
                            n += 1
                            r = end
                sp.wait_ge(s["vbd_in"], 16 * n)

            @block.gpsimd
            def _(pool):
                nc.gpsimd.memset(wdt[:], 0.0).then_inc(s["zeros"], 1)
                nc.gpsimd.memset(bias[:], 0.0).then_inc(s["zeros"], 1)
                nc.gpsimd.memset(apar[:], 0.0).then_inc(s["zeros"], 1)
                nc.gpsimd.memset(hold["ident"][:], 0.0).then_inc(s["zeros"], 1)
                nc.gpsimd.memset(tri[:], 1.0).then_inc(s["zeros"], 1)
                nc.gpsimd.memset(ones[:], 1.0).then_inc(s["zeros"], 1)
                nc.gpsimd.memset(hold["mask"][:], 0.0).then_inc(s["zeros"], 1)
                pool.wait_ge(s["zeros"], 7)
                nc.gpsimd.affine_select(out=hold["ident"][:], in_=hold["ident"][:], compare_op=ALU.not_equal, fill=1.0, base=0,
                                        pattern=[[-1, P]], channel_multiplier=1).then_inc(s["consts"], 1)
                nc.gpsimd.affine_select(out=tri[:], in_=tri[:], compare_op=ALU.is_ge, fill=0.0, base=0,
                                        pattern=[[1, P]], channel_multiplier=-1).then_inc(s["consts"], 1)
                nc.gpsimd.affine_select(out=hold["mask"][:], in_=hold["mask"][:], compare_op=ALU.is_ge, fill=NEG, base=0,
                                        pattern=[[-1, CTX]], channel_multiplier=1).then_inc(s["consts"], 1)
                nc.gpsimd.memset(hold["vbd"][:], 0.0).then_inc(s["zeros"], 1)
                nc.gpsimd.memset(hold["kbd"][:], 0.0).then_inc(s["zeros"], 1)
                nc.gpsimd.memset(sqbd[:], 0.0).then_inc(s["zeros"], 1)
                pool.wait_ge(s["consts"], 2)
                nc.gpsimd.tensor_copy(hold["tri"][:], tri[:]).then_inc(s["consts"], 1)

            @block.tensor
            def _(pe):
                pe.wait_ge(s["wdt_in"], 16)
                for b in range(BATCH):
                    for q in range(QB):
                        i = b * QB + q
                        pe.wait_ge(blk_in[i % 3], 16 * (i // 3 + 1))
                        for k in range(KC):
                            last = nc.tensor.matmul(bank[b][HD * q:HD * (q + 1), :], wdt[:, k, :], xblk[i % 3][:, k, :],
                                                    start=(k == 0), stop=(k == KC - 1))
                        last.then_inc(s["blk_used"], 1)
                pe.wait_ge(s["ctx_in"], 6 * 16)
                pe.wait_ge(s["kw_in"], 16)
                for g in range(GROUPS):
                    for k in range(KC):
                        last = nc.tensor.matmul(bank[2 + g // 2][:, (g % 2) * 256:(g % 2) * 256 + BATCH * CTX], wk[:, k, g * P:(g + 1) * P],
                                                ctxT[:, k, :], start=(k == 0), stop=(k == KC - 1))
                last.then_inc(s["k_ready"], 1)
                pe.wait_ge(s["vw_in"], 16)
                for b in range(BATCH):
                    for k in range(KC):
                        last = nc.tensor.matmul(bank[4 + b][0:CTX, :], ctxT[:, k, b * CTX:(b + 1) * CTX], wv[:, k, :],
                                                start=(k == 0), stop=(k == KC - 1))
                    last.then_inc(s["v_ready"], 1)
                pe.wait_ge(s["consts"], 2)
                for b in range(BATCH):
                    pe.wait_ge(s["a_ready"], b + 1)
                    for sub in range(4):
                        last = nc.tensor.transpose(bank[6 + b][:, sub * P:(sub + 1) * P], arow[:, b, sub * P:(sub + 1) * P], hold["ident"][:])
                    last.then_inc(s["a_turned"], 1)
                pe.wait_ge(s["atok_ready"], BATCH)
                nc.tensor.matmul(bank[0][:], tri[:], atok[:], start=True, stop=True)
                nc.tensor.matmul(bank[1][:], ones[:], atok[:], start=True, stop=True).then_inc(s["sums1"], 1)
                pe.wait_ge(s["qw_in"], 16)
                pe.wait_ge(s["atok_ready"], BATCH)
                for g in range(GROUPS):
                    for k in range(KC):
                        last = nc.tensor.matmul(bank[6][:, g * SLOTS:(g + 1) * SLOTS], wq[:, k, g * P:(g + 1) * P], slotT[:, k, :],
                                                start=(k == 0), stop=(k == KC - 1))
                last.then_inc(s["q_ready"], 1)
                pe.wait_ge(s["exp_ready"], 1)
                pe.wait_ge(s["cum_ready"], 1)
                nc.tensor.matmul(bank[0][:], tri[:], neg[:], start=True, stop=True)
                nc.tensor.matmul(bank[1][:], ones[:], neg[:], start=True, stop=True).then_inc(s["sums2"], 1)
                pe.wait_ge(s["kT_in"], 16)
                pe.wait_ge(s["sq_ready"], GROUPS)
                pe.wait_ge(s["kbd_done"], 1)
                pe.wait_ge(s["vtok_ready"], BATCH)
                for k in range(KC):
                    for g in range(GROUPS):
                        last = nc.tensor.matmul(bank[2 + k][:, g * HG * SLOTS:(g + 1) * HG * SLOTS], wkT[:, g, k * P:(k + 1) * P],
                                                sqbd[:, g, :, :], start=True, stop=True)
                last.then_inc(s["m1_ready"], 1)
                for g in range(GROUPS):
                    half = (g % 2) * HG * SLOTS
                    last = nc.tensor.matmul(bank[7][half:half + HG * SLOTS, g // 2:g // 2 + 1], sqbd[:, g, :, :], bk[:, g:g + 1],
                                            start=True, stop=True)
                last.then_inc(s["kbias_ready"], 1)

            @block.scalar
            def _(act):
                act.wait_ge(s["small"], SMALL_AP)
                for b in range(BATCH):
                    act.wait_ge(s["blk_used"], QB * (b + 1))
                    nc.scalar.activation(zabs[:, b, :], bank[b][:], ACT.Abs, bias=bias[:]).then_inc(s["softplus"], 1)
                    nc.scalar.activation(zrelu[:, b, :], bank[b][:], ACT.Relu, bias=bias[:]).then_inc(s["softplus"], 1)
                    act.wait_ge(s["softplus"], 4 * b + 2)
                    nc.scalar.activation(zexp[:, b, :], zabs[:, b, :], ACT.Exp, scale=-1.0).then_inc(s["softplus"], 1)
                    act.wait_ge(s["softplus"], 4 * b + 3)
                    nc.scalar.activation(zln[:, b, :], zexp[:, b, :], ACT.Ln, bias=1.0).then_inc(s["softplus"], 1)
                act.wait_ge(s["cum_ready"], 1)
                nc.scalar.activation(neg[:], cum[:], ACT.Exp, scale=-1.0).then_inc(s["exp_ready"], 1)
                nc.scalar.activation(pos[:], cum[:], ACT.Exp).then_inc(s["exp_ready"], 1)
                act.wait_ge(s["exp_ready"], 1)
                nc.scalar.activation(hold["decay"][:], neg[:, 0, :, :], ACT.Copy).then_inc(s["tables_ready"], 1)

            def running_sums(dve, sums, carry, out, first, before):
                step = first
                for c in range(1, CHUNKS):
                    dve.wait_ge(s["carry_steps"], step)
                    nc.vector.tensor_tensor(carry[:, :, c, :], carry[:, :, c - 1, :],
                                            before.rearrange("p (b c h) -> p b c h", b=BATCH, c=CHUNKS)[:, :, c - 1, :],
                                            ALU.add).then_inc(s["carry_steps"], 1)
                    step += 1
                dve.wait_ge(s["carry_steps"], step)
                return nc.vector.tensor_tensor(out[:], sums.rearrange("p (b c h) -> p b c h", b=BATCH, c=CHUNKS), carry[:], ALU.add)

            @block.vector
            def _(dve):
                nc.vector.memset(carry[:, :, 0, :], 0.0)
                nc.vector.memset(carry2[:, :, 0, :], 0.0).then_inc(s["carry_steps"], 1)
                dve.wait_ge(s["small"], SMALL_AP)
                for b in range(BATCH):
                    dve.wait_ge(s["softplus"], 4 * (b + 1))
                    nc.vector.tensor_tensor(arow[:, b, :], zrelu[:, b, :], zln[:, b, :], ALU.add).then_inc(s["dt_steps"], 1)
                    dve.wait_ge(s["dt_steps"], b + 1)
                    nc.vector.tensor_scalar(arow[:, b, :], arow[:, b, :], apar[:], None, ALU.mult).then_inc(s["a_ready"], 1)
                for b in range(BATCH):
                    dve.wait_ge(s["a_turned"], b + 1)
                    nc.vector.tensor_copy(atok[:, b, :, :].rearrange("p (q i) h -> p i q h", q=QB),
                                          bank[6 + b][:].rearrange("p (i q h) -> p i q h", i=4, q=QB)[:, :, :, 0:HEADS]).then_inc(s["atok_ready"], 1)
                dve.wait_ge(s["k_ready"], 1)
                dve.wait_ge(s["zeros"], 10)
                for g in range(GROUPS):
                    for h in range(HG):
                        r = slice(h * HD, (h + 1) * HD)
                        last = nc.vector.tensor_scalar(hold["kbd"][r, :, g, h, :],
                                                       bank[2 + g // 2][r, (g % 2) * 256:(g % 2) * 256 + BATCH * CTX].rearrange("p (b s) -> p b s", b=BATCH),
                                                       kb[r, g:g + 1], None, ALU.add)
                last.then_inc(s["kbd_done"], 1)
                for b in range(BATCH):
                    dve.wait_ge(s["v_ready"], b + 1)
                    nc.vector.tensor_tensor(vtok[:, b, :], bank[4 + b][0:CTX, :], vb[:], ALU.add).then_inc(s["vtok_ready"], 1)
                dve.wait_ge(s["sums1"], 1)
                running_sums(dve, bank[0][:], carry, cum, 1, bank[1][:]).then_inc(s["cum_ready"], 1)
                dve.wait_ge(s["q_ready"], 1)
                for g in range(GROUPS):
                    for h in range(HG):
                        r = slice(h * HD, (h + 1) * HD)
                        last = nc.vector.tensor_scalar(sqbd[r, g, h, :], bank[6][r, g * SLOTS:(g + 1) * SLOTS], qb[r, g:g + 1], None, ALU.add)
                    last.then_inc(s["sq_ready"], 1)
                dve.wait_ge(s["sums2"], 1)
                running_sums(dve, bank[0][:], carry2, cume, CHUNKS, bank[1][:]).then_inc(s["norm_steps"], 1)
                dve.wait_ge(s["exp_ready"], 2)
                dve.wait_ge(s["norm_steps"], 1)
                nc.vector.tensor_tensor(norm[:], pos[:], cume[:], ALU.mult).then_inc(s["norm_steps"], 1)
                dve.wait_ge(s["norm_steps"], 2)
                nc.vector.reciprocal(rnorm[:], norm[:]).then_inc(s["norm_steps"], 1)
                dve.wait_ge(s["norm_steps"], 3)
                for b in range(BATCH):
                    nc.vector.tensor_tensor(hold["rate"][:, b, :, :], pos[:, 0, :, :], rnorm[:, b, :, :], ALU.mult).then_inc(s["tables_ready"], 1)
                dve.wait_ge(s["m1_ready"], 1)
                for k in range(KC):
                    nc.vector.tensor_copy(hold["m1"][:, k, :], bank[2 + k][:, 0:SROWS]).then_inc(s["m1_done"], 1)
                dve.wait_ge(s["kbias_ready"], 1)
                nc.vector.tensor_scalar(hold["kbias"][:], bank[7][:, 0:SM], SCALE, None, ALU.mult).then_inc(s["m1_done"], 1)


LN_STEPS = 14
MAGIC = 0x5F3759DF


def norm_factors(nc, dve, sem, first, x, stats):
    n = len(x)
    var, y, t = stats[:, 0:n, 8:9], stats[:, 0:n, 9:10], stats[:, 0:n, 10:11]
    INT = mybir.dt.int32
    for i in range(n):
        last = nc.vector.bn_stats(stats[:, i, 0:6], x[i])
    last.then_inc(sem, 1)
    dve.wait_ge(sem, first + 1)
    nc.vector.memset(var, EPS)
    for i in range(n):
        last = nc.vector.bn_aggr(stats[:, i, 6:8], stats[:, i, 0:6])
    last.then_inc(sem, 1)
    dve.wait_ge(sem, first + 2)
    nc.vector.tensor_tensor(var, var, stats[:, 0:n, 7:8], ALU.add).then_inc(sem, 1)
    dve.wait_ge(sem, first + 3)
    nc.vector.tensor_scalar(y.bitcast(INT), var.bitcast(INT), 1, None, ALU.logical_shift_right).then_inc(sem, 1)
    dve.wait_ge(sem, first + 4)
    nc.vector.tensor_scalar(y.bitcast(INT), y.bitcast(INT), -1.0, float(MAGIC), ALU.mult, ALU.add).then_inc(sem, 1)
    for i in range(3):
        dve.wait_ge(sem, first + 5 + 3 * i)
        nc.vector.tensor_tensor(t, y, y, ALU.mult).then_inc(sem, 1)
        dve.wait_ge(sem, first + 6 + 3 * i)
        nc.vector.scalar_tensor_tensor(t, t, -0.5, var, ALU.mult, ALU.mult).then_inc(sem, 1)
        dve.wait_ge(sem, first + 7 + 3 * i)
        last = nc.vector.scalar_tensor_tensor(y, t, 1.5, y, ALU.add, ALU.mult)
        last.then_inc(sem, 1)
    dve.wait_ge(sem, first + LN_STEPS)


def layernorm(nc, dve, sem, first, x, stats, out):
    norm_factors(nc, dve, sem, first, x, stats)
    for i in range(len(x)):
        last = nc.vector.tensor_scalar(out[i], x[i], stats[:, i, 6:7], stats[:, i, 9:10], ALU.subtract, ALU.mult)
    return last


def mixer_weights(sp, io, hold, sem):
    for dst, src in ((hold["win"], io["WinT"][:, 0:CONV].rearrange("(k p) n -> p k n", p=P)), (hold["wout"], io["WoutT"].rearrange("(k p) n -> p k n", p=P)),
                     (hold["taps"], io["conv_w"]), (hold["convb"], io["conv_b"])):
        sp.dma_start(dst[:], src).then_inc(sem, 16)


MIXER_WEIGHTS = 4 * 16


def mixer_stage(nc, io, hold):
    with Stage(nc, "mix", hold["arena"]) as st:
        win, wout, taps, convb = hold["win"], hold["wout"], hold["taps"], hold["convb"]
        xT = [st.sb(f"xT{i}", [P, KC, P]) for i in range(2)]
        x_in = [st.sb(f"x_in{i}", [P, BATCH, D]) for i in range(2)]
        proj = [st.sb(f"proj{i}", [P, CT, HALO + P]) for i in range(2)]
        conv = [st.sb(f"conv{i}", [P, CT, P]) for i in range(2)]
        product = [st.sb(f"product{i}", [P, 4, P]) for i in range(2)]
        cbd = st.sb("cbd", [P, GROUPS, HG, P])
        btok = st.sb("btok", [P, D])
        xs = st.sb("xs", [P, D])
        scores = st.sb("scores", [P, HEADS, P])
        state = st.sb("state", [P, GROUPS, P])
        rate = st.sb("rate", [P, BATCH, HEADS, HD])
        rateT = st.sb("rateT", [P, BATCH, D])
        yT = st.sb("yT", [P, BATCH, D])
        xr = st.sb("xr", [P, BATCH, D])
        stats = st.sb("stats", [P, BATCH, 12])
        x1 = [st.sb(f"x1_{i}", [P, BATCH, D]) for i in range(2)]
        bank = st.banks()
        PROJ, XTURN, BTURN, Y, OUT = bank[0:3], bank[3], bank[4], bank[5], bank[6:8]
        SCORE = PROJ + [XTURN]
        STATE, RATE = BTURN, (XTURN, BTURN)
        s = st.sems("zeros", "proj_done", "proj_out", "halo_done", "convC", "convB", "convX", "conv_tap", "conv_tapX",
                    "cbd_done", "b_turned", "btok_done", "x_turned", "xs_done", "scores_done", "scores_masked", "state_done",
                    "state_added", "y_done", "rate_done", "rate_turned", "rateT_done", "yT_done", "out_done", "res_done",
                    "ln_step", "x1_done")
        xT_in, x_arrived, x1_stored = st.pair("xT_in"), st.pair("x_arrived"), st.pair("x1_stored")
        x_v = io["x"].rearrange("(b n) d -> n b d", b=BATCH)
        x1_v = io["x1"].rearrange("(b n) d -> n b d", b=BATCH)
        LAST = CHUNKS - 1

        def load_turned(sp, c, u):
            wait_later(sp, s["proj_done"], 3 * (c - 1))
            sp.dma_start(xT[u][:], io["xT"].rearrange("(k p) n -> p k n", p=P)[:, :, bass.ds(c * P, P)]).then_inc(xT_in[u], 16)

        def load_residual(sp, c, u):
            wait_later(sp, s["res_done"], 2 * (c - 1))
            sp.dma_start(x_in[u][:], x_v[bass.ds(c * P, P), :, :]).then_inc(x_arrived[u], 16)

        def store(sp, c, u):
            sp.wait_ge(s["x1_done"], c + 1)
            sp.dma_start(x1_v[bass.ds(c * P, P), :, :], x1[u][:]).then_inc(x1_stored[u], 16)

        def project(pe, c, u, half, grp):
            if grp == 0:
                pe.wait_ge(xT_in[u], 16 * (half + 1))
            wait_later(pe, s["proj_out"], 3 * (c - 1) + grp + 1)
            wait_later(pe, s["scores_masked"], 4 * (c - 2) + grp + 1)
            for m in range(4):
                for k in range(KC):
                    last = nc.tensor.matmul(PROJ[grp][:, m * P:(m + 1) * P], win[:, k, (grp * 4 + m) * P:(grp * 4 + m + 1) * P],
                                            xT[u][:, k, :], start=(k == 0), stop=(k == KC - 1))
            last.then_inc(s["proj_done"], 1)

        def turn(pe, c, u):
            pe.wait_ge(s["convB"], c + 1)
            wait_later(pe, s["rateT_done"], 2 * c)
            for g in range(GROUPS):
                last = nc.tensor.transpose(BTURN[:, g * P:(g + 1) * P], conv[u][:, 4 + g, :], hold["ident"][:])
            last.then_inc(s["b_turned"], 1)
            pe.wait_ge(s["convX"], c + 1)
            for g in range(GROUPS):
                last = nc.tensor.transpose(XTURN[:, g * P:(g + 1) * P], conv[u][:, 8 + g, :], hold["ident"][:])
            last.then_inc(s["x_turned"], 1)

        def score(pe, c, u, g):
            if g == 0:
                pe.wait_ge(s["cbd_done"], c + 1)
            if g == 3:
                pe.wait_ge(s["xs_done"], c + 1)
            else:
                pe.wait_ge(s["proj_out"], min(3 * (c + 1) + g + 1, 3 * CHUNKS) if isinstance(c, int) else 3 * (c + 1) + g + 1)
            nc.tensor.matmul(SCORE[g][:], conv[u][:, 4 + g, :], cbd[:, g, :, :], start=True, stop=True).then_inc(s["scores_done"], 1)

        def add_to_state(pe, c):
            pe.wait_ge(s["btok_done"], c + 1)
            pe.wait_ge(s["xs_done"], c + 1)
            for g in range(GROUPS):
                last = nc.tensor.matmul(STATE[:, g * P:(g + 1) * P], btok[:, g * P:(g + 1) * P], xs[:, g * P:(g + 1) * P], start=True, stop=True)
            last.then_inc(s["state_done"], 1)

        def weigh_steps(pe, c, u):
            wait_later(pe, s["yT_done"], 2 * c)
            wait_later(pe, s["state_added"], c)
            for g in range(GROUPS):
                nc.tensor.matmul(Y[:, g * P:(g + 1) * P], state[:, g, :], conv[u][:, g, :], start=True, stop=False, skip_group_check=True)
                pe.wait_ge(s["scores_masked"], 4 * c + g + 1)
                for h in range(HG):
                    hh = g * HG + h
                    last = nc.tensor.matmul(Y[h * HD:(h + 1) * HD, g * P:(g + 1) * P], xs[:, hh * HD:(hh + 1) * HD], scores[:, hh, :],
                                            start=False, stop=True, skip_group_check=True)
            last.then_inc(s["y_done"], 1)

        def turn_rates(pe, c):
            pe.wait_ge(s["rate_done"], c + 1)
            for b in range(BATCH):
                if b == 0:
                    pe.wait_ge(s["scores_masked"], 4 * c + 4)
                else:
                    pe.wait_ge(s["state_added"], c + 1)
                for g in range(GROUPS):
                    last = nc.tensor.transpose(RATE[b][:, g * P:(g + 1) * P], rate[:, b, g * HG:(g + 1) * HG, :], hold["ident"][:])
                last.then_inc(s["rate_turned"], 1)

        def project_out(pe, c):
            for b in range(BATCH):
                pe.wait_ge(s["yT_done"], 2 * c + b + 1)
                wait_later(pe, s["res_done"], 2 * c - 1 + b)
                for g in range(GROUPS):
                    last = nc.tensor.matmul(OUT[b][:], yT[:, b, g * P:(g + 1) * P], wout[:, g, :], start=(g == 0), stop=(g == GROUPS - 1))
                last.then_inc(s["out_done"], 1)

        def take_projection(act, c, u, grp):
            act.wait_ge(s["proj_done"], 3 * c + grp + 1)
            if grp == 0:
                wait_later(act, s["halo_done"], c - 1)
                wait_later(act, s["convB"], c - 1)
                wait_later(act, s["convX"], c - 1)
            nc.scalar.activation(proj[u][:, grp * 4:grp * 4 + 4, HALO:], PROJ[grp][:].rearrange("p (m t) -> p m t", m=4), ACT.Copy).then_inc(s["proj_out"], 1)

        def pass_halo(act, c, u):
            act.wait_ge(s["proj_out"], 3 * c + 3)
            wait_later(act, s["convB"], c)
            wait_later(act, s["convX"], c)
            nc.scalar.activation(proj[1 - u][:, :, 0:HALO], proj[u][:, :, P:P + HALO], ACT.Copy).then_inc(s["halo_done"], 1)

        def spread_c(act, c, u):
            act.wait_ge(s["convC"], c + 1)
            wait_later(act, s["scores_done"], 4 * c)
            for h in range(HG):
                r = slice(h * HD, (h + 1) * HD)
                last = nc.scalar.activation(cbd[r, :, h, :], conv[u][r, 0:GROUPS, :], ACT.Copy)
            last.then_inc(s["cbd_done"], 1)

        def spread_rates(act, c):
            wait_later(act, s["rate_turned"], 2 * c)
            for b in range(BATCH):
                last = nc.scalar.activation(rate[:, b, :, :], broadcast(hold["rate"][:, b, bass.ds(c, 1), :].rearrange("p o h -> p (o h)").unsqueeze(2), [P, HEADS, HD]), ACT.Copy)
            last.then_inc(s["rate_done"], 1)

        def take_b(act, c):
            act.wait_ge(s["b_turned"], c + 1)
            wait_later(act, s["state_done"], c)
            nc.scalar.activation(btok[:], BTURN[:], ACT.Copy).then_inc(s["btok_done"], 1)

        def take_rates(act, c):
            for b in range(BATCH):
                act.wait_ge(s["rate_turned"], 2 * c + b + 1)
                wait_later(act, s["yT_done"], 2 * c - 1 + b)
                nc.scalar.activation(rateT[:, b, :], RATE[b][:], ACT.Copy).then_inc(s["rateT_done"], 1)

        def convolve(dve, c, u):
            dve.wait_ge(s["proj_out"], 3 * c + 3)
            wait_later(dve, s["halo_done"], c)
            wait_later(dve, s["y_done"], c - 1)
            for m0, done, first in ((0, s["convC"], 0), (4, s["convB"], 3)):
                for k in range(TAPS):
                    if k:
                        dve.wait_ge(s["conv_tap"], 6 * c + first + k)
                    for m in range(m0, m0 + 4):
                        src = proj[u][:, m, k:k + P]
                        if k == 0:
                            last = nc.vector.tensor_scalar(conv[u][:, m, :], src, taps[:, m, 0:1], convb[:, m:m + 1], ALU.mult, ALU.add)
                        else:
                            last = nc.vector.scalar_tensor_tensor(conv[u][:, m, :], src, taps[:, m, k:k + 1], conv[u][:, m, :], ALU.mult, ALU.add)
                    last.then_inc(s["conv_tap"] if k < TAPS - 1 else done, 1)

        def weigh_x(dve, c):
            dve.wait_ge(s["x_turned"], c + 1)
            nc.vector.tensor_tensor(xs[:].rearrange("p (h d) -> p h d", h=HEADS), XTURN[:].rearrange("p (h d) -> p h d", h=HEADS),
                                    broadcast(hold["decay"][:, bass.ds(c, 1), :].rearrange("p o h -> p (o h)").unsqueeze(2), [P, HEADS, HD]),
                                    ALU.mult).then_inc(s["xs_done"], 1)

        def mask_scores(dve, c):
            for g in range(GROUPS):
                dve.wait_ge(s["scores_done"], 4 * c + g + 1)
                nc.vector.tensor_tensor(scores[:, g * HG:(g + 1) * HG, :], SCORE[g][:].rearrange("p (h l) -> p h l", h=HG),
                                        broadcast(hold["tri"][:].unsqueeze(1), [P, HG, P]), ALU.mult).then_inc(s["scores_masked"], 1)

        def advance_state(dve, c):
            dve.wait_ge(s["y_done"], c + 1)
            dve.wait_ge(s["state_done"], c + 1)
            for h in range(HG):
                r = slice(h * HD, (h + 1) * HD)
                last = nc.vector.tensor_tensor(state[r, :, r], STATE[r, :].rearrange("p (g q) -> p g q", g=GROUPS)[:, :, r], state[r, :, r], ALU.add)
            last.then_inc(s["state_added"], 1)

        def rate_outputs(dve, c):
            for b in range(BATCH):
                dve.wait_ge(s["rateT_done"], 2 * c + b + 1)
                wait_later(dve, s["out_done"], 2 * c - 1 + b)
                nc.vector.tensor_tensor(yT[:, b, :], Y[:], rateT[:, b, :], ALU.mult).then_inc(s["yT_done"], 1)

        def norm(dve, c, u, half):
            dve.wait_ge(x_arrived[u], 16 * (half + 1))
            wait_later(dve, s["x1_done"], c)
            for b in range(BATCH):
                dve.wait_ge(s["out_done"], 2 * c + b + 1)
                nc.vector.tensor_tensor(xr[:, b, :], OUT[b][:], x_in[u][:, b, :], ALU.add).then_inc(s["res_done"], 1)
            dve.wait_ge(s["res_done"], 2 * c + 2)
            wait_later(dve, x1_stored[u], 16 * half)
            layernorm(nc, dve, s["ln_step"], LN_STEPS * c, [xr[:, b, :] for b in range(BATCH)], stats,
                      [x1[u][:, b, :] for b in range(BATCH)]).then_inc(s["x1_done"], 1)

        def convolve_x(pool, c, u):
            pool.wait_ge(s["proj_out"], 3 * c + 3)
            wait_later(pool, s["halo_done"], c)
            wait_later(pool, s["x_turned"], c - 1)
            for k in range(TAPS):
                nc.gpsimd.tensor_tensor(product[k % 2][:], proj[u][:, 8:12, k:k + P], broadcast(taps[:, 8:12, k:k + 1], [P, 4, P]),
                                        ALU.mult).then_inc(s["conv_tapX"], 1)
                pool.wait_ge(s["conv_tapX"], 7 * c + 2 * k + 1)
                so_far = conv[u][:, 8:12, :] if k else broadcast(convb[:, 8:12].unsqueeze(2), [P, 4, P])
                last = nc.gpsimd.tensor_tensor(conv[u][:, 8:12, :], so_far, product[k % 2][:], ALU.add)
                if k < TAPS - 1:
                    last.then_inc(s["conv_tapX"], 1)
                else:
                    last.then_inc(s["convX"], 1)

        def chunks(eng, body):
            for c in range(4):
                body(c, c % 2, c // 2)
            with eng.Fori(2, CHUNKS // 2 - 2) as i:
                for u in (0, 1):
                    body(2 * i + u, u, i)
            for c in range(CHUNKS - 4, CHUNKS):
                body(c, c % 2, c // 2)

        def before(c, n):
            return not isinstance(c, int) or c >= n

        def ahead(c, n):
            return not isinstance(c, int) or c + n <= LAST

        with nc.Block() as block:
            @block.sync
            def _(sp):
                load_turned(sp, 0, 0)
                load_turned(sp, 1, 1)
                load_residual(sp, 0, 0)
                load_turned(sp, 2, 0)

                def step(c, u, half):
                    if ahead(c, 3):
                        load_turned(sp, c + 3, 1 - u)
                    if before(c, 2):
                        store(sp, c - 2, u)
                    if ahead(c, 1):
                        load_residual(sp, c + 1, 1 - u)
                chunks(sp, step)
                store(sp, LAST - 1, 0)
                store(sp, LAST, 1)
                for u in range(2):
                    sp.wait_ge(x1_stored[u], 16 * CHUNKS // 2)

            @block.tensor
            def _(pe):
                pe.wait_ge(hold["mixer_in"], MIXER_WEIGHTS)
                pe.wait_ge(s["zeros"], 3)
                for c in (0, 1):
                    for grp in range(3):
                        project(pe, c, c, 0, grp)

                def step(c, u, half):
                    turn(pe, c, u)
                    score(pe, c, u, 0)
                    score(pe, c, u, 1)
                    add_to_state(pe, c)
                    score(pe, c, u, 2)
                    score(pe, c, u, 3)
                    weigh_steps(pe, c, u)
                    if ahead(c, 2):
                        project(pe, c + 2, u, half + 1, 0)
                    turn_rates(pe, c)
                    if ahead(c, 2):
                        project(pe, c + 2, u, half + 1, 1)
                        project(pe, c + 2, u, half + 1, 2)
                    project_out(pe, c)
                chunks(pe, step)

            @block.scalar
            def _(act):
                for grp in range(3):
                    take_projection(act, 0, 0, grp)
                pass_halo(act, 0, 0)
                for grp in range(3):
                    take_projection(act, 1, 1, grp)
                act.wait_ge(s["zeros"], 3)
                spread_c(act, 0, 0)
                pass_halo(act, 1, 1)
                spread_rates(act, 0)

                def step(c, u, half):
                    take_b(act, c)
                    if ahead(c, 2):
                        take_projection(act, c + 2, u, 0)
                    take_rates(act, c)
                    if ahead(c, 2):
                        take_projection(act, c + 2, u, 1)
                        take_projection(act, c + 2, u, 2)
                    if ahead(c, 1):
                        spread_c(act, c + 1, 1 - u)
                    if ahead(c, 3):
                        pass_halo(act, c + 2, u)
                    if ahead(c, 1):
                        spread_rates(act, c + 1)
                chunks(act, step)

            @block.gpsimd
            def _(pool):
                nc.gpsimd.memset(cbd[:], 0.0).then_inc(s["zeros"], 1)
                nc.gpsimd.memset(proj[0][:, :, 0:HALO], 0.0).then_inc(s["zeros"], 1)
                nc.gpsimd.memset(state[:], 0.0).then_inc(s["zeros"], 1)
                pool.wait_ge(hold["mixer_in"], MIXER_WEIGHTS)
                pool.wait_ge(s["zeros"], 3)
                convolve_x(pool, 0, 0)

                def step(c, u, half):
                    if ahead(c, 1):
                        convolve_x(pool, c + 1, 1 - u)
                chunks(pool, step)

            @block.vector
            def _(dve):
                dve.wait_ge(hold["mixer_in"], MIXER_WEIGHTS)
                dve.wait_ge(s["zeros"], 3)
                convolve(dve, 0, 0)

                def step(c, u, half):
                    weigh_x(dve, c)
                    mask_scores(dve, c)
                    advance_state(dve, c)
                    if before(c, 1):
                        norm(dve, c - 1, 1 - u, half - 1 + u)
                    rate_outputs(dve, c)
                    if ahead(c, 1):
                        convolve(dve, c + 1, 1 - u)
                chunks(dve, step)
                norm(dve, LAST, 1, CHUNKS // 2 - 1)


def prefetch(sp, io, ring, ring_in, e, unit):
    kind, half = unit // 2, unit % 2
    if kind < 2:
        src = (io["e_W1"], io["e_Wg"])[kind].rearrange("e (p k) f -> e p (k f)", p=P)[bass.ds(e, 1), :, half * UNIT:(half + 1) * UNIT]
        dst = ring[:, unit, :]
        sp.dma_start(dst, src.rearrange("o p f -> (o p) f")).then_inc(ring_in[unit], 16)
    else:
        src = io["e_W2"].rearrange("e (q p s) n -> e p q (s n)", q=4, p=P)[bass.ds(e, 1), :, 2 * half:2 * half + 2, :]
        dst = ring[:, unit, :].rearrange("p (q n) -> p q n", q=2)
        sp.dma_start(dst, src.rearrange("o p q n -> (o p) q n")).then_inc(ring_in[unit], 16)


FIRST_UNITS = {1: (0, 1), CHUNKS - 2: (2, 3), CHUNKS: (4, 5)}


def cross_stage(nc, io, hold, ring, ring_in):
    with Stage(nc, "crs") as st:
        wq = st.sb("wq", [P, KC, D])
        wo = st.sb("wo", [P, KC, D])
        qbias = st.sb("qbias", [P, GROUPS])
        ob = st.sb("ob", [P, D])
        x1 = [st.sb(f"x1_{i}", [P, D]) for i in range(2)]
        x1b = [st.sb(f"x1b{i}", [P, D]) for i in range(2)]
        x1T = st.sb("x1T", [P, KC, P])
        qT = st.sb("qT", [P, GROUPS, P])
        pr = st.sb("pr", [P, HEADS, CTX])
        top = st.sb("top", [P, HEADS])
        den = st.sb("den", [P, HEADS])
        rden = st.sb("rden", [P, HEADS])
        prT = st.sb("prT", [PIECE, 3, GROUPS * P])
        y = st.sb("y", [P, D])
        yT = st.sb("yT", [P, KC, P])
        xr = st.sb("xr", [P, D])
        stats = st.sb("stats", [P, 1, 12])
        x2 = [st.sb(f"x2_{i}", [P, D]) for i in range(2)]
        x2T = [st.sb(f"x2T{i}", [P, KC, P]) for i in range(2)]
        tile_top = st.sb("tile_top", [P, SM])
        new_top = st.sb("new_top", [P, SM])
        drop = st.sb("drop", [P, SM])
        shift = st.sb("shift", [P, SM])
        alpha = st.sb("alpha", [P, SM])
        tile_sum = st.sb("tile_sum", [P, SM])
        sp_pr = st.sb("sp_pr", [P, SM, P])
        sp_prT = st.sb("sp_prT", [P, SROWS])
        bank = st.banks()
        SC, AV, TURN, OUT, SLOT, TOK = bank[0:3], bank[3], bank[4], bank[5], bank[6], bank[7]
        s = st.sems("weights_in", "zeros", "mix_turned", "x1T_done", "q_done", "qT_done", "sc_done", "masked", "top_done", "shifted", "exp_done",
                    "den_done", "rden_done", "pr_turned", "prT_done", "av_done", "y_done", "y_turned", "yT_done", "o_done", "x1b_done",
                    "res_done", "ln_step", "x2_done", "x2_turned", "x2T_done", "slot_sc", "slot_step", "slot_shift", "slot_alpha", "slot_exp", "slot_sum",
                    "slot_turned", "sp_prT_done", "z_done", "z_added")
        x1_in, x2_stored, x2T_stored = st.pair("x1_in"), st.pair("x2_stored"), st.pair("x2T_stored")
        LAST = TILES - 1
        SB = 512 // CTX
        HEADS_OF = [(i * SB, min((i + 1) * SB, HEADS)) for i in range(3)]

        def load(sp, t, u):
            wait_later(sp, s["mix_turned"], t - 1)
            wait_later(sp, s["x1b_done"], t - 1)
            sp.dma_start(x1[u][:], io["x1"][bass.ds(t * P, P), :]).then_inc(x1_in[u], 16)

        def store_x2(sp, t, u):
            sp.wait_ge(s["x2_done"], t + 1)
            sp.dma_start(io["x2"][bass.ds(t * P, P), :], x2[u][:]).then_inc(x2_stored[u], 16)

        def store_x2T(sp, t, u):
            sp.wait_ge(s["x2T_done"], t + 1)
            sp.dma_start(io["x2T"][bass.ds(t * P, P), :], x2T[u][:].rearrange("p k t -> p (k t)")).then_inc(x2T_stored[u], 16)

        def turn_x1(pe, t, u, half):
            pe.wait_ge(x1_in[u], 16 * (half + 1))
            wait_later(pe, s["z_added"], 2 * (t - 3))
            wait_later(pe, s["x1T_done"], t)
            for k in range(KC):
                last = nc.tensor.transpose(TOK[:, k * P:(k + 1) * P], x1[u][:, k * P:(k + 1) * P], hold["ident"][:])
            last.then_inc(s["mix_turned"], 1)

        def queries(pe, t):
            pe.wait_ge(s["x1T_done"], t + 1)
            wait_later(pe, s["qT_done"], t)
            wait_later(pe, s["y_done"], t - 1)
            for g in range(GROUPS):
                for k in range(KC):
                    last = nc.tensor.matmul(AV[:, g * P:(g + 1) * P], wq[:, k, g * P:(g + 1) * P], x1T[:, k, :],
                                            start=(k == 0), stop=(k == KC - 1))
            last.then_inc(s["q_done"], 1)

        def score(pe, t, b):
            pe.wait_ge(s["qT_done"], t + 1)
            wait_later(pe, s["prT_done"], 3 * t)
            for i, (h0, h1) in enumerate(HEADS_OF):
                for g in range(h0 // HG, -(-h1 // HG)):
                    a, z = max(h0, g * HG), min(h1, (g + 1) * HG)
                    last = nc.tensor.matmul(SC[i][:, (a - h0) * CTX:(z - h0) * CTX], qT[:, g, :],
                                            hold["kbd"][:, b, g, a - g * HG:z - g * HG, :], start=True, stop=True)
                last.then_inc(s["sc_done"], 1)

        def turn_probs(pe, t):
            pe.wait_ge(s["exp_done"], t + 1)
            for i, w in enumerate(PIECES):
                for g in range(GROUPS):
                    at = g * KROWS + i * PIECE
                    last = nc.tensor.transpose(SC[i][0:w, g * P:(g + 1) * P], pr[:].rearrange("p h s -> p (h s)")[:, at:at + w], hold["ident"][:])
                last.then_inc(s["pr_turned"], 1)

        def weigh_values(pe, t, b):
            pe.wait_ge(s["prT_done"], 3 * t + 3)
            pe.wait_ge(s["qT_done"], min(t + 2, TILES) if isinstance(t, int) else t + 2)
            for g in range(GROUPS):
                for i, w in enumerate(PIECES):
                    last = nc.tensor.matmul(AV[:, g * P:(g + 1) * P], prT[0:w, i, g * P:(g + 1) * P], hold["vbd"][0:w, b, i, g, :],
                                            start=(i == 0), stop=(i == 2))
            last.then_inc(s["av_done"], 1)

        def turn_y(pe, t):
            pe.wait_ge(s["y_done"], t + 1)
            wait_later(pe, s["x2T_done"], t)
            for k in range(KC):
                last = nc.tensor.transpose(TURN[:, k * P:(k + 1) * P], y[:, k * P:(k + 1) * P], hold["ident"][:])
            last.then_inc(s["y_turned"], 1)

        def project_out(pe, t):
            pe.wait_ge(s["yT_done"], t + 1)
            wait_later(pe, s["res_done"], t)
            for k in range(KC):
                last = nc.tensor.matmul(OUT[:], yT[:, k, :], wo[:, k, :], start=(k == 0), stop=(k == KC - 1))
            last.then_inc(s["o_done"], 1)

        def turn_x2(pe, t, u):
            pe.wait_ge(s["x2_done"], t + 1)
            pe.wait_ge(s["yT_done"], t + 1)
            for k in range(KC):
                last = nc.tensor.transpose(TURN[:, k * P:(k + 1) * P], x2[u][:, k * P:(k + 1) * P], hold["ident"][:])
            last.then_inc(s["x2_turned"], 1)

        def slot_scores(pe, t, u):
            pe.wait_ge(s["x2T_done"], t + 1)
            wait_later(pe, s["slot_exp"], t)
            for m in range(SM):
                for k in range(KC):
                    last = nc.tensor.matmul(SLOT[:, m * P:(m + 1) * P], hold["m1"][:, k, m * P:(m + 1) * P], x2T[u][:, k, :],
                                            start=(k == 0), stop=(k == KC - 1))
            last.then_inc(s["slot_sc"], 1)

        def turn_slots(pe, t):
            pe.wait_ge(s["slot_exp"], t + 1)
            wait_later(pe, s["sp_prT_done"], t)
            for m in range(SM):
                last = nc.tensor.transpose(SLOT[:, SROWS + m * P:SROWS + (m + 1) * P], sp_pr[:, m, :], hold["ident"][:])
            last.then_inc(s["slot_turned"], 1)

        def weigh_tokens(pe, t, u, m):
            pe.wait_ge(s["sp_prT_done"], t + 1)
            if m == 1:
                pe.wait_ge(s["z_added"], 2 * t + 1)
            else:
                wait_later(pe, s["z_added"], 2 * t)
                pe.wait_ge(s["x1T_done"], min(t + 4, TILES) if isinstance(t, int) else t + 4)
            nc.tensor.matmul(TOK[:], sp_prT[:, m * P:(m + 1) * P], x2[u][:], start=True, stop=True).then_inc(s["z_done"], 1)

        def take_x1T(act, t):
            act.wait_ge(s["mix_turned"], t + 1)
            wait_later(act, s["q_done"], t)
            nc.scalar.activation(x1T[:].rearrange("p k t -> p (k t)"), TOK[:], ACT.Copy).then_inc(s["x1T_done"], 1)

        def exponents(act, t):
            act.wait_ge(s["shifted"], t + 1)
            nc.scalar.activation(pr[:], pr[:], ACT.Exp, scale=SCALE).then_inc(s["exp_done"], 1)

        def take_x2T(act, t, u, half):
            act.wait_ge(s["x2_turned"], t + 1)
            wait_later(act, s["slot_sc"], t - 1)
            wait_later(act, x2T_stored[u], 16 * half)
            nc.scalar.activation(x2T[u][:].rearrange("p k t -> p (k t)"), TURN[:], ACT.Copy).then_inc(s["x2T_done"], 1)

        def slot_exponents(act, t):
            act.wait_ge(s["slot_shift"], t + 1)
            wait_later(act, s["z_added"], 2 * t)
            wait_later(act, s["slot_sum"], 2 * t)
            nc.scalar.activation(alpha[:], drop[:], ACT.Exp).then_inc(s["slot_alpha"], 1)
            wait_later(act, s["slot_turned"], t)
            for m in range(SM):
                last = nc.scalar.activation(sp_pr[:, m, :], SLOT[:, m * P:(m + 1) * P], ACT.Exp, bias=shift[:, m:m + 1], scale=SCALE,
                                            accum_out=tile_sum[:, m:m + 1])
            last.then_inc(s["slot_exp"], 1)

        def take_probsT(act, t):
            wait_later(act, s["av_done"], t)
            for i, w in enumerate(PIECES):
                act.wait_ge(s["pr_turned"], 3 * t + i + 1)
                nc.scalar.activation(prT[0:w, i, :], SC[i][0:w, :], ACT.Copy).then_inc(s["prT_done"], 1)

        def take_slotsT(act, t):
            act.wait_ge(s["slot_turned"], t + 1)
            wait_later(act, s["z_done"], 2 * t)
            nc.scalar.activation(sp_prT[:], SLOT[:, SROWS:2 * SROWS], ACT.Copy).then_inc(s["sp_prT_done"], 1)

        def take_yT(act, t):
            act.wait_ge(s["y_turned"], t + 1)
            wait_later(act, s["o_done"], t)
            nc.scalar.activation(yT[:].rearrange("p k t -> p (k t)"), TURN[:], ACT.Copy).then_inc(s["yT_done"], 1)

        def take_scores(dve, t, causal):
            src = [SC[i][:, 0:(h1 - h0) * CTX].rearrange("p (h s) -> p h s", s=CTX) for i, (h0, h1) in enumerate(HEADS_OF)]
            if causal:
                wait_later(dve, s["pr_turned"], 3 * t)
                for i, (h0, h1) in enumerate(HEADS_OF):
                    dve.wait_ge(s["sc_done"], 3 * t + i + 1)
                    last = nc.vector.tensor_tensor(pr[:, h0:h1, :], src[i], broadcast(hold["mask"][:].unsqueeze(1), [P, h1 - h0, CTX]), ALU.add)
                    src[i] = pr[:, h0:h1, :]
                last.then_inc(s["masked"], 1)
                dve.wait_ge(s["masked"], 1 if t == 0 else 2)
            for i, (h0, h1) in enumerate(HEADS_OF):
                dve.wait_ge(s["sc_done"], 3 * t + i + 1)
                last = nc.vector.tensor_reduce(top[:, h0:h1], src[i], AX.X, ALU.max)
            last.then_inc(s["top_done"], 1)
            dve.wait_ge(s["top_done"], t + 1)
            wait_later(dve, s["pr_turned"], 3 * t)
            for i, (h0, h1) in enumerate(HEADS_OF):
                last = nc.vector.tensor_tensor(pr[:, h0:h1, :], src[i], broadcast(top[:, h0:h1].unsqueeze(2), [P, h1 - h0, CTX]), ALU.subtract)
            last.then_inc(s["shifted"], 1)

        def take_queries(dve, t):
            dve.wait_ge(s["q_done"], t + 1)
            wait_later(dve, s["sc_done"], 3 * t)
            nc.vector.tensor_tensor(qT[:], AV[:].rearrange("p (g t) -> p g t", g=GROUPS), broadcast(qbias[:].unsqueeze(2), [P, GROUPS, P]),
                                    ALU.add).then_inc(s["qT_done"], 1)

        def slot_maxima(dve, t, b):
            st_top = hold["top"][:, b, :]
            dve.wait_ge(s["slot_sc"], t + 1)
            wait_later(dve, s["slot_exp"], t)
            first = 3 * t
            nc.vector.tensor_reduce(tile_top[:], SLOT[:, 0:SROWS].rearrange("p (m t) -> p m t", m=SM), AX.X, ALU.max).then_inc(s["slot_step"], 1)
            dve.wait_ge(s["slot_step"], first + 1)
            nc.vector.scalar_tensor_tensor(tile_top[:], tile_top[:], SCALE, hold["kbias"][:], ALU.mult, ALU.add).then_inc(s["slot_step"], 1)
            dve.wait_ge(s["slot_step"], first + 2)
            nc.vector.tensor_tensor(new_top[:], st_top, tile_top[:], ALU.max).then_inc(s["slot_step"], 1)
            dve.wait_ge(s["slot_step"], first + 3)
            nc.vector.tensor_tensor(drop[:], st_top, new_top[:], ALU.subtract)
            nc.vector.tensor_tensor(shift[:], hold["kbias"][:], new_top[:], ALU.subtract).then_inc(s["slot_shift"], 1)
            dve.wait_ge(s["slot_shift"], t + 1)
            nc.vector.tensor_copy(st_top, new_top[:])

        def denominators(dve, t):
            dve.wait_ge(s["exp_done"], t + 1)
            nc.vector.tensor_reduce(den[:], pr[:], AX.X, ALU.add).then_inc(s["den_done"], 1)
            dve.wait_ge(s["den_done"], t + 1)
            nc.vector.reciprocal(rden[:], den[:]).then_inc(s["rden_done"], 1)

        def slot_sums(dve, t, b):
            st_sum = hold["sum"][:, b, :]
            dve.wait_ge(s["slot_exp"], t + 1)
            nc.vector.tensor_tensor(st_sum, st_sum, alpha[:], ALU.mult).then_inc(s["slot_sum"], 1)
            dve.wait_ge(s["slot_sum"], 2 * t + 1)
            nc.vector.tensor_tensor(st_sum, st_sum, tile_sum[:], ALU.add).then_inc(s["slot_sum"], 1)

        def normalise(dve, t):
            dve.wait_ge(s["rden_done"], t + 1)
            dve.wait_ge(s["av_done"], t + 1)
            wait_later(dve, s["y_turned"], t)
            nc.vector.tensor_tensor(y[:].rearrange("p (h d) -> p h d", h=HEADS), AV[:].rearrange("p (h d) -> p h d", h=HEADS),
                                    broadcast(rden[:].unsqueeze(2), [P, HEADS, HD]), ALU.mult).then_inc(s["y_done"], 1)

        def add_tokens(dve, t, b, m):
            z = hold["z"][:, b, m, :]
            dve.wait_ge(s["z_done"], 2 * t + m + 1)
            nc.vector.scalar_tensor_tensor(z, z, alpha[:, m:m + 1], TOK[:], ALU.mult, ALU.add).then_inc(s["z_added"], 1)

        def residual(dve, t, u):
            dve.wait_ge(s["o_done"], t + 1)
            dve.wait_ge(s["x1b_done"], t + 1)
            wait_later(dve, s["x2_done"], t)
            nc.vector.tensor_tensor(xr[:], OUT[:], x1b[u][:], ALU.add).then_inc(s["res_done"], 1)

        def norm(dve, t, u, half):
            dve.wait_ge(s["res_done"], t + 1)
            wait_later(dve, x2_stored[u], 16 * half)
            wait_later(dve, s["z_done"], 2 * t - 2)
            layernorm(nc, dve, s["ln_step"], LN_STEPS * t, [xr[:]], stats, [x2[u][:]]).then_inc(s["x2_done"], 1)

        def add_bias(pool, t, u, half):
            pool.wait_ge(x1_in[u], 16 * (half + 1))
            wait_later(pool, s["res_done"], t - 1)
            nc.gpsimd.tensor_tensor(x1b[u][:], x1[u][:], ob[:], ALU.add).then_inc(s["x1b_done"], 1)

        def tiles(eng, body):
            def alone(*ts):
                for t in ts:
                    body(t, t % 2, t // 2, lambda d, t=t: (t + d) // CHUNKS)

            def loop(first, end, b):
                with eng.Fori(first // 2, end // 2) as i:
                    for u in (0, 1):
                        body(2 * i + u, u, i, lambda d: b)
            alone(0, 1, 2, 3)
            loop(4, CHUNKS - 2, 0)
            alone(CHUNKS - 2, CHUNKS - 1, CHUNKS, CHUNKS + 1)
            loop(CHUNKS + 2, TILES - 2, 1)
            alone(TILES - 2, TILES - 1)

        def before(t, tiles):
            return not isinstance(t, int) or t >= tiles

        def ahead(t, tiles):
            return not isinstance(t, int) or t + tiles <= LAST

        with nc.Block() as block:
            @block.sync
            def _(sp):
                load(sp, 0, 0)
                sp.dma_start(wq[:], io["q_w"].rearrange("(k p) n -> p k n", p=P)).then_inc(s["weights_in"], 16)
                sp.dma_start(qbias[:], io["q_b"]).then_inc(s["weights_in"], 16)
                load(sp, 1, 1)
                sp.dma_start(wo[:], io["o_w"].rearrange("(k p) n -> p k n", p=P)).then_inc(s["weights_in"], 16)
                sp.dma_start(ob[:], broadcast(io["o_b"].rearrange("(o n) -> o n", o=1), [P, D])).then_inc(s["weights_in"], 16)

                def step(t, u, half, seq):
                    if ahead(t, 2):
                        load(sp, t + 2, u)
                    if before(t, 1):
                        store_x2(sp, t - 1, 1 - u)
                        store_x2T(sp, t - 1, 1 - u)
                    if isinstance(t, int) and t in FIRST_UNITS:
                        for unit in FIRST_UNITS[t]:
                            prefetch(sp, io, ring, ring_in, 0, unit)
                tiles(sp, step)
                store_x2(sp, LAST, 1)
                store_x2T(sp, LAST, 1)
                for u in range(2):
                    sp.wait_ge(x2_stored[u], 16 * TILES // 2)
                    sp.wait_ge(x2T_stored[u], 16 * TILES // 2)

            @block.tensor
            def _(pe):
                pe.wait_ge(s["weights_in"], 4 * 16)
                turn_x1(pe, 0, 0, 0)
                queries(pe, 0)
                turn_x1(pe, 1, 1, 0)
                score(pe, 0, 0)
                queries(pe, 1)

                def step(t, u, half, seq):
                    turn_probs(pe, t)
                    if before(t, 1):
                        turn_x2(pe, t - 1, 1 - u)
                    if before(t, 2):
                        weigh_tokens(pe, t - 2, u, 1)
                    if before(t, 1):
                        slot_scores(pe, t - 1, 1 - u)
                    weigh_values(pe, t, seq(0))
                    if ahead(t, 1):
                        score(pe, t + 1, seq(1))
                    turn_y(pe, t)
                    if before(t, 1):
                        turn_slots(pe, t - 1)
                    if ahead(t, 2):
                        turn_x1(pe, t + 2, u, half + 1)
                    project_out(pe, t)
                    if before(t, 1):
                        weigh_tokens(pe, t - 1, 1 - u, 0)
                    if ahead(t, 2):
                        queries(pe, t + 2)
                tiles(pe, step)
                turn_x2(pe, LAST, 1)
                weigh_tokens(pe, LAST - 1, 0, 1)
                slot_scores(pe, LAST, 1)
                turn_slots(pe, LAST)
                for m in range(SM):
                    weigh_tokens(pe, LAST, 1, m)

            @block.scalar
            def _(act):
                take_x1T(act, 0)
                take_x1T(act, 1)
                exponents(act, 0)

                def step(t, u, half, seq):
                    take_probsT(act, t)
                    if before(t, 1):
                        take_x2T(act, t - 1, 1 - u, half - 1 + u)
                        slot_exponents(act, t - 1)
                    take_yT(act, t)
                    if before(t, 1):
                        take_slotsT(act, t - 1)
                    if ahead(t, 2):
                        take_x1T(act, t + 2)
                    if ahead(t, 1):
                        exponents(act, t + 1)
                tiles(act, step)
                take_x2T(act, LAST, 1, TILES // 2 - 1)
                slot_exponents(act, LAST)
                take_slotsT(act, LAST)

            @block.vector
            def _(dve):
                nc.vector.memset(hold["top"][:], NEG)
                nc.vector.memset(hold["sum"][:], 0.0)
                nc.vector.memset(hold["z"][:], 0.0).then_inc(s["zeros"], 1)
                dve.wait_ge(s["zeros"], 1)
                dve.wait_ge(s["weights_in"], 4 * 16)
                take_queries(dve, 0)
                take_scores(dve, 0, True)

                def step(t, u, half, seq):
                    if ahead(t, 1):
                        take_queries(dve, t + 1)
                    denominators(dve, t)
                    if before(t, 2):
                        add_tokens(dve, t - 2, seq(-2), 1)
                    if before(t, 1):
                        slot_maxima(dve, t - 1, seq(-1))
                    normalise(dve, t)
                    if before(t, 1):
                        slot_sums(dve, t - 1, seq(-1))
                    if ahead(t, 1):
                        take_scores(dve, t + 1, isinstance(t, int) and (t + 1) % CHUNKS == 0)
                    residual(dve, t, u)
                    if before(t, 1):
                        add_tokens(dve, t - 1, seq(-1), 0)
                    norm(dve, t, u, half)
                tiles(dve, step)
                add_tokens(dve, LAST - 1, 1, 1)
                slot_maxima(dve, LAST, 1)
                slot_sums(dve, LAST, 1)
                for m in range(SM):
                    add_tokens(dve, LAST, 1, m)

            @block.gpsimd
            def _(pool):
                pool.wait_ge(s["weights_in"], 4 * 16)
                add_bias(pool, 0, 0, 0)

                def step(t, u, half, seq):
                    if ahead(t, 1):
                        add_bias(pool, t + 1, 1 - u, half + u)
                tiles(pool, step)


ROWS = BATCH * SLOTS


def experts_stage(nc, io, hold, ring, ring_in):
    with Stage(nc, "exp") as st:
        dwv = st.sb("dwv", [P, KC, D])
        dwo = st.sb("dwo", [P, KC, D])
        dbv = st.sb("dbv", [P, GROUPS])
        dbo = st.sb("dbo", [ROWS, D])
        slot = st.sb("slot", [ROWS, D])
        ln_g = st.sb("ln_g", [ROWS, D])
        ln_b = st.sb("ln_b", [ROWS, D])
        b2 = st.sb("b2", [ROWS, D])
        rsum = st.sb("rsum", [P, BATCH, SM])
        znT = st.sb("znT", [P, KC, BATCH, SROWS])
        aoT = st.sb("aoT", [P, GROUPS, BATCH, SLOTS])
        o = st.sb("o", [ROWS, D])
        h = st.sb("h", [ROWS, D])
        stats = st.sb("stats", [ROWS, 1, 12])
        hT = st.sb("hT", [P, KC, ROWS])
        pick = st.sb("pick", [P, EXPERTS, ROWS])
        fold = st.sb("fold", [P, ROWS])
        hm = [st.sb(f"hm{i}", [P, KC, ROWS]) for i in range(2)]
        pm = [st.sb(f"pm{i}", [P, 4, ROWS]) for i in range(2)]
        quarter = st.sb("quarter", [P, 4, ROWS])
        bias = st.sb("bias", [P, 2, FQ])
        up = st.sb("up", [P, FQ])
        gate = st.sb("gate", [P, FQ])
        gu = st.sb("gu", [P, FQ])
        guT = st.sb("guT", [P, 4, P])
        y4 = st.sb("y4", [P, D])
        cwk, cwqT = dwv, dwo
        cwv = shaped(znT[:].rearrange("p k b r -> p (k b r)"), [P, KC, D])
        cwo = shaped(hold["z"][:].rearrange("p b m d -> p (b m d)"), [P, KC, D])
        cbk = st.sb("cbk", [P, GROUPS])
        cbv = st.sb("cbv", [P, GROUPS])
        cbq = st.sb("cbq", [P, GROUPS])
        cbo = st.sb("cbo", [P, D])
        cbqb = st.sb("cbqb", [P, GROUPS, P])
        oT = st.sb("oT", [P, KC, ROWS])
        kbd = st.sb("kbd", [P, GROUPS, BATCH, HG, SLOTS])
        vbd = st.sb("vbd", [P, GROUPS, BATCH, HG, SLOTS])
        bank = st.banks()
        s = st.sems("slot_w_in", "rows_in", "comb_w_in", "zeros", "consts", "rsum_done", "zn_done", "zn_turned", "znT_done", "ao_done", "aoT_done",
                    "wo_done", "o_step", "ln_step", "h_turned", "hT_done", "hm_done", "bias_in", "up_done", "silu_done", "gu_done",
                    "gu_turned", "guT_done", "y4_done", "fold_done", "o_done", "o_turned", "oT_done",
                    "k_done", "kbd_done", "v_done", "vbd_done", "qb_done", "m2_done", "m2_out", "kb_done", "vo_done", "vo_out")
        unit_used = [st.sem(f"unit_used{i}") for i in range(UNITS)]

        def expert(pe, e, u):
            pe.wait_ge(s["hm_done"], e + 1)
            wait_later(pe, s["silu_done"], 2 * e)
            pe.wait_ge(s["bias_in"], 32 * (e + 1))
            for w in range(2):
                for k in range(KC):
                    if k % 2 == 0:
                        pe.wait_ge(ring_in[2 * w + k // 2], 16 * (e + 1))
                    for q in range(4):
                        at = (k % 2) * F + q * FQ
                        last = nc.tensor.matmul(bank[w][q * ROWS:(q + 1) * ROWS, :], hm[u][:, k, :], ring[:, 2 * w + k // 2, at:at + FQ],
                                                start=(k == 0), stop=False)
                    if k % 2 == 1:
                        last.then_inc(unit_used[2 * w + k // 2], 1)
                for q in range(4):
                    last = nc.tensor.matmul(bank[w][q * ROWS:(q + 1) * ROWS, :], pm[u][:, q, :], bias[:, w, :], start=False, stop=True)
                last.then_inc(s["up_done"], 1)
            pe.wait_ge(s["gu_done"], e + 1)
            wait_later(pe, s["guT_done"], e)
            for i in range(4):
                last = nc.tensor.transpose(bank[2][:, i * P:(i + 1) * P], gu[:].rearrange("r (p i) -> r i p", i=4)[:, i, :], hold["ident"][:])
            last.then_inc(s["gu_turned"], 1)
            pe.wait_ge(s["guT_done"], e + 1)
            first = isinstance(e, int) and e == 0
            final = isinstance(e, int) and e == EXPERTS - 1
            for half in range(2):
                pe.wait_ge(ring_in[4 + half], 16 * (e + 1))
                for i in range(4):
                    for j in range(2):
                        q = 2 * half + j
                        last = nc.tensor.matmul(bank[3][q * ROWS:(q + 1) * ROWS, :], guT[:, i, q * ROWS:(q + 1) * ROWS],
                                                ring[:, 4 + half, (j * 4 + i) * D:(j * 4 + i + 1) * D],
                                                start=first and i == 0, stop=final and i == 3, skip_group_check=True)
                last.then_inc(unit_used[4 + half], 1)

        def masked(dve, e, u):
            wait_later(dve, s["up_done"], 2 * e - 2)
            nc.vector.tensor_tensor(hm[u][:], hT[:], broadcast(pick[:, bass.ds(e, 1), :], [P, KC, ROWS]), ALU.mult)
            nc.vector.tensor_tensor(pm[u][:], quarter[:], broadcast(pick[:, bass.ds(e, 1), :], [P, 4, ROWS]), ALU.mult).then_inc(s["hm_done"], 1)

        def combine_up(dve, e):
            dve.wait_ge(s["silu_done"], 2 * e + 2)
            wait_later(dve, s["gu_turned"], e)
            nc.vector.tensor_tensor(gu[:], up[:], gate[:], ALU.mult).then_inc(s["gu_done"], 1)
            dve.wait_ge(s["gu_turned"], e + 1)
            wait_later(dve, unit_used[5], e)
            nc.vector.tensor_copy(guT[:].rearrange("p i r -> p (i r)"), bank[2][:]).then_inc(s["guT_done"], 1)

        def activate(act, e):
            wait_later(act, s["gu_done"], e)
            for w, dst in ((0, up), (1, gate)):
                act.wait_ge(s["up_done"], 2 * e + w + 1)
                nc.scalar.activation(dst[:], bank[w][:], ACT.Silu).then_inc(s["silu_done"], 1)

        def experts(eng, body):
            for e in (0, 1):
                body(e, e)
            with eng.Fori(1, EXPERTS // 2 - 1) as i:
                for u in (0, 1):
                    body(2 * i + u, u)
            for e in (EXPERTS - 2, EXPERTS - 1):
                body(e, e % 2)

        with nc.Block() as block:
            @block.sync
            def _(sp):
                for dst, src in ((dwv, io["d_Wv"]), (dwo, io["d_Wo"])):
                    sp.dma_start(dst[:], src.rearrange("(k p) n -> p k n", p=P)).then_inc(s["slot_w_in"], 16)
                sp.dma_start(dbv[:], io["d_bv"]).then_inc(s["slot_w_in"], 16)
                sp.dma_start(dbo[:], broadcast(io["d_bo"].rearrange("(o n) -> o n", o=1), [ROWS, D])).then_inc(s["rows_in"], 16)
                for dst, src in ((slot, io["slot"]), (ln_g, io["e_ln_g"]), (ln_b, io["e_ln_b"]), (b2, io["e_b2"])):
                    for b in range(BATCH):
                        sp.dma_start(dst[b * SLOTS:(b + 1) * SLOTS, :], src).then_inc(s["rows_in"], 16)

                def step(e, u):
                    if isinstance(e, int) and e == 0:
                        return
                    for unit in range(UNITS):
                        sp.wait_ge(unit_used[unit], e)
                        prefetch(sp, io, ring, ring_in, e, unit)
                    if isinstance(e, int) and e == 1:
                        sp.wait_ge(s["wo_done"], 1)
                        for dst, src in ((cwk, io["c_Wk"]), (cwqT, io["c_WqT"]), (cwv, io["c_Wv"]), (cwo, io["c_Wo"])):
                            sp.dma_start(dst[:], src.rearrange("(k p) n -> p k n", p=P)).then_inc(s["comb_w_in"], 16)
                        for dst, src in ((cbk, io["c_bk"]), (cbv, io["c_bv"]), (cbq, io["c_bq"]),
                                         (cbo, broadcast(io["c_bo"].rearrange("(o n) -> o n", o=1), [P, D]))):
                            sp.dma_start(dst[:], src).then_inc(s["comb_w_in"], 16)
                experts(sp, step)

            @block.gpsimd
            def _(pool):
                nc.gpsimd.memset(pick[:], 0.0).then_inc(s["zeros"], 1)
                nc.gpsimd.memset(fold[:], 0.0).then_inc(s["zeros"], 1)
                nc.gpsimd.memset(bias[:], 0.0).then_inc(s["zeros"], 1)
                nc.gpsimd.memset(quarter[:], 0.0).then_inc(s["zeros"], 1)
                pool.wait_ge(s["zeros"], 4)
                nc.gpsimd.affine_select(out=quarter[:], in_=quarter[:], compare_op=ALU.not_equal, fill=1.0, base=0,
                                        pattern=[[-1, 4], [0, ROWS]], channel_multiplier=1).then_inc(s["consts"], 1)
                p4 = pick[:].rearrange("p e (b r) -> p e b r", b=BATCH)
                nc.gpsimd.affine_select(out=p4, in_=p4, compare_op=ALU.not_equal, fill=1.0, base=0,
                                        pattern=[[1, EXPERTS], [0, BATCH], [-1, SLOTS]], channel_multiplier=0).then_inc(s["consts"], 1)
                for q in range(4):
                    nc.gpsimd.affine_select(out=fold[:], in_=fold[:], compare_op=ALU.not_equal, fill=1.0, base=-q * ROWS,
                                            pattern=[[-1, ROWS]], channel_multiplier=1).then_inc(s["consts"], 1)
                    pool.wait_ge(s["consts"], q + 3)
                nc.gpsimd.memset(kbd[:], 0.0).then_inc(s["zeros"], 1)
                nc.gpsimd.memset(vbd[:], 0.0).then_inc(s["zeros"], 1)

                def step(e, u):
                    wait_later(pool, s["up_done"], 2 * e)
                    for w, src in ((0, io["e_b1"]), (1, io["e_bg"])):
                        pool.dma_start(bias[0:4, w, :], src.rearrange("e (q f) -> e q f", q=4)[bass.ds(e, 1), :, :].rearrange("o q f -> (o q) f")).then_inc(s["bias_in"], 16)
                experts(pool, step)
                pool.wait_ge(s["comb_w_in"], 8 * 16)
                nc.gpsimd.tensor_copy(cbqb[:], broadcast(cbq[:].unsqueeze(2), [P, GROUPS, P])).then_inc(s["qb_done"], 1)

            @block.tensor
            def _(pe):
                for b in range(BATCH):
                    for m in range(SM):
                        i = b * SM + m
                        pe.wait_ge(s["zn_done"], i + 1)
                        for k in range(KC):
                            last = nc.tensor.transpose(bank[i][:, k * P:(k + 1) * P], hold["z"][:, b, m, k * P:(k + 1) * P], hold["ident"][:])
                        last.then_inc(s["zn_turned"], 1)
                pe.wait_ge(s["slot_w_in"], 3 * 16)
                pe.wait_ge(s["znT_done"], 4)
                for g in range(GROUPS):
                    for k in range(KC):
                        last = nc.tensor.matmul(bank[4][:, g * P:(g + 1) * P], dwv[:, k, g * P:(g + 1) * P],
                                                znT[:, k, :, g * HG * SLOTS:(g + 1) * HG * SLOTS], start=(k == 0), stop=(k == KC - 1))
                last.then_inc(s["ao_done"], 1)
                pe.wait_ge(s["aoT_done"], 1)
                for g in range(GROUPS):
                    last = nc.tensor.matmul(bank[5][0:ROWS, :], aoT[:, g, :, :], dwo[:, g, :], start=(g == 0), stop=(g == GROUPS - 1))
                last.then_inc(s["wo_done"], 1)
                pe.wait_ge(s["o_step"], 4)
                for k in range(KC):
                    last = nc.tensor.transpose(bank[6][:, k * ROWS:(k + 1) * ROWS], h[:].rearrange("r (p k) -> r k p", k=KC)[:, k, :],
                                               hold["ident"][0:ROWS, 0:ROWS])
                last.then_inc(s["h_turned"], 1)
                experts(pe, lambda e, u: expert(pe, e, u))
                pe.wait_ge(s["y4_done"], 1)
                nc.tensor.matmul(bank[4][0:ROWS, :], fold[:], y4[:], start=True, stop=True).then_inc(s["fold_done"], 1)
                pe.wait_ge(s["o_done"], 1)
                for k in range(KC):
                    last = nc.tensor.transpose(bank[5][:, k * ROWS:(k + 1) * ROWS], o[:, k * P:(k + 1) * P], hold["ident"][0:ROWS, 0:ROWS])
                last.then_inc(s["o_turned"], 1)
                pe.wait_ge(s["comb_w_in"], 8 * 16)
                pe.wait_ge(s["oT_done"], 1)
                for w, bk, sem in ((cwk, bank[6], s["k_done"]), (cwv, bank[7], s["v_done"])):
                    for g in range(GROUPS):
                        for k in range(KC):
                            last = nc.tensor.matmul(bk[:, g * ROWS:(g + 1) * ROWS], w[:, k, g * P:(g + 1) * P], oT[:, k, :],
                                                    start=(k == 0), stop=(k == KC - 1))
                    last.then_inc(sem, 1)
                pe.wait_ge(s["kbd_done"], 1)
                for k in range(KC):
                    for g in range(GROUPS):
                        last = nc.tensor.matmul(bank[k][:, g * P:(g + 1) * P], cwqT[:, g, k * P:(k + 1) * P], kbd[:, g, :, :, :], start=True, stop=True)
                    last.then_inc(s["m2_done"], 1)
                pe.wait_ge(s["qb_done"], 1)
                for g in range(GROUPS):
                    last = nc.tensor.matmul(bank[6][:, g * P:(g + 1) * P], cbqb[:, g, :], kbd[:, g, :, :, :], start=True, stop=True)
                last.then_inc(s["kb_done"], 1)
                pe.wait_ge(s["vbd_done"], 1)
                half = HG * SLOTS
                for b in range(BATCH):
                    for m in range(SM):
                        out = bank[(4, 5, 7, 0)[b * SM + m]]
                        if b * SM + m == 3:
                            pe.wait_ge(s["m2_out"], 1)
                        for j in range(2):
                            last = nc.tensor.matmul(out[j * half:(j + 1) * half, :], vbd[:, 2 * m + j, b, :, :], cwo[:, 2 * m + j, :], start=True, stop=True)
                        last.then_inc(s["vo_done"], 1)

            @block.scalar
            def _(act):
                for i in range(BATCH * SM):
                    act.wait_ge(s["zn_turned"], i + 1)
                    nc.scalar.activation(znT[:, :, i // SM, (i % SM) * P:(i % SM + 1) * P], bank[i][:].rearrange("p (k r) -> p k r", k=KC),
                                         ACT.Copy).then_inc(s["znT_done"], 1)
                experts(act, lambda e, u: activate(act, e))
                for k in range(KC):
                    act.wait_ge(s["m2_done"], k + 1)
                    nc.scalar.activation(hold["m2"][:, :, k, :, :].rearrange("p b g r -> p g b r"),
                                         bank[k][:].rearrange("p (g b r) -> p g b r", g=GROUPS, b=BATCH), ACT.Copy).then_inc(s["m2_out"], 1)
                act.wait_ge(s["kb_done"], 1)
                nc.scalar.activation(hold["kb2"][:].rearrange("p b g r -> p g b r"), bank[6][:].rearrange("p (g b r) -> p g b r", g=GROUPS, b=BATCH),
                                     ACT.Copy, scale=SCALE).then_inc(s["m2_out"], 1)

            @block.vector
            def _(dve):
                nc.vector.reciprocal(rsum[:], hold["sum"][:]).then_inc(s["rsum_done"], 1)
                dve.wait_ge(s["rsum_done"], 1)
                for b in range(BATCH):
                    for m in range(SM):
                        nc.vector.tensor_scalar(hold["z"][:, b, m, :], hold["z"][:, b, m, :], rsum[:, b, m:m + 1], None, ALU.mult).then_inc(s["zn_done"], 1)
                dve.wait_ge(s["slot_w_in"], 3 * 16)
                dve.wait_ge(s["ao_done"], 1)
                for g in range(GROUPS):
                    for hh in range(HG):
                        r = slice(hh * HD, (hh + 1) * HD)
                        src = bank[4][r, g * P:(g + 1) * P].rearrange("p (b h q) -> p b h q", b=BATCH, h=HG)[:, :, hh, :]
                        last = nc.vector.tensor_scalar(aoT[r, g, :, :], src, dbv[r, g:g + 1], None, ALU.add)
                last.then_inc(s["aoT_done"], 1)
                dve.wait_ge(s["rows_in"], 9 * 16)
                nc.vector.tensor_tensor(slot[:], slot[:], dbo[:], ALU.add).then_inc(s["o_step"], 1)
                dve.wait_ge(s["o_step"], 1)
                dve.wait_ge(s["wo_done"], 1)
                nc.vector.tensor_tensor(o[:], bank[5][0:ROWS, :], slot[:], ALU.add).then_inc(s["o_step"], 1)
                dve.wait_ge(s["o_step"], 2)
                layernorm(nc, dve, s["ln_step"], 0, [o[:]], stats, [h[:]]).then_inc(s["ln_step"], 1)
                dve.wait_ge(s["ln_step"], LN_STEPS + 1)
                nc.vector.tensor_tensor(h[:], h[:], ln_g[:], ALU.mult).then_inc(s["o_step"], 1)
                dve.wait_ge(s["o_step"], 3)
                nc.vector.tensor_tensor(h[:], h[:], ln_b[:], ALU.add).then_inc(s["o_step"], 1)
                nc.vector.tensor_tensor(o[:], o[:], b2[:], ALU.add).then_inc(s["o_step"], 1)
                dve.wait_ge(s["h_turned"], 1)
                nc.vector.tensor_copy(hT[:].rearrange("p k r -> p (k r)"), bank[6][:, 0:KC * ROWS]).then_inc(s["hT_done"], 1)
                dve.wait_ge(s["hT_done"], 1)
                dve.wait_ge(s["consts"], 6)
                masked(dve, 0, 0)

                def step(e, u):
                    if not (isinstance(e, int) and e == EXPERTS - 1):
                        masked(dve, e + 1, 1 - u)
                    combine_up(dve, e)
                experts(dve, step)
                dve.wait_ge(unit_used[5], EXPERTS)
                nc.vector.tensor_copy(y4[:], bank[3][:]).then_inc(s["y4_done"], 1)
                dve.wait_ge(s["fold_done"], 1)
                dve.wait_ge(s["o_step"], 5)
                nc.vector.tensor_tensor(o[:], bank[4][0:ROWS, :], o[:], ALU.add).then_inc(s["o_done"], 1)
                dve.wait_ge(s["o_turned"], 1)
                nc.vector.tensor_copy(oT[:].rearrange("p k r -> p (k r)"), bank[5][:, 0:KC * ROWS]).then_inc(s["oT_done"], 1)
                dve.wait_ge(s["comb_w_in"], 8 * 16)
                dve.wait_ge(s["zeros"], 6)
                for src, dst, bias_, ready, done in ((bank[6], kbd, cbk, s["k_done"], s["kbd_done"]), (bank[7], vbd, cbv, s["v_done"], s["vbd_done"])):
                    dve.wait_ge(ready, 1)
                    for g in range(GROUPS):
                        for hh in range(HG):
                            r = slice(hh * HD, (hh + 1) * HD)
                            last = nc.vector.tensor_scalar(dst[r, g, :, hh, :], src[r, g * ROWS:(g + 1) * ROWS].rearrange("p (b q) -> p b q", b=BATCH),
                                                           bias_[r, g:g + 1], None, ALU.add)
                    last.then_inc(done, 1)
                for i in range(BATCH * SM):
                    dve.wait_ge(s["vo_done"], i + 1)
                    nc.vector.scalar_tensor_tensor(hold["vo"][:, i // SM, i % SM, :], cbo[:], 1.0 / HEADS, bank[(4, 5, 7, 0)[i]][:],
                                                   ALU.mult, ALU.add).then_inc(s["vo_out"], 1)


def combine_stage(nc, io, hold):
    with Stage(nc, "cmb") as st:
        T2 = 2
        STEPS = TILES // T2
        PER_SEQ = STEPS // BATCH
        x2T = [st.sb(f"x2T{i}", [P, T2, KC, P]) for i in range(2)]
        x2 = [st.sb(f"x2_{i}", [P, T2, D]) for i in range(2)]
        sc = [st.sb(f"sc{i}", [P, T2, SROWS]) for i in range(2)]
        pr = [st.sb(f"pr{i}", [P, T2, SROWS]) for i in range(2)]
        top = [st.sb(f"top{i}", [P, T2 * HEADS]) for i in range(2)]
        den = st.sb("den", [P, T2 * HEADS])
        rden = [st.sb(f"rden{i}", [P, T2 * HEADS]) for i in range(2)]
        prT = [st.sb(f"prT{i}", [P, T2, SM, P]) for i in range(2)]
        xr = [st.sb(f"xr{i}", [P, T2, D]) for i in range(2)]
        stats = [st.sb(f"stats{i}", [P, T2, 12]) for i in range(2)]
        out = [st.sb(f"out{i}", [P, T2, D]) for i in range(2)]
        bank = st.banks()
        s = st.sems("sc_done", "sc_out", "top_done", "shifted", "exp_done", "den_done", "rden_done", "normed", "pr_turned", "prT_done",
                    "o_done", "res_done", "ln_step", "stats_done", "out_done")
        x2T_in, x2_in, stored = st.pair("x2T_in"), st.pair("x2_in"), st.pair("stored")
        LAST = STEPS - 1
        x2T_v = io["x2T"].rearrange("(t p) n -> p t n", p=P)
        x2_v = io["x2"].rearrange("(t p) n -> p t n", p=P)
        out_v = io["out"].rearrange("(t p) n -> p t n", p=P)

        def load_turned(sp, i, u):
            wait_later(sp, s["sc_done"], i - 1)
            sp.dma_start(x2T[u][:].rearrange("p t k n -> p t (k n)"), x2T_v[:, bass.ds(i * T2, T2), :]).then_inc(x2T_in[u], 16)

        def load_tokens(sp, i, u):
            wait_later(sp, s["res_done"], i - 1)
            sp.dma_start(x2[u][:], x2_v[:, bass.ds(i * T2, T2), :]).then_inc(x2_in[u], 16)

        def store(sp, i, u):
            sp.wait_ge(s["out_done"], i + 1)
            sp.dma_start(out_v[:, bass.ds(i * T2, T2), :], out[u][:]).then_inc(stored[u], 16)

        def score(pe, i, u, half, b):
            pe.wait_ge(x2T_in[u], 16 * (half + 1))
            wait_later(pe, s["sc_out"], i - 1)
            for j in range(T2):
                for k in range(KC):
                    last = nc.tensor.matmul(bank[u][:, j * SROWS:(j + 1) * SROWS], x2T[u][:, j, k, :], hold["m2"][:, b, k, :, :],
                                            start=(k == 0), stop=(k == KC - 1))
            last.then_inc(s["sc_done"], 1)

        def turn(pe, i, u):
            pe.wait_ge(s["normed"], i + 1)
            wait_later(pe, s["prT_done"], i - 1)
            for j in range(T2):
                for m in range(SM):
                    at = (j * SM + m) * P
                    last = nc.tensor.transpose(bank[2 + u][:, at:at + P], pr[u][:, j, m * P:(m + 1) * P], hold["ident"][:])
            last.then_inc(s["pr_turned"], 1)

        def project_out(pe, i, u, b):
            pe.wait_ge(s["prT_done"], i + 1)
            wait_later(pe, s["res_done"], i - 1)
            for j in range(T2):
                for m in range(SM):
                    last = nc.tensor.matmul(bank[4 + 2 * u + j][:], prT[u][:, j, m, :], hold["vo"][:, b, m, :], start=(m == 0), stop=(m == SM - 1))
                last.then_inc(s["o_done"], 1)

        def take_scores(dve, i, u, b):
            dve.wait_ge(s["sc_done"], i + 1)
            wait_later(dve, s["shifted"], i - 1)
            nc.vector.scalar_tensor_tensor(sc[u][:], bank[u][:].rearrange("p (t r) -> p t r", t=T2), SCALE,
                                           broadcast(hold["kb2"][:, b, :, :].rearrange("p g r -> p (g r)").unsqueeze(1), [P, T2, SROWS]),
                                           ALU.mult, ALU.add).then_inc(s["sc_out"], 1)
            dve.wait_ge(s["sc_out"], i + 1)
            nc.vector.tensor_reduce(top[u][:], sc[u][:].rearrange("p t (h q) -> p (t h) q", q=SLOTS), AX.X, ALU.max).then_inc(s["top_done"], 1)

        def denominators(dve, i, u):
            dve.wait_ge(s["exp_done"], i + 1)
            nc.vector.tensor_reduce(den[:], pr[u][:].rearrange("p t (h q) -> p (t h) q", q=SLOTS), AX.X, ALU.add).then_inc(s["den_done"], 1)
            dve.wait_ge(s["den_done"], i + 1)
            wait_later(dve, s["normed"], i - 1)
            nc.vector.reciprocal(rden[u][:], den[:]).then_inc(s["rden_done"], 1)

        def residual(dve, i, u, half):
            dve.wait_ge(x2_in[u], 16 * (half + 1))
            wait_later(dve, s["out_done"], i - 1)
            for j in range(T2):
                dve.wait_ge(s["o_done"], T2 * i + j + 1)
                last = nc.vector.tensor_tensor(xr[u][:, j, :], bank[4 + 2 * u + j][:], x2[u][:, j, :], ALU.add)
            last.then_inc(s["res_done"], 1)
            dve.wait_ge(s["res_done"], i + 1)
            norm_factors(nc, dve, s["ln_step"], LN_STEPS * i, [xr[u][:, j, :] for j in range(T2)], stats[u])
            nc.vector.scalar_tensor_tensor(stats[u][:, :, 11:12], stats[u][:, :, 6:7], -1.0, stats[u][:, :, 9:10], ALU.mult, ALU.mult).then_inc(s["stats_done"], 1)

        def exponents(act, i, u):
            act.wait_ge(s["shifted"], i + 1)
            nc.scalar.activation(pr[u][:], pr[u][:], ACT.Exp).then_inc(s["exp_done"], 1)

        def take_turned(act, i, u):
            act.wait_ge(s["pr_turned"], i + 1)
            wait_later(act, s["o_done"], T2 * (i - 1))
            nc.scalar.activation(prT[u][:].rearrange("p t m r -> p (t m r)"), bank[2 + u][:], ACT.Copy).then_inc(s["prT_done"], 1)

        def normalise(act, i, u, half):
            act.wait_ge(s["stats_done"], i + 1)
            wait_later(act, stored[u], 16 * half)
            for j in range(T2):
                last = nc.scalar.activation(out[u][:, j, :], xr[u][:, j, :], ACT.Identity, bias=stats[u][:, j, 11:12], scale=stats[u][:, j, 9:10])
            last.then_inc(s["out_done"], 1)

        def softmax_shift(pool, i, u):
            pool.wait_ge(s["top_done"], i + 1)
            wait_later(pool, s["pr_turned"], i - 1)
            nc.gpsimd.tensor_tensor(pr[u][:].rearrange("p t (h q) -> p (t h) q", q=SLOTS), sc[u][:].rearrange("p t (h q) -> p (t h) q", q=SLOTS),
                                    broadcast(top[u][:].unsqueeze(2), [P, T2 * HEADS, SLOTS]), ALU.subtract).then_inc(s["shifted"], 1)

        def softmax_norm(pool, i, u):
            pool.wait_ge(s["rden_done"], i + 1)
            nc.gpsimd.tensor_tensor(pr[u][:].rearrange("p t (h q) -> p (t h) q", q=SLOTS), pr[u][:].rearrange("p t (h q) -> p (t h) q", q=SLOTS),
                                    broadcast(rden[u][:].unsqueeze(2), [P, T2 * HEADS, SLOTS]), ALU.mult).then_inc(s["normed"], 1)

        def steps(eng, body):
            def alone(*ts):
                for i in ts:
                    body(i, i % 2, i // 2, lambda d, i=i: (i + d) // PER_SEQ)

            def loop(first, end, b):
                with eng.Fori(first // 2, end // 2) as p:
                    for u in (0, 1):
                        body(2 * p + u, u, p, lambda d: b)
            alone(0, 1)
            loop(2, PER_SEQ - 2, 0)
            alone(PER_SEQ - 2, PER_SEQ - 1)
            loop(PER_SEQ, STEPS - 4, 1)
            alone(*range(STEPS - 4, STEPS))

        def before(i, n):
            return not isinstance(i, int) or i >= n

        def ahead(i, n):
            return not isinstance(i, int) or i + n <= LAST

        with nc.Block() as block:
            @block.sync
            def _(sp):
                load_turned(sp, 0, 0)
                load_turned(sp, 1, 1)
                load_tokens(sp, 0, 0)
                load_turned(sp, 2, 0)

                def step(i, u, half, seq):
                    if ahead(i, 3):
                        load_turned(sp, i + 3, 1 - u)
                    if ahead(i, 1):
                        load_tokens(sp, i + 1, 1 - u)
                    if before(i, 1):
                        store(sp, i - 1, 1 - u)
                steps(sp, step)
                store(sp, LAST, 1)
                for u in range(2):
                    sp.wait_ge(stored[u], 16 * STEPS // 2)

            @block.tensor
            def _(pe):
                score(pe, 0, 0, 0, 0)
                score(pe, 1, 1, 0, 0)
                turn(pe, 0, 0)

                def step(i, u, half, seq):
                    if ahead(i, 2):
                        score(pe, i + 2, u, half + 1, seq(2))
                    project_out(pe, i, u, seq(0))
                    if ahead(i, 1):
                        turn(pe, i + 1, 1 - u)
                steps(pe, step)

            @block.scalar
            def _(act):
                exponents(act, 0, 0)
                exponents(act, 1, 1)
                take_turned(act, 0, 0)

                def step(i, u, half, seq):
                    if ahead(i, 2):
                        exponents(act, i + 2, u)
                    if ahead(i, 1):
                        take_turned(act, i + 1, 1 - u)
                    normalise(act, i, u, half)
                steps(act, step)

            @block.vector
            def _(dve):
                for i in (0, 1):
                    take_scores(dve, i, i, 0)
                    denominators(dve, i, i)

                def step(i, u, half, seq):
                    if ahead(i, 2):
                        take_scores(dve, i + 2, u, seq(2))
                    residual(dve, i, u, half)
                    if ahead(i, 2):
                        denominators(dve, i + 2, u)
                steps(dve, step)

            @block.gpsimd
            def _(pool):
                for i in (0, 1):
                    softmax_shift(pool, i, i)
                    softmax_norm(pool, i, i)

                def step(i, u, half, seq):
                    if ahead(i, 2):
                        softmax_shift(pool, i + 2, u)
                        softmax_norm(pool, i + 2, u)
                steps(pool, step)


def decoder_layer(nc, io):
    with Stage(nc, "all") as keep:
        ring = keep.sb("ring", [P, UNITS, UNIT])
        ring_in = [nc.alloc_semaphore(f"ring_in{i}") for i in range(UNITS)]
        hold = dict(
            arena=ring[:].rearrange("p u n -> p (u n)"),
            ident=keep.sb("ident", [P, P]),
            tri=keep.sb("tri", [P, P]),
            decay=keep.sb("decay", [P, CHUNKS, HEADS]),
            rate=keep.sb("rate", [P, BATCH, CHUNKS, HEADS]),
            kbias=keep.sb("kbias", [P, SM]),
            top=keep.sb("top", [P, BATCH, SM]),
            sum=keep.sb("sum", [P, BATCH, SM]),
            z=keep.sb("z", [P, BATCH, SM, D]),
        )
        with Stage(nc, "att") as att:
            hold["mask"] = att.sb("mask", [P, CTX])
            hold["kbd"] = att.sb("kbd", [P, BATCH, GROUPS, HG, CTX])
            hold["vbd"] = att.sb("vbd", [PIECE, BATCH, 3, GROUPS, P])
            hold["m1"] = att.sb("m1", [P, KC, SROWS])
            with Stage(nc, "mxw") as mxw:
                hold["win"] = mxw.sb("win", [P, KC, CONV])
                hold["wout"] = mxw.sb("wout", [P, KC, D])
                hold["taps"] = mxw.sb("taps", [P, CT, TAPS])
                hold["convb"] = mxw.sb("convb", [P, CT])
                hold["mixer_in"] = mxw.sem("mixer_in")
                tables_stage(nc, io, hold)
                mixer_stage(nc, io, hold)
            cross_stage(nc, io, hold, ring, ring_in)
        with Stage(nc, "slt") as slt:
            hold["m2"] = slt.sb("m2", [P, BATCH, KC, GROUPS, HG * SLOTS])
            hold["kb2"] = slt.sb("kb2", [P, BATCH, GROUPS, HG * SLOTS])
            hold["vo"] = slt.sb("vo", [P, BATCH, SM, D])
            experts_stage(nc, io, hold, ring, ring_in)
            combine_stage(nc, io, hold)


INPUTS = {"conv_w": "L0_attn_conv_w", "conv_b": "L0_attn_conv_b", "A_param": "L0_attn_A_param", "dt_bias": "L0_attn_dt_bias",
          "q_w": "L0_xattn_q_w", "q_b": "L0_xattn_q_b", "k_w": "L0_xattn_k_w", "k_b": "L0_xattn_k_b", "v_w": "L0_xattn_v_w",
          "v_b": "L0_xattn_v_b", "o_w": "L0_xattn_o_w", "o_b": "L0_xattn_o_b"}
for _n in ("d_Wq", "d_Wv", "d_Wo", "d_bq", "d_bk", "d_bv", "d_bo", "c_Wk", "c_Wv", "c_Wo", "c_bq", "c_bk", "c_bv", "c_bo",
           "e_ln_g", "e_ln_b", "e_W1", "e_b1", "e_Wg", "e_bg", "e_W2", "e_b2"):
    INPUTS[_n] = "L0_ffn_" + _n


def kernel(**inputs):
    import concourse.bacc as bacc
    import numpy as np
    from concourse.bass_utils import run_bass_kernel_spmd

    x = np.asarray(inputs["x"]).reshape(TOKENS, D)
    arrays = {name: np.ascontiguousarray(inputs[of]) for name, of in INPUTS.items()}
    arrays["x"] = np.ascontiguousarray(x)
    arrays["xT"] = np.ascontiguousarray(x.T)
    arrays["ctxT"] = np.ascontiguousarray(np.asarray(inputs["ctx_1024"]).reshape(BATCH * CTX, D).T)
    arrays["WinT"] = np.ascontiguousarray(np.asarray(inputs["L0_attn_W_in"]).T)
    arrays["WoutT"] = np.ascontiguousarray(np.asarray(inputs["L0_attn_W_out"]).T)
    slot = np.asarray(inputs["L0_ffn_slot_query"]).reshape(SLOTS, D)
    arrays["slot"] = np.ascontiguousarray(slot)
    arrays["slotT"] = np.ascontiguousarray(slot.T)
    arrays["d_WkT"] = np.ascontiguousarray(np.asarray(inputs["L0_ffn_d_Wk"]).T)
    arrays["c_WqT"] = np.ascontiguousarray(np.asarray(inputs["L0_ffn_c_Wq"]).T)

    arrays["conv_w"] = np.ascontiguousarray(arrays["conv_w"].reshape(CT, P, TAPS).transpose(1, 0, 2))
    for name in ("conv_b", "q_b", "k_b", "d_bq", "d_bk", "d_bv", "c_bq", "c_bk", "c_bv"):
        arrays[name] = np.ascontiguousarray(arrays[name].reshape(-1, P).T)

    nc = bacc.Bacc("TRN2", target_bir_lowering=False, num_devices=1)
    io = {name: nc.dram_tensor(f"in_{name}", a.shape, F32, kind="ExternalInput").ap() for name, a in arrays.items()}
    io["out"] = nc.dram_tensor("out", [TOKENS, D], F32, kind="ExternalOutput").ap()
    io["x1"] = nc.dram_tensor("scratch_x1", [TOKENS, D], F32).ap()
    io["x2"] = nc.dram_tensor("scratch_x2", [TOKENS, D], F32).ap()
    io["x2T"] = nc.dram_tensor("scratch_x2T", [TOKENS, D], F32).ap()
    decoder_layer(nc, io)
    got = run_bass_kernel_spmd(nc, [{f"in_{name}": a for name, a in arrays.items()}], core_ids=[0])
    return got.results[0]["out"].reshape(BATCH, SEQ, D)
```

```python
from contextlib import ExitStack

import concourse.bass as bass
import concourse.mybir as mybir

F32 = mybir.dt.float32
ALU = mybir.AluOpType
ACT = mybir.ActivationFunctionType
AX = mybir.AxisListType

P = 128
BATCH, SEQ, D = 2, 2048, 512
TOKENS = BATCH * SEQ
TILES = TOKENS // P
CHUNKS = SEQ // P
KC = D // P
HEADS = 16
HD = D // HEADS
HG = P // HD
GROUPS = HEADS // HG
TAPS = 4
HALO = TAPS - 1
CONV = 3 * D
CT = CONV // P
CTX = 77
SLOTS = 16
SROWS = HEADS * SLOTS
SM = SROWS // P
EXPERTS = 16
F = 2048
EPS = 1e-5
SCALE = float(HD) ** -0.5
NEG = -3.0e38
KROWS = HG * CTX
PIECE = -(-KROWS // 3)
PIECES = [min(PIECE, KROWS - i * PIECE) for i in range(3)]
UNIT = 4096
UNITS = 6
FQ = F // 4


def broadcast(ap, shape):
    return ap.broadcast_to(shape)


RESERVED = UNITS * UNIT - 2 * CT * P


class Stage:

    def __init__(self, nc, tag, arena=None):
        self.nc, self.tag, self.stack, self.arena, self.used, self.taken = nc, tag, ExitStack(), arena, 0, []

    def __enter__(self):
        return self

    def __exit__(self, *a):
        if self.taken and a[0] is None:
            self.nc.clear_and_free_semaphores(self.taken)
            self.nc.all_engine_barrier()
        return self.stack.__exit__(*a)

    def sb(self, name, shape):
        size = 1
        for n in shape[1:]:
            size *= n
        if self.arena is not None and self.used + size <= RESERVED:
            flat = self.arena[0:shape[0], self.used:self.used + size]
            self.used += size
            return shaped(flat, shape)
        return self.stack.enter_context(self.nc.sbuf_tensor(f"{self.tag}_{name}", shape, F32))

    def banks(self, n=8):
        return [self.stack.enter_context(self.nc.psum_tensor(f"{self.tag}_bank{i}", [P, 512], F32)) for i in range(n)]

    def sem(self, name):
        self.taken.append(self.nc.alloc_semaphore(f"{self.tag}_{name}"))
        return self.taken[-1]

    def sems(self, *names):
        return {n: self.sem(n) for n in names}

    def pair(self, name):
        return [self.sem(f"{name}{i}") for i in range(2)]


def shaped(flat, shape):
    names = "abcd"[:len(shape) - 1]
    dims = dict(zip(names, shape[1:]))
    return flat.rearrange(f"p ({' '.join(names)}) -> p {' '.join(names)}", **dims)


def wait_later(eng, sem, value):
    if not isinstance(value, int) or value > 0:
        eng.wait_ge(sem, value)


def mixer_weights(sp, io, hold, sem):
    for dst, src in ((hold["win"], io["WinT"][:, 0:CONV].rearrange("(k p) n -> p k n", p=P)), (hold["taps"], io["conv_w"]),
                     (hold["convb"], io["conv_b"]), (hold["wout"], io["WoutT"].rearrange("(k p) n -> p k n", p=P))):
        sp.dma_start(dst[:], src).then_inc(sem, 16)


MIXER_WEIGHTS = 4 * 16
MIXER_SEMS = ("zeros", "proj_done", "proj_out", "halo_done", "convC", "convB", "convX", "conv_tap", "conv_tapX",
              "cbd_done", "b_turned", "btok_done", "x_turned", "xs_done", "scores_done", "scores_masked", "state_done",
              "state_added", "y_done", "rate_done", "rate_turned", "rateT_done", "yT_done", "out_done", "res_done",
              "ln_step", "x1_done")


def project_group(nc, hold, grp, xT, bank):
    for m in range(4):
        for k in range(KC):
            last = nc.tensor.matmul(bank[:, m * P:(m + 1) * P], hold["win"][:, k, (grp * 4 + m) * P:(grp * 4 + m + 1) * P],
                                    xT[:, k, :], start=(k == 0), stop=(k == KC - 1))
    last.then_inc(hold["mix"]["proj_done"], 1)


def take_projection(nc, act, hold, c, u, grp, bank):
    s = hold["mix"]
    act.wait_ge(s["proj_done"], 3 * c + grp + 1)
    if grp == 0:
        wait_later(act, s["halo_done"], c - 1)
        wait_later(act, s["convB"], c - 1)
        wait_later(act, s["convX"], c - 1)
    nc.scalar.activation(hold["proj"][u][:, grp * 4:grp * 4 + 4, HALO:], bank[:].rearrange("p (m t) -> p m t", m=4), ACT.Copy).then_inc(s["proj_out"], 1)


def pass_halo(nc, act, hold, c, u):
    s, proj = hold["mix"], hold["proj"]
    act.wait_ge(s["proj_out"], 3 * c + 3)
    wait_later(act, s["convB"], c)
    wait_later(act, s["convX"], c)
    nc.scalar.activation(proj[1 - u][:, :, 0:HALO], proj[u][:, :, P:P + HALO], ACT.Copy).then_inc(s["halo_done"], 1)


def convolve(nc, dve, hold, c, u):
    s, proj, conv, taps, convb = hold["mix"], hold["proj"], hold["conv"], hold["taps"], hold["convb"]
    dve.wait_ge(s["proj_out"], 3 * c + 3)
    wait_later(dve, s["halo_done"], c)
    wait_later(dve, s["y_done"], c - 1)
    for m0, done, first in ((0, s["convC"], 0), (4, s["convB"], 3)):
        for k in range(TAPS):
            if k:
                dve.wait_ge(s["conv_tap"], 6 * c + first + k)
            for m in range(m0, m0 + 4):
                src = proj[u][:, m, k:k + P]
                if k == 0:
                    last = nc.vector.tensor_scalar(conv[u][:, m, :], src, taps[:, m, 0:1], convb[:, m:m + 1], ALU.mult, ALU.add)
                else:
                    last = nc.vector.scalar_tensor_tensor(conv[u][:, m, :], src, taps[:, m, k:k + 1], conv[u][:, m, :], ALU.mult, ALU.add)
            last.then_inc(s["conv_tap"] if k < TAPS - 1 else done, 1)


def convolve_x(nc, pool, hold, c, u):
    s, proj, conv, taps, convb, product = hold["mix"], hold["proj"], hold["conv"], hold["taps"], hold["convb"], hold["product"]
    pool.wait_ge(s["proj_out"], 3 * c + 3)
    wait_later(pool, s["halo_done"], c)
    wait_later(pool, s["x_turned"], c - 1)
    for k in range(TAPS):
        nc.gpsimd.tensor_tensor(product[k % 2][:], proj[u][:, 8:12, k:k + P], broadcast(taps[:, 8:12, k:k + 1], [P, 4, P]),
                                ALU.mult).then_inc(s["conv_tapX"], 1)
        pool.wait_ge(s["conv_tapX"], 7 * c + 2 * k + 1)
        so_far = conv[u][:, 8:12, :] if k else broadcast(convb[:, 8:12].unsqueeze(2), [P, 4, P])
        last = nc.gpsimd.tensor_tensor(conv[u][:, 8:12, :], so_far, product[k % 2][:], ALU.add)
        if k < TAPS - 1:
            last.then_inc(s["conv_tapX"], 1)
        else:
            last.then_inc(s["convX"], 1)


def tables_stage(nc, io, hold):
    with Stage(nc, "tab", hold["arena"]) as st:
        wdt = st.sb("wdt", [P, KC, HD])
        xblk = [st.sb(f"xblk{i}", [P, KC, 512]) for i in range(3)]
        bias = st.sb("bias", [P, 1])
        apar = st.sb("apar", [P, 1])
        zabs = st.sb("zabs", [P, BATCH, 512])
        zrelu = st.sb("zrelu", [P, BATCH, 512])
        zexp = zln = zabs
        arow = zrelu
        atok = st.sb("atok", [P, BATCH, CHUNKS, HEADS])
        carry = st.sb("carry", [P, BATCH, CHUNKS, HEADS])
        carry2 = st.sb("carry2", [P, BATCH, CHUNKS, HEADS])
        cum = st.sb("cum", [P, BATCH, CHUNKS, HEADS])
        neg = st.sb("neg", [P, BATCH, CHUNKS, HEADS])
        pos = st.sb("pos", [P, BATCH, CHUNKS, HEADS])
        cume = st.sb("cume", [P, BATCH, CHUNKS, HEADS])
        norm = st.sb("norm", [P, BATCH, CHUNKS, HEADS])
        rnorm = st.sb("rnorm", [P, BATCH, CHUNKS, HEADS])
        tri = st.sb("tri", [P, P])
        ones = st.sb("ones", [P, P])
        xT01 = st.sb("xT01", [P, KC, 2 * P])
        wk = st.sb("wk", [P, KC, D])
        wv = st.sb("wv", [P, KC, D])
        wq, wkT = hold["q_w"], hold["o_w"]
        ctxT = st.sb("ctxT", [P, KC, BATCH * CTX])
        kb = st.sb("kb", [P, GROUPS])
        qb = st.sb("qb", [P, GROUPS])
        bk = st.sb("bk", [P, GROUPS])
        vb = st.sb("vb", [CTX, D])
        vtok = st.sb("vtok", [CTX, BATCH, D])
        slotT = st.sb("slotT", [P, KC, SLOTS])
        sqbd = st.sb("sqbd", [P, GROUPS, HG, SLOTS])
        bank = st.banks()
        PROJ01 = ((bank[6], bank[7], bank[4]), (bank[5], bank[6], bank[7]))
        M1, KBIAS = (bank[0], bank[1], bank[3], bank[4]), bank[5]
        s = st.sems("consts", "zeros", "small", "wdt_in", "ctx_in", "kw_in", "vw_in", "qw_in", "kT_in", "blk_used",
                    "dt_ready", "softplus", "dt_steps", "a_ready", "a_turned", "atok_ready", "cum_ready", "exp_ready",
                    "sums1", "sums2", "carry_steps", "norm_steps", "tables_ready", "tables_done", "k_ready", "v_ready", "vtok_ready", "xT01_in", "halo_zeros",
                    "vbd_in", "q_ready", "sq_ready", "m1_ready", "kbias_ready", "kbd_done", "m1_done")
        blk_in = [st.sem(f"blk_in{i}") for i in range(3)]
        QB = SEQ // 512

        def small_loads(act):
            act.wait_ge(s["zeros"], 3)
            for q in range(QB):
                act.dma_start(bias[HD * q:HD * q + HEADS, :], io["dt_bias"].rearrange("(h o) -> h o", o=1)).then_inc(s["small"], 16)
                act.dma_start(apar[HD * q:HD * q + HEADS, :], io["A_param"].rearrange("(h o) -> h o", o=1)).then_inc(s["small"], 16)
        SMALL_AP = 2 * QB * 16

        with nc.Block() as block:
            @block.sync
            def _(sp):
                def block_in(i):
                    sp.dma_start(xblk[i % 3][:], io["xT"][:, i * 512:(i + 1) * 512].rearrange("(k p) n -> p k n", p=P)).then_inc(blk_in[i % 3], 16)

                block_in(0)
                sp.wait_ge(s["zeros"], 1)
                sp.dma_start(wdt[:, :, 0:HEADS], io["WinT"][:, CONV:].rearrange("(k p) n -> p k n", p=P)).then_inc(s["wdt_in"], 16)
                def weights_in(dst, src, sem):
                    sp.dma_start(dst[:], src.rearrange("(k p) n -> p k n", p=P)).then_inc(sem, 16)

                for i in range(1, BATCH * QB):
                    if i >= 3:
                        sp.wait_ge(s["blk_used"], i - 2)
                    block_in(i)
                    if i == QB + 1:
                        weights_in(wk, io["k_w"], s["kw_in"])
                        sp.dma_start(ctxT[:], io["ctxT"].rearrange("(k p) n -> p k n", p=P)).then_inc(s["ctx_in"], 16)
                        sp.dma_start(slotT[:], io["slotT"].rearrange("(k p) n -> p k n", p=P)).then_inc(s["ctx_in"], 16)
                        sp.dma_start(vb[:], broadcast(io["v_b"].rearrange("(o n) -> o n", o=1), [CTX, D])).then_inc(s["ctx_in"], 16)
                        for dst, src in ((kb, io["k_b"]), (qb, io["d_bq"]), (bk, io["d_bk"])):
                            sp.dma_start(dst[:], src).then_inc(s["ctx_in"], 16)
                        weights_in(wv, io["v_w"], s["vw_in"])
                weights_in(xT01, io["xT"][:, 0:2 * P], s["xT01_in"])
                mixer_weights(sp, io, hold, hold["mixer_in"])
                weights_in(wq, io["d_Wq"], s["qw_in"])
                weights_in(wkT, io["d_WkT"], s["kT_in"])
                sp.wait_ge(s["vtok_ready"], BATCH)
                n = 0
                for b in range(BATCH):
                    for h in range(HG):
                        r = h * CTX
                        while r < (h + 1) * CTX:
                            piece = r // PIECE
                            end = min((h + 1) * CTX, (piece + 1) * PIECE)
                            src = vtok[r - h * CTX:end - h * CTX, b, :].rearrange("s (g h p) -> s g h p", g=GROUPS, h=HG)[:, :, h, :]
                            sp.dma_start(hold["vbd"][r - piece * PIECE:end - piece * PIECE, b, piece, :, h * HD:(h + 1) * HD], src).then_inc(s["vbd_in"], 16)
                            n += 1
                            r = end
                sp.wait_ge(s["vbd_in"], 16 * n)

            @block.gpsimd
            def _(pool):
                nc.gpsimd.memset(wdt[:], 0.0).then_inc(s["zeros"], 1)
                nc.gpsimd.memset(bias[:], 0.0).then_inc(s["zeros"], 1)
                nc.gpsimd.memset(apar[:], 0.0).then_inc(s["zeros"], 1)
                nc.gpsimd.memset(hold["ident"][:], 0.0).then_inc(s["zeros"], 1)
                nc.gpsimd.memset(tri[:], 1.0).then_inc(s["zeros"], 1)
                nc.gpsimd.memset(ones[:], 1.0).then_inc(s["zeros"], 1)
                nc.gpsimd.memset(hold["mask"][:], 0.0).then_inc(s["zeros"], 1)
                pool.wait_ge(s["zeros"], 7)
                nc.gpsimd.affine_select(out=hold["ident"][:], in_=hold["ident"][:], compare_op=ALU.not_equal, fill=1.0, base=0,
                                        pattern=[[-1, P]], channel_multiplier=1).then_inc(s["consts"], 1)
                nc.gpsimd.affine_select(out=tri[:], in_=tri[:], compare_op=ALU.is_ge, fill=0.0, base=0,
                                        pattern=[[1, P]], channel_multiplier=-1).then_inc(s["consts"], 1)
                nc.gpsimd.affine_select(out=hold["mask"][:], in_=hold["mask"][:], compare_op=ALU.is_ge, fill=NEG, base=0,
                                        pattern=[[-1, CTX]], channel_multiplier=1).then_inc(s["consts"], 1)
                nc.gpsimd.memset(hold["vbd"][:], 0.0).then_inc(s["zeros"], 1)
                nc.gpsimd.memset(hold["kbd"][:], 0.0).then_inc(s["zeros"], 1)
                nc.gpsimd.memset(sqbd[:], 0.0).then_inc(s["zeros"], 1)
                nc.gpsimd.memset(hold["proj"][0][:, :, 0:HALO], 0.0).then_inc(s["halo_zeros"], 1)
                pool.wait_ge(s["consts"], 2)
                nc.gpsimd.tensor_copy(hold["tri"][:], tri[:]).then_inc(s["consts"], 1)
                pool.wait_ge(hold["mixer_in"], MIXER_WEIGHTS)
                pool.wait_ge(s["halo_zeros"], 1)
                convolve_x(nc, pool, hold, 0, 0)

            @block.tensor
            def _(pe):
                pe.wait_ge(s["wdt_in"], 16)
                def step_sizes(b, qs):
                    for q in qs:
                        i = b * QB + q
                        pe.wait_ge(blk_in[i % 3], 16 * (i // 3 + 1))
                        for k in range(KC):
                            last = nc.tensor.matmul(bank[b][HD * q:HD * (q + 1), :], wdt[:, k, :], xblk[i % 3][:, k, :],
                                                    start=(k == 0), stop=(k == KC - 1))
                        last.then_inc(s["blk_used"], 1)

                step_sizes(0, range(QB))
                step_sizes(1, range(2))
                pe.wait_ge(s["ctx_in"], 6 * 16)
                pe.wait_ge(s["kw_in"], 16)
                for g in range(GROUPS):
                    for k in range(KC):
                        last = nc.tensor.matmul(bank[2 + g // 2][:, (g % 2) * 256:(g % 2) * 256 + BATCH * CTX], wk[:, k, g * P:(g + 1) * P],
                                                ctxT[:, k, :], start=(k == 0), stop=(k == KC - 1))
                last.then_inc(s["k_ready"], 1)
                step_sizes(1, range(2, QB))
                pe.wait_ge(s["vw_in"], 16)
                for b in range(BATCH):
                    for k in range(KC):
                        last = nc.tensor.matmul(bank[4 + b][0:CTX, :], ctxT[:, k, b * CTX:(b + 1) * CTX], wv[:, k, :],
                                                start=(k == 0), stop=(k == KC - 1))
                    last.then_inc(s["v_ready"], 1)
                def turn_steps(b):
                    pe.wait_ge(s["a_ready"], b + 1)
                    for sub in range(4):
                        last = nc.tensor.transpose(bank[6 + b][:, sub * P:(sub + 1) * P], arow[:, b, sub * P:(sub + 1) * P], hold["ident"][:])
                    last.then_inc(s["a_turned"], 1)

                def project(c, grp, to):
                    project_group(nc, hold, grp, xT01[:, :, c * P:(c + 1) * P], to)

                pe.wait_ge(s["consts"], 2)
                turn_steps(0)
                turn_steps(1)
                pe.wait_ge(s["atok_ready"], BATCH)
                nc.tensor.matmul(bank[0][:], tri[:], atok[:], start=True, stop=True)
                nc.tensor.matmul(bank[1][:], ones[:], atok[:], start=True, stop=True).then_inc(s["sums1"], 1)
                pe.wait_ge(hold["mixer_in"], MIXER_WEIGHTS)
                pe.wait_ge(s["xT01_in"], 16)
                project(0, 0, PROJ01[0][0])
                pe.wait_ge(s["exp_ready"], 1)
                pe.wait_ge(s["cum_ready"], 1)
                nc.tensor.matmul(bank[0][:], tri[:], neg[:], start=True, stop=True)
                nc.tensor.matmul(bank[1][:], ones[:], neg[:], start=True, stop=True).then_inc(s["sums2"], 1)
                project(0, 1, PROJ01[0][1])
                pe.wait_ge(s["vtok_ready"], BATCH)
                project(0, 2, PROJ01[0][2])
                pe.wait_ge(s["qw_in"], 16)
                pe.wait_ge(s["kbd_done"], 1)
                for g in range(GROUPS):
                    for k in range(KC):
                        last = nc.tensor.matmul(bank[2][:, g * SLOTS:(g + 1) * SLOTS], wq[:, k, g * P:(g + 1) * P], slotT[:, k, :],
                                                start=(k == 0), stop=(k == KC - 1))
                last.then_inc(s["q_ready"], 1)
                project(1, 0, PROJ01[1][0])
                for grp in (1, 2):
                    pe.wait_ge(hold["mix"]["proj_out"], grp)
                    project(1, grp, PROJ01[1][grp])
                pe.wait_ge(s["kT_in"], 16)
                pe.wait_ge(s["sq_ready"], 1)
                pe.wait_ge(s["norm_steps"], 1)
                pe.wait_ge(hold["mix"]["proj_out"], 4)
                for k in range(KC):
                    for g in range(GROUPS):
                        last = nc.tensor.matmul(M1[k][:, g * HG * SLOTS:(g + 1) * HG * SLOTS], wkT[:, g, k * P:(k + 1) * P],
                                                sqbd[:, g, :, :], start=True, stop=True)
                    last.then_inc(s["m1_ready"], 1)
                for g in range(GROUPS):
                    half = (g % 2) * HG * SLOTS
                    last = nc.tensor.matmul(KBIAS[half:half + HG * SLOTS, g // 2:g // 2 + 1], sqbd[:, g, :, :], bk[:, g:g + 1],
                                            start=True, stop=True)
                last.then_inc(s["kbias_ready"], 1)

            @block.scalar
            def _(act):
                small_loads(act)
                act.wait_ge(s["small"], SMALL_AP)
                for b in range(BATCH):
                    act.wait_ge(s["blk_used"], QB * (b + 1))
                    nc.scalar.activation(zabs[:, b, :], bank[b][:], ACT.Abs, bias=bias[:]).then_inc(s["softplus"], 1)
                    nc.scalar.activation(zrelu[:, b, :], bank[b][:], ACT.Relu, bias=bias[:]).then_inc(s["softplus"], 1)
                    act.wait_ge(s["softplus"], 4 * b + 2)
                    nc.scalar.activation(zexp[:, b, :], zabs[:, b, :], ACT.Exp, scale=-1.0).then_inc(s["softplus"], 1)
                    act.wait_ge(s["softplus"], 4 * b + 3)
                    nc.scalar.activation(zln[:, b, :], zexp[:, b, :], ACT.Ln, bias=1.0).then_inc(s["softplus"], 1)
                act.wait_ge(s["cum_ready"], 1)
                nc.scalar.activation(neg[:], cum[:], ACT.Exp, scale=-1.0).then_inc(s["exp_ready"], 1)
                nc.scalar.activation(pos[:], cum[:], ACT.Exp).then_inc(s["exp_ready"], 1)
                act.wait_ge(s["exp_ready"], 1)
                nc.scalar.activation(hold["decay"][:], neg[:, 0, :, :], ACT.Copy).then_inc(s["tables_ready"], 1)
                for c in range(2):
                    for grp in range(3):
                        take_projection(nc, act, hold, c, c, grp, PROJ01[c][grp])
                    if c == 0:
                        pass_halo(nc, act, hold, 0, 0)
                for k in range(KC):
                    act.wait_ge(s["m1_ready"], k + 1)
                    nc.scalar.activation(hold["m1"][:, k, :], M1[k][:, 0:SROWS], ACT.Copy).then_inc(s["m1_done"], 1)

            def running_sums(dve, sums, carry, out, first, before):
                step = first
                for c in range(1, CHUNKS):
                    dve.wait_ge(s["carry_steps"], step)
                    nc.vector.tensor_tensor(carry[:, :, c, :], carry[:, :, c - 1, :],
                                            before.rearrange("p (b c h) -> p b c h", b=BATCH, c=CHUNKS)[:, :, c - 1, :],
                                            ALU.add).then_inc(s["carry_steps"], 1)
                    step += 1
                dve.wait_ge(s["carry_steps"], step)
                return nc.vector.tensor_tensor(out[:], sums.rearrange("p (b c h) -> p b c h", b=BATCH, c=CHUNKS), carry[:], ALU.add)

            @block.vector
            def _(dve):
                nc.vector.memset(carry[:, :, 0, :], 0.0)
                nc.vector.memset(carry2[:, :, 0, :], 0.0).then_inc(s["carry_steps"], 1)
                dve.wait_ge(s["small"], SMALL_AP)
                for b in range(BATCH):
                    dve.wait_ge(s["softplus"], 4 * (b + 1))
                    nc.vector.tensor_tensor(arow[:, b, :], zrelu[:, b, :], zln[:, b, :], ALU.add).then_inc(s["dt_steps"], 1)
                    dve.wait_ge(s["dt_steps"], b + 1)
                    nc.vector.tensor_scalar(arow[:, b, :], arow[:, b, :], apar[:], None, ALU.mult).then_inc(s["a_ready"], 1)
                for b in range(BATCH):
                    dve.wait_ge(s["a_turned"], b + 1)
                    nc.vector.tensor_copy(atok[:, b, :, :].rearrange("p (q i) h -> p i q h", q=QB),
                                          bank[6 + b][:].rearrange("p (i q h) -> p i q h", i=4, q=QB)[:, :, :, 0:HEADS]).then_inc(s["atok_ready"], 1)
                dve.wait_ge(s["sums1"], 1)
                running_sums(dve, bank[0][:], carry, cum, 1, bank[1][:]).then_inc(s["cum_ready"], 1)
                dve.wait_ge(s["k_ready"], 1)
                dve.wait_ge(s["zeros"], 10)
                for i in range(GROUPS // 2):
                    for h in range(HG):
                        r, gs = slice(h * HD, (h + 1) * HD), slice(2 * i, 2 * i + 2)
                        src = bank[2 + i][r, :].rearrange("p (g r) -> p g r", g=2)[:, :, 0:BATCH * CTX].rearrange("p g (b s) -> p g b s", b=BATCH)
                        last = nc.vector.tensor_tensor(hold["kbd"][r, :, gs, h, :].rearrange("p b g s -> p g b s"), src,
                                                       broadcast(kb[r, gs].unsqueeze(2).unsqueeze(3), [HD, 2, BATCH, CTX]), ALU.add)
                last.then_inc(s["kbd_done"], 1)
                for b in range(BATCH):
                    dve.wait_ge(s["v_ready"], b + 1)
                    nc.vector.tensor_tensor(vtok[:, b, :], bank[4 + b][0:CTX, :], vb[:], ALU.add).then_inc(s["vtok_ready"], 1)
                dve.wait_ge(s["sums2"], 1)
                running_sums(dve, bank[0][:], carry2, cume, CHUNKS, bank[1][:]).then_inc(s["norm_steps"], 1)
                dve.wait_ge(s["exp_ready"], 2)
                dve.wait_ge(s["norm_steps"], 1)
                nc.vector.tensor_tensor(norm[:], pos[:], cume[:], ALU.mult).then_inc(s["norm_steps"], 1)
                dve.wait_ge(s["norm_steps"], 2)
                nc.vector.reciprocal(rnorm[:], norm[:]).then_inc(s["norm_steps"], 1)
                dve.wait_ge(s["norm_steps"], 3)
                for b in range(BATCH):
                    nc.vector.tensor_tensor(hold["rate"][:, b, :, :], pos[:, 0, :, :], rnorm[:, b, :, :], ALU.mult).then_inc(s["tables_done"], 1)
                dve.wait_ge(hold["mixer_in"], MIXER_WEIGHTS)
                dve.wait_ge(s["halo_zeros"], 1)
                convolve(nc, dve, hold, 0, 0)
                dve.wait_ge(s["q_ready"], 1)
                for h in range(HG):
                    r = slice(h * HD, (h + 1) * HD)
                    last = nc.vector.tensor_tensor(sqbd[r, :, h, :], bank[2][r, 0:GROUPS * SLOTS].rearrange("p (g q) -> p g q", g=GROUPS),
                                                   broadcast(qb[r, :].unsqueeze(2), [HD, GROUPS, SLOTS]), ALU.add)
                last.then_inc(s["sq_ready"], 1)
                dve.wait_ge(s["kbias_ready"], 1)
                nc.vector.tensor_scalar(hold["kbias"][:], KBIAS[:, 0:SM], SCALE, None, ALU.mult).then_inc(s["tables_done"], 1)


LN_STEPS = 14
MAGIC = 0x5F3759DF


def norm_factors(nc, dve, sem, first, x, stats):
    n = len(x)
    var, y, t = stats[:, 0:n, 8:9], stats[:, 0:n, 9:10], stats[:, 0:n, 10:11]
    INT = mybir.dt.int32
    for i in range(n):
        last = nc.vector.bn_stats(stats[:, i, 0:6], x[i])
    last.then_inc(sem, 1)
    dve.wait_ge(sem, first + 1)
    nc.vector.memset(var, EPS)
    for i in range(n):
        last = nc.vector.bn_aggr(stats[:, i, 6:8], stats[:, i, 0:6])
    last.then_inc(sem, 1)
    dve.wait_ge(sem, first + 2)
    nc.vector.tensor_tensor(var, var, stats[:, 0:n, 7:8], ALU.add).then_inc(sem, 1)
    dve.wait_ge(sem, first + 3)
    nc.vector.tensor_scalar(y.bitcast(INT), var.bitcast(INT), 1, None, ALU.logical_shift_right).then_inc(sem, 1)
    dve.wait_ge(sem, first + 4)
    nc.vector.tensor_scalar(y.bitcast(INT), y.bitcast(INT), -1.0, float(MAGIC), ALU.mult, ALU.add).then_inc(sem, 1)
    for i in range(3):
        dve.wait_ge(sem, first + 5 + 3 * i)
        nc.vector.tensor_tensor(t, y, y, ALU.mult).then_inc(sem, 1)
        dve.wait_ge(sem, first + 6 + 3 * i)
        nc.vector.scalar_tensor_tensor(t, t, -0.5, var, ALU.mult, ALU.mult).then_inc(sem, 1)
        dve.wait_ge(sem, first + 7 + 3 * i)
        last = nc.vector.scalar_tensor_tensor(y, t, 1.5, y, ALU.add, ALU.mult)
        last.then_inc(sem, 1)
    dve.wait_ge(sem, first + LN_STEPS)


def layernorm(nc, dve, sem, first, x, stats, out):
    norm_factors(nc, dve, sem, first, x, stats)
    for i in range(len(x)):
        last = nc.vector.tensor_scalar(out[i], x[i], stats[:, i, 6:7], stats[:, i, 9:10], ALU.subtract, ALU.mult)
    return last


def mixer_stage(nc, io, hold):
    with Stage(nc, "mix", hold["arena"]) as st:
        wout, conv = hold["wout"], hold["conv"]
        xT = [st.sb(f"xT{i}", [P, KC, P]) for i in range(2)]
        x_in = [st.sb(f"x_in{i}", [P, BATCH, D]) for i in range(2)]
        cbd = st.sb("cbd", [P, GROUPS, HG, P])
        btok = st.sb("btok", [P, D])
        xs = st.sb("xs", [P, D])
        scores = st.sb("scores", [P, HEADS, P])
        state = st.sb("state", [P, GROUPS, P])
        rate = st.sb("rate", [P, BATCH, HEADS, HD])
        rateT = st.sb("rateT", [P, BATCH, D])
        yT = st.sb("yT", [P, BATCH, D])
        xr = st.sb("xr", [P, BATCH, D])
        stats = st.sb("stats", [P, BATCH, 12])
        x1 = [st.sb(f"x1_{i}", [P, BATCH, D]) for i in range(2)]
        bank = st.banks()
        PROJ, XTURN, BTURN, Y, OUT = bank[0:3], bank[3], bank[4], bank[5], bank[6:8]
        SCORE = PROJ + [XTURN]
        STATE, RATE = BTURN, (XTURN, BTURN)
        s = hold["mix"]
        xT_in, x_arrived, x1_stored = st.pair("xT_in"), st.pair("x_arrived"), st.pair("x1_stored")
        x_v = io["x"].rearrange("(b n) d -> n b d", b=BATCH)
        x1_v = io["x1"].rearrange("(b n) d -> n b d", b=BATCH)
        LAST = CHUNKS - 1

        def load_turned(sp, c, u):
            wait_later(sp, s["proj_done"], 3 * (c - 1))
            sp.dma_start(xT[u][:], io["xT"].rearrange("(k p) n -> p k n", p=P)[:, :, bass.ds(c * P, P)]).then_inc(xT_in[u], 16)

        def load_residual(sp, c, u):
            wait_later(sp, s["res_done"], 2 * (c - 1))
            sp.dma_start(x_in[u][:], x_v[bass.ds(c * P, P), :, :]).then_inc(x_arrived[u], 16)

        def store(sp, c, u):
            sp.wait_ge(s["x1_done"], c + 1)
            sp.dma_start(x1_v[bass.ds(c * P, P), :, :], x1[u][:]).then_inc(x1_stored[u], 16)

        def project(pe, c, u, half, grp):
            if grp == 0:
                pe.wait_ge(xT_in[u], 16 * half)
            wait_later(pe, s["proj_out"], 3 * (c - 1) + grp + 1)
            wait_later(pe, s["scores_masked"], 4 * (c - 2) + grp + 1)
            project_group(nc, hold, grp, xT[u], PROJ[grp])

        def turn(pe, c, u):
            pe.wait_ge(s["convB"], c + 1)
            wait_later(pe, s["rateT_done"], 2 * c)
            for g in range(GROUPS):
                last = nc.tensor.transpose(BTURN[:, g * P:(g + 1) * P], conv[u][:, 4 + g, :], hold["ident"][:])
            last.then_inc(s["b_turned"], 1)
            pe.wait_ge(s["convX"], c + 1)
            for g in range(GROUPS):
                last = nc.tensor.transpose(XTURN[:, g * P:(g + 1) * P], conv[u][:, 8 + g, :], hold["ident"][:])
            last.then_inc(s["x_turned"], 1)

        def score(pe, c, u, g):
            if g == 0:
                pe.wait_ge(s["cbd_done"], c + 1)
            if g == 3:
                pe.wait_ge(s["xs_done"], c + 1)
            else:
                pe.wait_ge(s["proj_out"], min(3 * (c + 1) + g + 1, 3 * CHUNKS) if isinstance(c, int) else 3 * (c + 1) + g + 1)
            nc.tensor.matmul(SCORE[g][:], conv[u][:, 4 + g, :], cbd[:, g, :, :], start=True, stop=True).then_inc(s["scores_done"], 1)

        def add_to_state(pe, c):
            pe.wait_ge(s["btok_done"], c + 1)
            pe.wait_ge(s["xs_done"], c + 1)
            for g in range(GROUPS):
                last = nc.tensor.matmul(STATE[:, g * P:(g + 1) * P], btok[:, g * P:(g + 1) * P], xs[:, g * P:(g + 1) * P], start=True, stop=True)
            last.then_inc(s["state_done"], 1)

        def weigh_steps(pe, c, u):
            wait_later(pe, s["yT_done"], 2 * c)
            wait_later(pe, s["state_added"], c)
            for g in range(GROUPS):
                nc.tensor.matmul(Y[:, g * P:(g + 1) * P], state[:, g, :], conv[u][:, g, :], start=True, stop=False, skip_group_check=True)
                pe.wait_ge(s["scores_masked"], 4 * c + g + 1)
                for h in range(HG):
                    hh = g * HG + h
                    last = nc.tensor.matmul(Y[h * HD:(h + 1) * HD, g * P:(g + 1) * P], xs[:, hh * HD:(hh + 1) * HD], scores[:, hh, :],
                                            start=False, stop=True, skip_group_check=True)
            last.then_inc(s["y_done"], 1)

        def turn_rates(pe, c):
            pe.wait_ge(s["rate_done"], c + 1)
            for b in range(BATCH):
                if b == 0:
                    pe.wait_ge(s["scores_masked"], 4 * c + 4)
                else:
                    pe.wait_ge(s["state_added"], c + 1)
                for g in range(GROUPS):
                    last = nc.tensor.transpose(RATE[b][:, g * P:(g + 1) * P], rate[:, b, g * HG:(g + 1) * HG, :], hold["ident"][:])
                last.then_inc(s["rate_turned"], 1)

        def project_out(pe, c):
            for b in range(BATCH):
                pe.wait_ge(s["yT_done"], 2 * c + b + 1)
                wait_later(pe, s["res_done"], 2 * c - 1 + b)
                for g in range(GROUPS):
                    last = nc.tensor.matmul(OUT[b][:], yT[:, b, g * P:(g + 1) * P], wout[:, g, :], start=(g == 0), stop=(g == GROUPS - 1))
                last.then_inc(s["out_done"], 1)

        def spread_c(act, c, u):
            act.wait_ge(s["convC"], c + 1)
            wait_later(act, s["scores_done"], 4 * c)
            for h in range(HG):
                r = slice(h * HD, (h + 1) * HD)
                last = nc.scalar.activation(cbd[r, :, h, :], conv[u][r, 0:GROUPS, :], ACT.Copy)
            last.then_inc(s["cbd_done"], 1)

        def spread_rates(act, c):
            wait_later(act, s["rate_turned"], 2 * c)
            for b in range(BATCH):
                last = nc.scalar.activation(rate[:, b, :, :], broadcast(hold["rate"][:, b, bass.ds(c, 1), :].rearrange("p o h -> p (o h)").unsqueeze(2), [P, HEADS, HD]), ACT.Copy)
            last.then_inc(s["rate_done"], 1)

        def take_b(act, c):
            act.wait_ge(s["b_turned"], c + 1)
            wait_later(act, s["state_done"], c)
            nc.scalar.activation(btok[:], BTURN[:], ACT.Copy).then_inc(s["btok_done"], 1)

        def take_rates(act, c):
            for b in range(BATCH):
                act.wait_ge(s["rate_turned"], 2 * c + b + 1)
                wait_later(act, s["yT_done"], 2 * c - 1 + b)
                nc.scalar.activation(rateT[:, b, :], RATE[b][:], ACT.Copy).then_inc(s["rateT_done"], 1)

        def weigh_x(dve, c):
            dve.wait_ge(s["x_turned"], c + 1)
            nc.vector.tensor_tensor(xs[:].rearrange("p (h d) -> p h d", h=HEADS), XTURN[:].rearrange("p (h d) -> p h d", h=HEADS),
                                    broadcast(hold["decay"][:, bass.ds(c, 1), :].rearrange("p o h -> p (o h)").unsqueeze(2), [P, HEADS, HD]),
                                    ALU.mult).then_inc(s["xs_done"], 1)

        def mask_scores(dve, c):
            for g in range(GROUPS):
                dve.wait_ge(s["scores_done"], 4 * c + g + 1)
                nc.vector.tensor_tensor(scores[:, g * HG:(g + 1) * HG, :], SCORE[g][:].rearrange("p (h l) -> p h l", h=HG),
                                        broadcast(hold["tri"][:].unsqueeze(1), [P, HG, P]), ALU.mult).then_inc(s["scores_masked"], 1)

        def advance_state(dve, c):
            dve.wait_ge(s["y_done"], c + 1)
            dve.wait_ge(s["state_done"], c + 1)
            for h in range(HG):
                r = slice(h * HD, (h + 1) * HD)
                last = nc.vector.tensor_tensor(state[r, :, r], STATE[r, :].rearrange("p (g q) -> p g q", g=GROUPS)[:, :, r], state[r, :, r], ALU.add)
            last.then_inc(s["state_added"], 1)

        def rate_outputs(dve, c):
            for b in range(BATCH):
                dve.wait_ge(s["rateT_done"], 2 * c + b + 1)
                wait_later(dve, s["out_done"], 2 * c - 1 + b)
                nc.vector.tensor_tensor(yT[:, b, :], Y[:], rateT[:, b, :], ALU.mult).then_inc(s["yT_done"], 1)

        def norm(dve, c, u, half):
            dve.wait_ge(x_arrived[u], 16 * (half + 1))
            wait_later(dve, s["x1_done"], c)
            for b in range(BATCH):
                dve.wait_ge(s["out_done"], 2 * c + b + 1)
                nc.vector.tensor_tensor(xr[:, b, :], OUT[b][:], x_in[u][:, b, :], ALU.add).then_inc(s["res_done"], 1)
            dve.wait_ge(s["res_done"], 2 * c + 2)
            wait_later(dve, x1_stored[u], 16 * half)
            layernorm(nc, dve, s["ln_step"], LN_STEPS * c, [xr[:, b, :] for b in range(BATCH)], stats,
                      [x1[u][:, b, :] for b in range(BATCH)]).then_inc(s["x1_done"], 1)

        def chunks(eng, body):
            for c in range(4):
                body(c, c % 2, c // 2)
            with eng.Fori(2, CHUNKS // 2 - 2) as i:
                for u in (0, 1):
                    body(2 * i + u, u, i)
            for c in range(CHUNKS - 4, CHUNKS):
                body(c, c % 2, c // 2)

        def before(c, n):
            return not isinstance(c, int) or c >= n

        def ahead(c, n):
            return not isinstance(c, int) or c + n <= LAST

        with nc.Block() as block:
            @block.sync
            def _(sp):
                load_turned(sp, 2, 0)
                load_residual(sp, 0, 0)

                def step(c, u, half):
                    if ahead(c, 3):
                        load_turned(sp, c + 3, 1 - u)
                    if before(c, 2):
                        store(sp, c - 2, u)
                    if ahead(c, 1):
                        load_residual(sp, c + 1, 1 - u)
                    if isinstance(c, int) and c == 1:
                        for dst, src in ((hold["q_w"], io["q_w"]), (hold["o_w"], io["o_w"])):
                            sp.dma_start(dst[:], src.rearrange("(k p) n -> p k n", p=P)).then_inc(hold["cross_in"], 16)
                        sp.dma_start(hold["qbias"][:], io["q_b"]).then_inc(hold["cross_in"], 16)
                chunks(sp, step)
                store(sp, LAST - 1, 0)
                store(sp, LAST, 1)
                for u in range(2):
                    sp.wait_ge(x1_stored[u], 16 * CHUNKS // 2)

            @block.tensor
            def _(pe):
                pe.wait_ge(hold["mixer_in"], MIXER_WEIGHTS)
                pe.wait_ge(s["zeros"], 2)

                def step(c, u, half):
                    turn(pe, c, u)
                    score(pe, c, u, 0)
                    score(pe, c, u, 1)
                    add_to_state(pe, c)
                    score(pe, c, u, 2)
                    score(pe, c, u, 3)
                    weigh_steps(pe, c, u)
                    if ahead(c, 2):
                        project(pe, c + 2, u, half + 1, 0)
                    turn_rates(pe, c)
                    if ahead(c, 2):
                        project(pe, c + 2, u, half + 1, 1)
                        project(pe, c + 2, u, half + 1, 2)
                    project_out(pe, c)
                chunks(pe, step)

            @block.scalar
            def _(act):
                act.wait_ge(s["zeros"], 2)
                spread_c(act, 0, 0)
                pass_halo(nc, act, hold, 1, 1)
                spread_rates(act, 0)

                def step(c, u, half):
                    take_b(act, c)
                    if ahead(c, 2):
                        take_projection(nc, act, hold, c + 2, u, 0, PROJ[0])
                    take_rates(act, c)
                    if ahead(c, 2):
                        take_projection(nc, act, hold, c + 2, u, 1, PROJ[1])
                        take_projection(nc, act, hold, c + 2, u, 2, PROJ[2])
                    if ahead(c, 1):
                        spread_c(act, c + 1, 1 - u)
                    if ahead(c, 3):
                        pass_halo(nc, act, hold, c + 2, u)
                    if ahead(c, 1):
                        spread_rates(act, c + 1)
                chunks(act, step)

            @block.gpsimd
            def _(pool):
                nc.gpsimd.memset(cbd[:], 0.0).then_inc(s["zeros"], 1)
                nc.gpsimd.memset(state[:], 0.0).then_inc(s["zeros"], 1)

                def step(c, u, half):
                    if ahead(c, 1):
                        convolve_x(nc, pool, hold, c + 1, 1 - u)
                chunks(pool, step)

            @block.vector
            def _(dve):
                dve.wait_ge(s["zeros"], 2)

                def step(c, u, half):
                    weigh_x(dve, c)
                    mask_scores(dve, c)
                    advance_state(dve, c)
                    if not ahead(c, 1):
                        rate_outputs(dve, c)
                    if before(c, 1):
                        norm(dve, c - 1, 1 - u, half - 1 + u)
                    if ahead(c, 1):
                        rate_outputs(dve, c)
                    if ahead(c, 1):
                        convolve(nc, dve, hold, c + 1, 1 - u)
                chunks(dve, step)
                norm(dve, LAST, 1, CHUNKS // 2 - 1)


def prefetch(sp, io, ring, ring_in, e, unit):
    fetch_unit(sp, io, ring[:, unit, :], ring_in[unit], e, unit)


def fetch_unit(sp, io, dst, arrived, e, unit):
    kind, half = unit // 2, unit % 2
    if kind < 2:
        src = (io["e_W1"], io["e_Wg"])[kind].rearrange("e (p k) f -> e p (k f)", p=P)[bass.ds(e, 1), :, half * UNIT:(half + 1) * UNIT]
        sp.dma_start(dst, src.rearrange("o p f -> (o p) f")).then_inc(arrived, 16)
    else:
        src = io["e_W2"].rearrange("e (q p s) n -> e p q (s n)", q=4, p=P)[bass.ds(e, 1), :, 2 * half:2 * half + 2, :]
        sp.dma_start(dst.rearrange("p (q n) -> p q n", q=2), src.rearrange("o p q n -> (o p) q n")).then_inc(arrived, 16)


FIRST_UNITS = {1: (0, 1), CHUNKS - 2: (2, 3), CHUNKS: (4, 5)}


def cross_stage(nc, io, hold, ring, ring_in):
    with Stage(nc, "crs") as st:
        wq, wo, qbias = hold["q_w"], hold["o_w"], hold["qbias"]
        ob = st.sb("ob", [P, D])
        x1 = [st.sb(f"x1_{i}", [P, D]) for i in range(2)]
        x1b = [st.sb(f"x1b{i}", [P, D]) for i in range(2)]
        x1T = st.sb("x1T", [P, KC, P])
        qT = st.sb("qT", [P, GROUPS, P])
        pr = st.sb("pr", [P, HEADS, CTX])
        top = st.sb("top", [P, HEADS])
        den = st.sb("den", [P, HEADS])
        rden = st.sb("rden", [P, HEADS])
        prT = st.sb("prT", [PIECE, 3, GROUPS * P])
        y = st.sb("y", [P, D])
        yT = st.sb("yT", [P, KC, P])
        xr = st.sb("xr", [P, D])
        stats = st.sb("stats", [P, 1, 12])
        x2 = [st.sb(f"x2_{i}", [P, D]) for i in range(2)]
        x2T = [st.sb(f"x2T{i}", [P, KC, P]) for i in range(2)]
        tile_top = st.sb("tile_top", [P, SM])
        new_top = st.sb("new_top", [P, SM])
        drop = st.sb("drop", [P, SM])
        shift = st.sb("shift", [P, SM])
        alpha = st.sb("alpha", [P, SM])
        tile_sum = st.sb("tile_sum", [P, SM])
        sp_pr = st.sb("sp_pr", [P, SM, P])
        sp_prT = st.sb("sp_prT", [P, SROWS])
        bank = st.banks()
        SC, AV, TURN, OUT, SLOT, TOK = bank[0:3], bank[3], bank[4], bank[5], bank[6], bank[7]
        s = st.sems("ob_in", "zeros", "mix_turned", "x1T_done", "q_done", "qT_done", "sc_done", "masked", "top_done", "shifted", "exp_done",
                    "den_done", "rden_done", "pr_turned", "prT_done", "av_done", "y_done", "y_turned", "yT_done", "o_done", "x1b_done",
                    "res_done", "ln_step", "x2_done", "x2_turned", "x2T_done", "slot_sc", "slot_step", "slot_shift", "slot_alpha", "slot_exp", "slot_sum",
                    "slot_turned", "sp_prT_done", "z_done", "z_added")
        x1_in, x2_stored, x2T_stored = st.pair("x1_in"), st.pair("x2_stored"), st.pair("x2T_stored")
        LAST = TILES - 1
        SB = 512 // CTX
        HEADS_OF = [(i * SB, min((i + 1) * SB, HEADS)) for i in range(3)]

        def load(sp, t, u):
            wait_later(sp, s["mix_turned"], t - 1)
            wait_later(sp, s["x1b_done"], t - 1)
            sp.dma_start(x1[u][:], io["x1"][bass.ds(t * P, P), :]).then_inc(x1_in[u], 16)

        def store_x2(sp, t, u):
            sp.wait_ge(s["x2_done"], t + 1)
            sp.dma_start(io["x2"][bass.ds(t * P, P), :], x2[u][:]).then_inc(x2_stored[u], 16)

        def store_x2T(sp, t, u):
            sp.wait_ge(s["x2T_done"], t + 1)
            sp.dma_start(io["x2T"][bass.ds(t * P, P), :], x2T[u][:].rearrange("p k t -> p (k t)")).then_inc(x2T_stored[u], 16)

        def turn_x1(pe, t, u, half):
            pe.wait_ge(x1_in[u], 16 * (half + 1))
            wait_later(pe, s["z_added"], 2 * (t - 3))
            wait_later(pe, s["x1T_done"], t)
            for k in range(KC):
                last = nc.tensor.transpose(TOK[:, k * P:(k + 1) * P], x1[u][:, k * P:(k + 1) * P], hold["ident"][:])
            last.then_inc(s["mix_turned"], 1)

        def queries(pe, t):
            pe.wait_ge(s["x1T_done"], t + 1)
            wait_later(pe, s["qT_done"], t)
            wait_later(pe, s["y_done"], t - 1)
            for g in range(GROUPS):
                for k in range(KC):
                    last = nc.tensor.matmul(AV[:, g * P:(g + 1) * P], wq[:, k, g * P:(g + 1) * P], x1T[:, k, :],
                                            start=(k == 0), stop=(k == KC - 1))
            last.then_inc(s["q_done"], 1)

        def score(pe, t, b, between=None):
            pe.wait_ge(s["qT_done"], t + 1)
            wait_later(pe, s["prT_done"], 3 * t)
            for i, (h0, h1) in enumerate(HEADS_OF):
                if i == 2 and between:
                    between()
                for g in range(h0 // HG, -(-h1 // HG)):
                    a, z = max(h0, g * HG), min(h1, (g + 1) * HG)
                    last = nc.tensor.matmul(SC[i][:, (a - h0) * CTX:(z - h0) * CTX], qT[:, g, :],
                                            hold["kbd"][:, b, g, a - g * HG:z - g * HG, :], start=True, stop=True)
                last.then_inc(s["sc_done"], 1)

        def turn_probs(pe, t):
            pe.wait_ge(s["exp_done"], t + 1)
            for i, w in enumerate(PIECES):
                for g in range(GROUPS):
                    at = g * KROWS + i * PIECE
                    last = nc.tensor.transpose(SC[i][0:w, g * P:(g + 1) * P], pr[:].rearrange("p h s -> p (h s)")[:, at:at + w], hold["ident"][:])
                last.then_inc(s["pr_turned"], 1)

        def weigh_values(pe, t, b):
            pe.wait_ge(s["prT_done"], 3 * t + 3)
            pe.wait_ge(s["qT_done"], min(t + 2, TILES) if isinstance(t, int) else t + 2)
            for g in range(GROUPS):
                for i, w in enumerate(PIECES):
                    last = nc.tensor.matmul(AV[:, g * P:(g + 1) * P], prT[0:w, i, g * P:(g + 1) * P], hold["vbd"][0:w, b, i, g, :],
                                            start=(i == 0), stop=(i == 2))
            last.then_inc(s["av_done"], 1)

        def turn_y(pe, t):
            pe.wait_ge(s["y_done"], t + 1)
            wait_later(pe, s["x2T_done"], t)
            for k in range(KC):
                last = nc.tensor.transpose(TURN[:, k * P:(k + 1) * P], y[:, k * P:(k + 1) * P], hold["ident"][:])
            last.then_inc(s["y_turned"], 1)

        def project_out(pe, t):
            pe.wait_ge(s["yT_done"], t + 1)
            wait_later(pe, s["res_done"], t)
            for k in range(KC):
                last = nc.tensor.matmul(OUT[:], yT[:, k, :], wo[:, k, :], start=(k == 0), stop=(k == KC - 1))
            last.then_inc(s["o_done"], 1)

        def turn_x2(pe, t, u):
            pe.wait_ge(s["x2_done"], t + 1)
            pe.wait_ge(s["yT_done"], t + 1)
            for k in range(KC):
                last = nc.tensor.transpose(TURN[:, k * P:(k + 1) * P], x2[u][:, k * P:(k + 1) * P], hold["ident"][:])
            last.then_inc(s["x2_turned"], 1)

        def slot_scores(pe, t, u):
            pe.wait_ge(s["x2T_done"], t + 1)
            wait_later(pe, s["slot_exp"], t)
            for m in range(SM):
                for k in range(KC):
                    last = nc.tensor.matmul(SLOT[:, m * P:(m + 1) * P], hold["m1"][:, k, m * P:(m + 1) * P], x2T[u][:, k, :],
                                            start=(k == 0), stop=(k == KC - 1))
            last.then_inc(s["slot_sc"], 1)

        def turn_slots(pe, t):
            pe.wait_ge(s["slot_exp"], t + 1)
            wait_later(pe, s["sp_prT_done"], t)
            for m in range(SM):
                last = nc.tensor.transpose(SLOT[:, SROWS + m * P:SROWS + (m + 1) * P], sp_pr[:, m, :], hold["ident"][:])
            last.then_inc(s["slot_turned"], 1)

        def weigh_tokens(pe, t, u, m):
            pe.wait_ge(s["sp_prT_done"], t + 1)
            if m == 1:
                pe.wait_ge(s["z_added"], 2 * t + 1)
            else:
                wait_later(pe, s["z_added"], 2 * t)
                pe.wait_ge(s["x1T_done"], min(t + 4, TILES) if isinstance(t, int) else t + 4)
            nc.tensor.matmul(TOK[:], sp_prT[:, m * P:(m + 1) * P], x2[u][:], start=True, stop=True).then_inc(s["z_done"], 1)

        def take_x1T(act, t):
            act.wait_ge(s["mix_turned"], t + 1)
            wait_later(act, s["q_done"], t)
            nc.scalar.activation(x1T[:].rearrange("p k t -> p (k t)"), TOK[:], ACT.Copy).then_inc(s["x1T_done"], 1)

        def exponents(act, t):
            act.wait_ge(s["shifted"], t + 1)
            nc.scalar.activation(pr[:], pr[:], ACT.Exp, scale=SCALE).then_inc(s["exp_done"], 1)

        def take_x2T(act, t, u, half):
            act.wait_ge(s["x2_turned"], t + 1)
            wait_later(act, s["slot_sc"], t - 1)
            wait_later(act, x2T_stored[u], 16 * half)
            nc.scalar.activation(x2T[u][:].rearrange("p k t -> p (k t)"), TURN[:], ACT.Copy).then_inc(s["x2T_done"], 1)

        def slot_exponents(act, t):
            act.wait_ge(s["slot_shift"], t + 1)
            wait_later(act, s["z_added"], 2 * t)
            wait_later(act, s["slot_sum"], 2 * t)
            nc.scalar.activation(alpha[:], drop[:], ACT.Exp).then_inc(s["slot_alpha"], 1)
            wait_later(act, s["slot_turned"], t)
            for m in range(SM):
                last = nc.scalar.activation(sp_pr[:, m, :], SLOT[:, m * P:(m + 1) * P], ACT.Exp, bias=shift[:, m:m + 1], scale=SCALE,
                                            accum_out=tile_sum[:, m:m + 1])
            last.then_inc(s["slot_exp"], 1)

        def take_probsT(act, t, between=None):
            wait_later(act, s["av_done"], t)
            for i, w in enumerate(PIECES):
                if i == 2 and between:
                    between()
                act.wait_ge(s["pr_turned"], 3 * t + i + 1)
                nc.scalar.activation(prT[0:w, i, :], SC[i][0:w, :], ACT.Copy).then_inc(s["prT_done"], 1)

        def take_slotsT(act, t):
            act.wait_ge(s["slot_turned"], t + 1)
            wait_later(act, s["z_done"], 2 * t)
            nc.scalar.activation(sp_prT[:], SLOT[:, SROWS:2 * SROWS], ACT.Copy).then_inc(s["sp_prT_done"], 1)

        def take_yT(act, t):
            act.wait_ge(s["y_turned"], t + 1)
            wait_later(act, s["o_done"], t)
            nc.scalar.activation(yT[:].rearrange("p k t -> p (k t)"), TURN[:], ACT.Copy).then_inc(s["yT_done"], 1)

        def take_scores(dve, t, causal):
            src = [SC[i][:, 0:(h1 - h0) * CTX].rearrange("p (h s) -> p h s", s=CTX) for i, (h0, h1) in enumerate(HEADS_OF)]
            if causal:
                wait_later(dve, s["pr_turned"], 3 * t)
                for i, (h0, h1) in enumerate(HEADS_OF):
                    dve.wait_ge(s["sc_done"], 3 * t + i + 1)
                    last = nc.vector.tensor_tensor(pr[:, h0:h1, :], src[i], broadcast(hold["mask"][:].unsqueeze(1), [P, h1 - h0, CTX]), ALU.add)
                    src[i] = pr[:, h0:h1, :]
                last.then_inc(s["masked"], 1)
                dve.wait_ge(s["masked"], 1 if t == 0 else 2)
            for i, (h0, h1) in enumerate(HEADS_OF):
                dve.wait_ge(s["sc_done"], 3 * t + i + 1)
                last = nc.vector.tensor_reduce(top[:, h0:h1], src[i], AX.X, ALU.max)
            last.then_inc(s["top_done"], 1)
            dve.wait_ge(s["top_done"], t + 1)
            wait_later(dve, s["pr_turned"], 3 * t)
            for i, (h0, h1) in enumerate(HEADS_OF):
                last = nc.vector.tensor_tensor(pr[:, h0:h1, :], src[i], broadcast(top[:, h0:h1].unsqueeze(2), [P, h1 - h0, CTX]), ALU.subtract)
            last.then_inc(s["shifted"], 1)

        def take_queries(dve, t):
            dve.wait_ge(s["q_done"], t + 1)
            wait_later(dve, s["sc_done"], 3 * t)
            nc.vector.tensor_tensor(qT[:], AV[:].rearrange("p (g t) -> p g t", g=GROUPS), broadcast(qbias[:].unsqueeze(2), [P, GROUPS, P]),
                                    ALU.add).then_inc(s["qT_done"], 1)

        def slot_maxima(dve, t, b):
            st_top = hold["top"][:, b, :]
            dve.wait_ge(s["slot_sc"], t + 1)
            wait_later(dve, s["slot_exp"], t)
            first = 3 * t
            nc.vector.tensor_reduce(tile_top[:], SLOT[:, 0:SROWS].rearrange("p (m t) -> p m t", m=SM), AX.X, ALU.max).then_inc(s["slot_step"], 1)
            dve.wait_ge(s["slot_step"], first + 1)
            nc.vector.scalar_tensor_tensor(tile_top[:], tile_top[:], SCALE, hold["kbias"][:], ALU.mult, ALU.add).then_inc(s["slot_step"], 1)
            dve.wait_ge(s["slot_step"], first + 2)
            nc.vector.tensor_tensor(new_top[:], st_top, tile_top[:], ALU.max).then_inc(s["slot_step"], 1)
            dve.wait_ge(s["slot_step"], first + 3)
            nc.vector.tensor_tensor(drop[:], st_top, new_top[:], ALU.subtract)
            nc.vector.tensor_tensor(shift[:], hold["kbias"][:], new_top[:], ALU.subtract).then_inc(s["slot_shift"], 1)
            dve.wait_ge(s["slot_shift"], t + 1)
            nc.vector.tensor_copy(st_top, new_top[:])

        def denominators(dve, t):
            dve.wait_ge(s["exp_done"], t + 1)
            nc.vector.tensor_reduce(den[:], pr[:], AX.X, ALU.add).then_inc(s["den_done"], 1)
            dve.wait_ge(s["den_done"], t + 1)
            nc.vector.reciprocal(rden[:], den[:]).then_inc(s["rden_done"], 1)

        def slot_sums(dve, t, b):
            st_sum = hold["sum"][:, b, :]
            dve.wait_ge(s["slot_exp"], t + 1)
            nc.vector.tensor_tensor(st_sum, st_sum, alpha[:], ALU.mult).then_inc(s["slot_sum"], 1)
            dve.wait_ge(s["slot_sum"], 2 * t + 1)
            nc.vector.tensor_tensor(st_sum, st_sum, tile_sum[:], ALU.add).then_inc(s["slot_sum"], 1)

        def normalise(dve, t):
            dve.wait_ge(s["rden_done"], t + 1)
            dve.wait_ge(s["av_done"], t + 1)
            wait_later(dve, s["y_turned"], t)
            nc.vector.tensor_tensor(y[:].rearrange("p (h d) -> p h d", h=HEADS), AV[:].rearrange("p (h d) -> p h d", h=HEADS),
                                    broadcast(rden[:].unsqueeze(2), [P, HEADS, HD]), ALU.mult).then_inc(s["y_done"], 1)

        def add_tokens(dve, t, b, m):
            z = hold["z"][:, b, m, :]
            dve.wait_ge(s["z_done"], 2 * t + m + 1)
            nc.vector.scalar_tensor_tensor(z, z, alpha[:, m:m + 1], TOK[:], ALU.mult, ALU.add).then_inc(s["z_added"], 1)

        def residual(dve, t, u):
            dve.wait_ge(s["o_done"], t + 1)
            dve.wait_ge(s["x1b_done"], t + 1)
            wait_later(dve, s["x2_done"], t)
            nc.vector.tensor_tensor(xr[:], OUT[:], x1b[u][:], ALU.add).then_inc(s["res_done"], 1)

        def norm(dve, t, u, half):
            dve.wait_ge(s["res_done"], t + 1)
            wait_later(dve, x2_stored[u], 16 * half)
            wait_later(dve, s["z_done"], 2 * t - 2)
            layernorm(nc, dve, s["ln_step"], LN_STEPS * t, [xr[:]], stats, [x2[u][:]]).then_inc(s["x2_done"], 1)

        def add_bias(pool, t, u, half):
            pool.wait_ge(x1_in[u], 16 * (half + 1))
            wait_later(pool, s["res_done"], t - 1)
            nc.gpsimd.tensor_tensor(x1b[u][:], x1[u][:], ob[:], ALU.add).then_inc(s["x1b_done"], 1)

        def tiles(eng, body):
            def alone(*ts):
                for t in ts:
                    body(t, t % 2, t // 2, lambda d, t=t: (t + d) // CHUNKS)

            def loop(first, end, b):
                with eng.Fori(first // 2, end // 2) as i:
                    for u in (0, 1):
                        body(2 * i + u, u, i, lambda d: b)
            alone(0, 1, 2, 3)
            loop(4, CHUNKS - 2, 0)
            alone(CHUNKS - 2, CHUNKS - 1, CHUNKS, CHUNKS + 1)
            loop(CHUNKS + 2, TILES - 2, 1)
            alone(TILES - 2, TILES - 1)

        def before(t, tiles):
            return not isinstance(t, int) or t >= tiles

        def ahead(t, tiles):
            return not isinstance(t, int) or t + tiles <= LAST

        with nc.Block() as block:
            @block.sync
            def _(sp):
                load(sp, 0, 0)
                load(sp, 1, 1)
                sp.dma_start(ob[:], broadcast(io["o_b"].rearrange("(o n) -> o n", o=1), [P, D])).then_inc(s["ob_in"], 16)

                def step(t, u, half, seq):
                    if ahead(t, 2):
                        load(sp, t + 2, u)
                    if before(t, 1):
                        store_x2(sp, t - 1, 1 - u)
                        store_x2T(sp, t - 1, 1 - u)
                    if isinstance(t, int) and t == 2:
                        for dst, src in ((hold["dwv"], io["d_Wv"]), (hold["dwo"], io["d_Wo"])):
                            sp.dma_start(dst[:], src.rearrange("(k p) n -> p k n", p=P)).then_inc(hold["slot_w_in"], 16)
                    if isinstance(t, int) and t in FIRST_UNITS:
                        for unit in FIRST_UNITS[t]:
                            prefetch(sp, io, ring, ring_in, 0, unit)
                tiles(sp, step)
                store_x2(sp, LAST, 1)
                store_x2T(sp, LAST, 1)
                for u in range(2):
                    sp.wait_ge(x2_stored[u], 16 * TILES // 2)
                    sp.wait_ge(x2T_stored[u], 16 * TILES // 2)

            @block.tensor
            def _(pe):
                pe.wait_ge(hold["cross_in"], 3 * 16)
                turn_x1(pe, 0, 0, 0)
                queries(pe, 0)
                turn_x1(pe, 1, 1, 0)
                score(pe, 0, 0)
                queries(pe, 1)

                def step(t, u, half, seq):
                    turn_probs(pe, t)
                    if before(t, 1):
                        turn_x2(pe, t - 1, 1 - u)
                    if before(t, 2):
                        weigh_tokens(pe, t - 2, u, 1)
                    if before(t, 1):
                        slot_scores(pe, t - 1, 1 - u)
                    weigh_values(pe, t, seq(0))
                    if ahead(t, 1):
                        score(pe, t + 1, seq(1), lambda: turn_y(pe, t))
                    else:
                        turn_y(pe, t)
                    if before(t, 1):
                        turn_slots(pe, t - 1)
                    if ahead(t, 2):
                        turn_x1(pe, t + 2, u, half + 1)
                    project_out(pe, t)
                    if before(t, 1):
                        weigh_tokens(pe, t - 1, 1 - u, 0)
                    if ahead(t, 2):
                        queries(pe, t + 2)
                tiles(pe, step)
                turn_x2(pe, LAST, 1)
                weigh_tokens(pe, LAST - 1, 0, 1)
                slot_scores(pe, LAST, 1)
                turn_slots(pe, LAST)
                for m in range(SM):
                    weigh_tokens(pe, LAST, 1, m)

            @block.scalar
            def _(act):
                take_x1T(act, 0)
                take_x1T(act, 1)
                exponents(act, 0)

                def step(t, u, half, seq):
                    if before(t, 1):
                        take_probsT(act, t, lambda: take_x2T(act, t - 1, 1 - u, half - 1 + u))
                        slot_exponents(act, t - 1)
                    else:
                        take_probsT(act, t)
                    take_yT(act, t)
                    if before(t, 1):
                        take_slotsT(act, t - 1)
                    if ahead(t, 2):
                        take_x1T(act, t + 2)
                    if ahead(t, 1):
                        exponents(act, t + 1)
                tiles(act, step)
                take_x2T(act, LAST, 1, TILES // 2 - 1)
                slot_exponents(act, LAST)
                take_slotsT(act, LAST)

            @block.vector
            def _(dve):
                nc.vector.memset(hold["top"][:], NEG)
                nc.vector.memset(hold["sum"][:], 0.0)
                nc.vector.memset(hold["z"][:], 0.0).then_inc(s["zeros"], 1)
                dve.wait_ge(s["zeros"], 1)
                dve.wait_ge(hold["cross_in"], 3 * 16)
                take_queries(dve, 0)
                take_scores(dve, 0, True)

                def step(t, u, half, seq):
                    if ahead(t, 1):
                        take_queries(dve, t + 1)
                    denominators(dve, t)
                    if before(t, 2):
                        add_tokens(dve, t - 2, seq(-2), 1)
                    if before(t, 1):
                        slot_maxima(dve, t - 1, seq(-1))
                    normalise(dve, t)
                    if before(t, 1):
                        slot_sums(dve, t - 1, seq(-1))
                    if ahead(t, 1):
                        take_scores(dve, t + 1, isinstance(t, int) and (t + 1) % CHUNKS == 0)
                    residual(dve, t, u)
                    if before(t, 1):
                        add_tokens(dve, t - 1, seq(-1), 0)
                    norm(dve, t, u, half)
                tiles(dve, step)
                add_tokens(dve, LAST - 1, 1, 1)
                slot_maxima(dve, LAST, 1)
                slot_sums(dve, LAST, 1)
                for m in range(SM):
                    add_tokens(dve, LAST, 1, m)

            @block.gpsimd
            def _(pool):
                pool.wait_ge(s["ob_in"], 16)
                add_bias(pool, 0, 0, 0)

                def step(t, u, half, seq):
                    if ahead(t, 1):
                        add_bias(pool, t + 1, 1 - u, half + u)
                tiles(pool, step)


ROWS = BATCH * SLOTS
EXTRA = 3


def experts_stage(nc, io, hold, ring, ring_in):
    with Stage(nc, "exp") as st:
        dwv, dwo = hold["dwv"], hold["dwo"]
        dbv = st.sb("dbv", [P, GROUPS])
        rsum = st.sb("rsum", [P, BATCH, SM])
        znT = st.sb("znT", [P, KC, BATCH, SROWS])
        aoT = st.sb("aoT", [P, GROUPS, BATCH, SLOTS])
        o = st.sb("o", [ROWS, D])
        stats = st.sb("stats", [ROWS, 1, 12])
        hT = st.sb("hT", [P, KC, ROWS])
        pick = st.sb("pick", [P, EXPERTS, ROWS])
        fold = st.sb("fold", [P, ROWS])
        hm = [st.sb(f"hm{i}", [P, KC, ROWS]) for i in range(2)]
        pm = [st.sb(f"pm{i}", [P, 4, ROWS]) for i in range(2)]
        quarter = st.sb("quarter", [P, 4, ROWS])
        bias = [st.sb(f"bias{i}", [P, 2, FQ]) for i in range(2)]
        up = st.sb("up", [P, FQ])
        gate = st.sb("gate", [P, FQ])
        gu = st.sb("gu", [P, FQ])
        guT = st.sb("guT", [P, 4, P])
        cbo = st.sb("cbo", [P, D])
        cbqb = st.sb("cbqb", [P, GROUPS, P])
        extra = [st.sb(f"extra{i}", [P, UNIT]) for i in range(EXTRA - 1)] + [hold["late"]]
        slot, dbo, ln_g, b2 = up[0:ROWS, :], gate[0:ROWS, :], gu[0:ROWS, :], cbo[0:ROWS, :]
        ln_b = guT[0:ROWS, :, :].rearrange("p i r -> p (i r)")
        h = cbqb[0:ROWS, :, :].rearrange("p g r -> p (g r)")
        cwk, cwqT = dwv, dwo
        cwv = shaped(znT[:].rearrange("p k b r -> p (k b r)"), [P, KC, D])
        cwo = shaped(hold["z"][:].rearrange("p b m d -> p (b m d)"), [P, KC, D])
        VO_BANKS = (4, 5, 7, 0)
        cbk = st.sb("cbk", [P, GROUPS])
        cbv = st.sb("cbv", [P, GROUPS])
        cbq = st.sb("cbq", [P, GROUPS])
        y4, k4, v4 = bias[0][:, 0, :], up, gate
        oT = hT
        kbd = shaped(gu[:], [P, GROUPS, BATCH, HG, SLOTS])
        vbd = shaped(guT[:].rearrange("p i r -> p (i r)"), [P, GROUPS, BATCH, HG, SLOTS])
        bank = st.banks()
        slot_w_in = hold["slot_w_in"]
        s = st.sems("dbv_in", "rows_in", "comb_w_in", "zeros", "consts", "rsum_done", "zn_done", "zn_turned", "znT_done", "ao_done", "aoT_done",
                    "wo_done", "o_step", "ln_step", "h_turned", "hT_done", "hm_done", "up_done", "silu_done", "gu_done",
                    "gu_turned", "guT_done", "y4_done", "o_turned", "oT_done",
                    "k4_done", "k4_out", "v4_done", "v4_out", "k_done", "kbd_done", "v_done", "vbd_done", "qb_done", "m2_done", "m2_out", "kb_done", "vo_done", "vo_out")
        unit_used = [st.sem(f"unit_used{i}") for i in range(UNITS)]
        bias_in = st.pair("bias_in")
        extra_in = [st.sem(f"extra_in{i}") for i in range(EXTRA)]

        def uses(unit, e):
            skipped = unit < EXTRA and not (isinstance(e, int) and e < 2)
            return e - 1 if skipped else e

        def unit_of(pe, e, unit):
            if isinstance(e, int) and e == 1 and unit < EXTRA:
                pe.wait_ge(extra_in[unit], 16)
                return extra[unit][:]
            pe.wait_ge(ring_in[unit], 16 * (uses(unit, e) + 1))
            return ring[:, unit, :]

        def release(last, e, unit):
            if not (isinstance(e, int) and e == 1 and unit < EXTRA):
                last.then_inc(unit_used[unit], 1)

        def expert(pe, e, u, half):
            pe.wait_ge(s["hm_done"], e + 1)
            wait_later(pe, s["silu_done"], 2 * e)
            for w in range(2):
                for k in range(KC):
                    if k % 2 == 0:
                        weights = unit_of(pe, e, 2 * w + k // 2)
                    for q in range(4):
                        at = (k % 2) * F + q * FQ
                        last = nc.tensor.matmul(bank[w][q * ROWS:(q + 1) * ROWS, :], hm[u][:, k, :], weights[:, at:at + FQ],
                                                start=(k == 0), stop=False)
                    if k % 2 == 1:
                        release(last, e, 2 * w + k // 2)
                if w == 0:
                    pe.wait_ge(bias_in[u], 32 * (half + 1))
                for q in range(4):
                    last = nc.tensor.matmul(bank[w][q * ROWS:(q + 1) * ROWS, :], pm[u][:, q, :], bias[u][:, w, :], start=False, stop=True)
                last.then_inc(s["up_done"], 1)
            pe.wait_ge(s["gu_done"], e + 1)
            wait_later(pe, s["guT_done"], e)
            for i in range(4):
                last = nc.tensor.transpose(bank[2][:, i * P:(i + 1) * P], gu[:].rearrange("r (p i) -> r i p", i=4)[:, i, :], hold["ident"][:])
            last.then_inc(s["gu_turned"], 1)
            pe.wait_ge(s["guT_done"], e + 1)
            first = isinstance(e, int) and e == 0
            final = isinstance(e, int) and e == EXPERTS - 1
            for half in range(2):
                weights = unit_of(pe, e, 4 + half)
                for i in range(4):
                    for j in range(2):
                        q = 2 * half + j
                        last = nc.tensor.matmul(bank[3][q * ROWS:(q + 1) * ROWS, :], guT[:, i, q * ROWS:(q + 1) * ROWS],
                                                weights[:, (j * 4 + i) * D:(j * 4 + i + 1) * D],
                                                start=first and i == 0, stop=final and i == 3, skip_group_check=True)
                release(last, e, 4 + half)

        def masked(dve, e, u):
            wait_later(dve, s["up_done"], 2 * e - 2)
            nc.vector.tensor_tensor(hm[u][:], hT[:], broadcast(pick[:, bass.ds(e, 1), :], [P, KC, ROWS]), ALU.mult)
            nc.vector.tensor_tensor(pm[u][:], quarter[:], broadcast(pick[:, bass.ds(e, 1), :], [P, 4, ROWS]), ALU.mult).then_inc(s["hm_done"], 1)

        def combine_up(dve, e):
            dve.wait_ge(s["silu_done"], 2 * e + 2)
            wait_later(dve, s["gu_turned"], e)
            nc.vector.tensor_tensor(gu[:], up[:], gate[:], ALU.mult).then_inc(s["gu_done"], 1)
            dve.wait_ge(s["gu_turned"], e + 1)
            wait_later(dve, unit_used[5], e)
            nc.vector.tensor_copy(guT[:].rearrange("p i r -> p (i r)"), bank[2][:]).then_inc(s["guT_done"], 1)

        def activate(act, e):
            wait_later(act, s["gu_done"], e)
            for w, dst in ((0, up), (1, gate)):
                act.wait_ge(s["up_done"], 2 * e + w + 1)
                nc.scalar.activation(dst[:], bank[w][:], ACT.Silu).then_inc(s["silu_done"], 1)

        def experts(eng, body):
            for e in (0, 1):
                body(e, e, 0)
            with eng.Fori(1, EXPERTS // 2 - 1) as i:
                for u in (0, 1):
                    body(2 * i + u, u, i)
            for e in (EXPERTS - 2, EXPERTS - 1):
                body(e, e % 2, e // 2)

        with nc.Block() as block:
            @block.sync
            def _(sp):
                sp.dma_start(dbv[:], io["d_bv"]).then_inc(s["dbv_in"], 16)
                sp.dma_start(dbo, broadcast(io["d_bo"].rearrange("(o n) -> o n", o=1), [ROWS, D])).then_inc(s["rows_in"], 16)
                for dst, src in ((slot, io["slot"]), (ln_g, io["e_ln_g"]), (ln_b, io["e_ln_b"]), (b2, io["e_b2"])):
                    for b in range(BATCH):
                        sp.dma_start(dst[b * SLOTS:(b + 1) * SLOTS, :], src).then_inc(s["rows_in"], 16)
                for unit in range(EXTRA):
                    fetch_unit(sp, io, extra[unit][:], extra_in[unit], 1, unit)

                def step(e, u, half):
                    if isinstance(e, int) and e == 0:
                        return
                    for unit in range(UNITS):
                        if isinstance(e, int) and e == 1 and unit < EXTRA:
                            continue
                        sp.wait_ge(unit_used[unit], uses(unit, e))
                        prefetch(sp, io, ring, ring_in, e, unit)
                    if isinstance(e, int) and e == 1:
                        sp.wait_ge(s["o_step"], 5)
                        for dst, src in ((cwk, io["c_Wk"]), (cwqT, io["c_WqT"]), (cwv, io["c_Wv"]), (cwo, io["c_Wo"])):
                            sp.dma_start(dst[:], src.rearrange("(k p) n -> p k n", p=P)).then_inc(s["comb_w_in"], 16)
                        for dst, src in ((cbk, io["c_bk"]), (cbv, io["c_bv"]), (cbq, io["c_bq"]),
                                         (cbo, broadcast(io["c_bo"].rearrange("(o n) -> o n", o=1), [P, D]))):
                            sp.dma_start(dst[:], src).then_inc(s["comb_w_in"], 16)
                experts(sp, step)
                sp.wait_ge(unit_used[0], EXPERTS - 1)
                fetch_turned(sp, io, hold, 0, 0)
                fetch_turned(sp, io, hold, 1, 1)
                fetch_tokens(sp, io, hold, 0, 0)

            @block.gpsimd
            def _(pool):
                nc.gpsimd.memset(pick[:], 0.0).then_inc(s["zeros"], 1)
                nc.gpsimd.memset(fold[:], 0.0).then_inc(s["zeros"], 1)
                for i in range(2):
                    nc.gpsimd.memset(bias[i][:], 0.0).then_inc(s["zeros"], 1)
                nc.gpsimd.memset(quarter[:], 0.0).then_inc(s["zeros"], 1)
                pool.wait_ge(s["zeros"], 5)
                nc.gpsimd.affine_select(out=quarter[:], in_=quarter[:], compare_op=ALU.not_equal, fill=1.0, base=0,
                                        pattern=[[-1, 4], [0, ROWS]], channel_multiplier=1).then_inc(s["consts"], 1)
                p4 = pick[:].rearrange("p e (b r) -> p e b r", b=BATCH)
                nc.gpsimd.affine_select(out=p4, in_=p4, compare_op=ALU.not_equal, fill=1.0, base=0,
                                        pattern=[[1, EXPERTS], [0, BATCH], [-1, SLOTS]], channel_multiplier=0).then_inc(s["consts"], 1)
                for q in range(4):
                    nc.gpsimd.affine_select(out=fold[:], in_=fold[:], compare_op=ALU.not_equal, fill=1.0, base=-q * ROWS,
                                            pattern=[[-1, ROWS]], channel_multiplier=1).then_inc(s["consts"], 1)
                    pool.wait_ge(s["consts"], q + 3)

                def step(e, u, half):
                    wait_later(pool, s["up_done"], 2 * e - 2)
                    for w, src in ((0, io["e_b1"]), (1, io["e_bg"])):
                        pool.dma_start(bias[u][0:4, w, :], src.rearrange("e (q f) -> e q f", q=4)[bass.ds(e, 1), :, :].rearrange("o q f -> (o q) f")).then_inc(bias_in[u], 16)
                experts(pool, step)
                pool.wait_ge(s["comb_w_in"], 8 * 16)
                pool.wait_ge(s["hT_done"], 1)
                nc.gpsimd.tensor_copy(cbqb[:], broadcast(cbq[:].unsqueeze(2), [P, GROUPS, P])).then_inc(s["qb_done"], 1)
                pool.wait_ge(unit_used[5], EXPERTS)
                nc.gpsimd.memset(kbd[:], 0.0).then_inc(s["zeros"], 1)
                nc.gpsimd.memset(vbd[:], 0.0).then_inc(s["zeros"], 1)

            @block.tensor
            def _(pe):
                for b in range(BATCH):
                    for m in range(SM):
                        i = b * SM + m
                        pe.wait_ge(s["zn_done"], i + 1)
                        for k in range(KC):
                            last = nc.tensor.transpose(bank[i][:, k * P:(k + 1) * P], hold["z"][:, b, m, k * P:(k + 1) * P], hold["ident"][:])
                        last.then_inc(s["zn_turned"], 1)
                pe.wait_ge(slot_w_in, 2 * 16)
                pe.wait_ge(s["znT_done"], 4)
                for g in range(GROUPS):
                    for k in range(KC):
                        last = nc.tensor.matmul(bank[4][:, g * P:(g + 1) * P], dwv[:, k, g * P:(g + 1) * P],
                                                znT[:, k, :, g * HG * SLOTS:(g + 1) * HG * SLOTS], start=(k == 0), stop=(k == KC - 1))
                last.then_inc(s["ao_done"], 1)
                pe.wait_ge(s["aoT_done"], 1)
                for g in range(GROUPS):
                    last = nc.tensor.matmul(bank[5][0:ROWS, :], aoT[:, g, :, :], dwo[:, g, :], start=(g == 0), stop=(g == GROUPS - 1))
                last.then_inc(s["wo_done"], 1)
                pe.wait_ge(s["o_step"], 4)
                for k in range(KC):
                    last = nc.tensor.transpose(bank[6][:, k * ROWS:(k + 1) * ROWS], h.rearrange("r (p k) -> r k p", k=KC)[:, k, :],
                                               hold["ident"][0:ROWS, 0:ROWS])
                last.then_inc(s["h_turned"], 1)
                experts(pe, lambda e, u, half: expert(pe, e, u, half))
                pe.wait_ge(s["o_step"], 5)
                pe.wait_ge(s["y4_done"], 1)
                for k in range(KC):
                    out = bank[5][:, k * ROWS:(k + 1) * ROWS]
                    nc.tensor.matmul(out, o[:, k * P:(k + 1) * P], hold["ident"][0:ROWS, 0:ROWS], start=True, stop=False)
                    last = nc.tensor.matmul(out, y4[:, k * P:(k + 1) * P], fold[:], start=False, stop=True)
                last.then_inc(s["o_turned"], 1)
                pe.wait_ge(s["comb_w_in"], 8 * 16)
                pe.wait_ge(s["oT_done"], 1)
                for w, bk, sem in ((cwk, bank[6], s["k4_done"]), (cwv, bank[7], s["v4_done"])):
                    for k in range(KC):
                        last = nc.tensor.matmul(bk[k * ROWS:(k + 1) * ROWS, :], oT[:, k, :], w[:, k, :], start=True, stop=True)
                    last.then_inc(sem, 1)
                for src, bk, ready, sem in ((k4, bank[4], s["k4_out"], s["k_done"]), (v4, bank[5], s["v4_out"], s["v_done"])):
                    pe.wait_ge(ready, 1)
                    for g in range(GROUPS):
                        last = nc.tensor.matmul(bk[:, g * ROWS:(g + 1) * ROWS], src[:, g * P:(g + 1) * P], fold[:], start=True, stop=True)
                    last.then_inc(sem, 1)
                pe.wait_ge(s["kbd_done"], 1)
                for k in range(KC):
                    for g in range(GROUPS):
                        last = nc.tensor.matmul(bank[k][:, g * P:(g + 1) * P], cwqT[:, g, k * P:(k + 1) * P], kbd[:, g, :, :, :], start=True, stop=True)
                    last.then_inc(s["m2_done"], 1)
                pe.wait_ge(s["qb_done"], 1)
                pe.wait_ge(s["k4_out"], 1)
                for g in range(GROUPS):
                    last = nc.tensor.matmul(bank[6][:, g * P:(g + 1) * P], cbqb[:, g, :], kbd[:, g, :, :, :], start=True, stop=True)
                last.then_inc(s["kb_done"], 1)
                pe.wait_ge(s["vbd_done"], 1)
                pe.wait_ge(s["v4_out"], 1)
                half = HG * SLOTS
                for b in range(BATCH):
                    for m in range(SM):
                        out = bank[VO_BANKS[b * SM + m]]
                        if b * SM + m == 3:
                            pe.wait_ge(s["m2_out"], 1)
                        for j in range(2):
                            last = nc.tensor.matmul(out[j * half:(j + 1) * half, :], vbd[:, 2 * m + j, b, :, :], cwo[:, 2 * m + j, :], start=True, stop=True)
                        last.then_inc(s["vo_done"], 1)

            @block.scalar
            def _(act):
                for i in range(BATCH * SM):
                    act.wait_ge(s["zn_turned"], i + 1)
                    nc.scalar.activation(znT[:, :, i // SM, (i % SM) * P:(i % SM + 1) * P], bank[i][:].rearrange("p (k r) -> p k r", k=KC),
                                         ACT.Copy).then_inc(s["znT_done"], 1)
                experts(act, lambda e, u, half: activate(act, e))
                act.wait_ge(s["k4_done"], 1)
                nc.scalar.activation(k4[:], bank[6][:], ACT.Copy).then_inc(s["k4_out"], 1)
                for k in range(KC):
                    act.wait_ge(s["m2_done"], k + 1)
                    nc.scalar.activation(hold["m2"][:, :, k, :].rearrange("p b (g r) -> p g b r", g=GROUPS),
                                         bank[k][:].rearrange("p (g b r) -> p g b r", g=GROUPS, b=BATCH), ACT.Copy).then_inc(s["m2_out"], 1)
                act.wait_ge(s["kb_done"], 1)
                nc.scalar.activation(hold["kb2"][:].rearrange("p b g r -> p g b r"), bank[6][:].rearrange("p (g b r) -> p g b r", g=GROUPS, b=BATCH),
                                     ACT.Copy, scale=SCALE).then_inc(s["m2_out"], 1)

            @block.vector
            def _(dve):
                nc.vector.reciprocal(rsum[:], hold["sum"][:]).then_inc(s["rsum_done"], 1)
                dve.wait_ge(s["rsum_done"], 1)
                for b in range(BATCH):
                    for m in range(SM):
                        nc.vector.tensor_scalar(hold["z"][:, b, m, :], hold["z"][:, b, m, :], rsum[:, b, m:m + 1], None, ALU.mult).then_inc(s["zn_done"], 1)
                dve.wait_ge(s["rows_in"], 9 * 16)
                nc.vector.tensor_tensor(slot, slot, dbo, ALU.add).then_inc(s["o_step"], 1)
                dve.wait_ge(s["dbv_in"], 16)
                dve.wait_ge(s["ao_done"], 1)
                for hh in range(HG):
                    r = slice(hh * HD, (hh + 1) * HD)
                    src = bank[4][r, :].rearrange("p (gb h q) -> p gb h q", h=HG, q=SLOTS)[:, :, hh, :].rearrange("p (g b) q -> p g b q", g=GROUPS)
                    last = nc.vector.tensor_tensor(aoT[r, :, :, :], src,
                                                   broadcast(dbv[r, :].unsqueeze(2).unsqueeze(3), [HD, GROUPS, BATCH, SLOTS]), ALU.add)
                last.then_inc(s["aoT_done"], 1)
                dve.wait_ge(s["o_step"], 1)
                dve.wait_ge(s["wo_done"], 1)
                nc.vector.tensor_tensor(o[:], bank[5][0:ROWS, :], slot, ALU.add).then_inc(s["o_step"], 1)
                dve.wait_ge(s["o_step"], 2)
                layernorm(nc, dve, s["ln_step"], 0, [o[:]], stats, [h]).then_inc(s["ln_step"], 1)
                dve.wait_ge(s["ln_step"], LN_STEPS + 1)
                nc.vector.tensor_tensor(h, h, ln_g, ALU.mult).then_inc(s["o_step"], 1)
                dve.wait_ge(s["o_step"], 3)
                nc.vector.tensor_tensor(h, h, ln_b, ALU.add).then_inc(s["o_step"], 1)
                nc.vector.tensor_tensor(o[:], o[:], b2, ALU.add).then_inc(s["o_step"], 1)
                dve.wait_ge(s["h_turned"], 1)
                nc.vector.tensor_copy(hT[:].rearrange("p k r -> p (k r)"), bank[6][:, 0:KC * ROWS]).then_inc(s["hT_done"], 1)
                dve.wait_ge(s["hT_done"], 1)
                dve.wait_ge(s["consts"], 6)
                masked(dve, 0, 0)

                def step(e, u, half):
                    if not (isinstance(e, int) and e == EXPERTS - 1):
                        masked(dve, e + 1, 1 - u)
                    combine_up(dve, e)
                experts(dve, step)
                dve.wait_ge(unit_used[5], EXPERTS)
                nc.vector.tensor_copy(y4, bank[3][:]).then_inc(s["y4_done"], 1)
                dve.wait_ge(s["o_turned"], 1)
                dve.wait_ge(s["hm_done"], EXPERTS)
                nc.vector.tensor_copy(oT[:].rearrange("p k r -> p (k r)"), bank[5][:, 0:KC * ROWS]).then_inc(s["oT_done"], 1)
                dve.wait_ge(s["v4_done"], 1)
                nc.vector.tensor_copy(v4[:], bank[7][:]).then_inc(s["v4_out"], 1)
                dve.wait_ge(s["comb_w_in"], 8 * 16)
                dve.wait_ge(s["zeros"], 7)
                for src, dst, bias_, ready, done in ((bank[4], kbd, cbk, s["k_done"], s["kbd_done"]), (bank[5], vbd, cbv, s["v_done"], s["vbd_done"])):
                    dve.wait_ge(ready, 1)
                    for hh in range(HG):
                        r = slice(hh * HD, (hh + 1) * HD)
                        last = nc.vector.tensor_tensor(dst[r, :, :, hh, :], src[r, 0:GROUPS * ROWS].rearrange("p (g b q) -> p g b q", g=GROUPS, b=BATCH),
                                                       broadcast(bias_[r, :].unsqueeze(2).unsqueeze(3), [HD, GROUPS, BATCH, SLOTS]), ALU.add)
                    last.then_inc(done, 1)
                for i in range(BATCH * SM):
                    dve.wait_ge(s["vo_done"], i + 1)
                    nc.vector.scalar_tensor_tensor(hold["vo"][:, i // SM, i % SM, :], cbo[:], 1.0 / HEADS, bank[VO_BANKS[i]][:],
                                                   ALU.mult, ALU.add).then_inc(s["vo_out"], 1)


T2 = 2


def fetch_turned(sp, io, hold, i, u):
    sp.dma_start(hold["x2T"][u][:].rearrange("p t k n -> p t (k n)"),
                 io["x2T"].rearrange("(t p) n -> p t n", p=P)[:, bass.ds(i * T2, T2), :]).then_inc(hold["x2T_in"][u], 16)


def fetch_tokens(sp, io, hold, i, u):
    sp.dma_start(hold["x2"][u][:], io["x2"].rearrange("(t p) n -> p t n", p=P)[:, bass.ds(i * T2, T2), :]).then_inc(hold["x2_in"][u], 16)


def combine_stage(nc, io, hold):
    with Stage(nc, "cmb") as st:
        STEPS = TILES // T2
        PER_SEQ = STEPS // BATCH
        x2T, x2, x2T_in, x2_in = hold["x2T"], hold["x2"], hold["x2T_in"], hold["x2_in"]
        sc = [st.sb(f"sc{i}", [P, T2, SROWS]) for i in range(2)]
        pr = [st.sb(f"pr{i}", [P, T2, SROWS]) for i in range(2)]
        top = [st.sb(f"top{i}", [P, T2 * HEADS]) for i in range(2)]
        den = st.sb("den", [P, T2 * HEADS])
        rden = [st.sb(f"rden{i}", [P, T2 * HEADS]) for i in range(2)]
        prT = [st.sb(f"prT{i}", [P, T2, SM, P]) for i in range(2)]
        xr = [st.sb(f"xr{i}", [P, T2, D]) for i in range(2)]
        stats = [st.sb(f"stats{i}", [P, T2, 12]) for i in range(2)]
        out = [st.sb(f"out{i}", [P, T2, D]) for i in range(2)]
        bank = st.banks()
        s = st.sems("sc_done", "sc_out", "top_done", "shifted", "exp_done", "den_done", "rden_done", "normed", "pr_turned", "prT_done",
                    "o_done", "res_done", "ln_step", "stats_done", "out_done")
        stored = st.pair("stored")
        LAST = STEPS - 1
        out_v = io["out"].rearrange("(t p) n -> p t n", p=P)

        def load_turned(sp, i, u):
            wait_later(sp, s["sc_done"], i - 1)
            fetch_turned(sp, io, hold, i, u)

        def load_tokens(sp, i, u):
            wait_later(sp, s["res_done"], i - 1)
            fetch_tokens(sp, io, hold, i, u)

        def store(sp, i, u):
            sp.wait_ge(s["out_done"], i + 1)
            sp.dma_start(out_v[:, bass.ds(i * T2, T2), :], out[u][:]).then_inc(stored[u], 16)

        def score(pe, i, u, half, b):
            pe.wait_ge(x2T_in[u], 16 * (half + 1))
            wait_later(pe, s["sc_out"], i - 1)
            for j in range(T2):
                for k in range(KC):
                    last = nc.tensor.matmul(bank[u][:, j * SROWS:(j + 1) * SROWS], x2T[u][:, j, k, :], hold["m2"][:, b, k, :],
                                            start=(k == 0), stop=(k == KC - 1))
            last.then_inc(s["sc_done"], 1)

        def turn(pe, i, u):
            pe.wait_ge(s["normed"], i + 1)
            wait_later(pe, s["prT_done"], i - 1)
            for j in range(T2):
                for m in range(SM):
                    at = (j * SM + m) * P
                    last = nc.tensor.transpose(bank[2 + u][:, at:at + P], pr[u][:, j, m * P:(m + 1) * P], hold["ident"][:])
            last.then_inc(s["pr_turned"], 1)

        def project_out(pe, i, u, b):
            pe.wait_ge(s["prT_done"], i + 1)
            wait_later(pe, s["res_done"], i - 1)
            for j in range(T2):
                for m in range(SM):
                    last = nc.tensor.matmul(bank[4 + 2 * u + j][:], prT[u][:, j, m, :], hold["vo"][:, b, m, :], start=(m == 0), stop=(m == SM - 1))
                last.then_inc(s["o_done"], 1)

        def take_scores(dve, i, u, b):
            dve.wait_ge(s["sc_done"], i + 1)
            wait_later(dve, s["shifted"], i - 1)
            nc.vector.scalar_tensor_tensor(sc[u][:], bank[u][:].rearrange("p (t r) -> p t r", t=T2), SCALE,
                                           broadcast(hold["kb2"][:, b, :, :].rearrange("p g r -> p (g r)").unsqueeze(1), [P, T2, SROWS]),
                                           ALU.mult, ALU.add).then_inc(s["sc_out"], 1)
            dve.wait_ge(s["sc_out"], i + 1)
            nc.vector.tensor_reduce(top[u][:], sc[u][:].rearrange("p t (h q) -> p (t h) q", q=SLOTS), AX.X, ALU.max).then_inc(s["top_done"], 1)

        def denominators(dve, i, u):
            dve.wait_ge(s["exp_done"], i + 1)
            nc.vector.tensor_reduce(den[:], pr[u][:].rearrange("p t (h q) -> p (t h) q", q=SLOTS), AX.X, ALU.add).then_inc(s["den_done"], 1)
            dve.wait_ge(s["den_done"], i + 1)
            wait_later(dve, s["normed"], i - 1)
            nc.vector.reciprocal(rden[u][:], den[:]).then_inc(s["rden_done"], 1)

        def residual(dve, i, u, half):
            dve.wait_ge(x2_in[u], 16 * (half + 1))
            wait_later(dve, s["out_done"], i - 1)
            for j in range(T2):
                dve.wait_ge(s["o_done"], T2 * i + j + 1)
                last = nc.vector.tensor_tensor(xr[u][:, j, :], bank[4 + 2 * u + j][:], x2[u][:, j, :], ALU.add)
            last.then_inc(s["res_done"], 1)
            dve.wait_ge(s["res_done"], i + 1)
            norm_factors(nc, dve, s["ln_step"], LN_STEPS * i, [xr[u][:, j, :] for j in range(T2)], stats[u])
            nc.vector.scalar_tensor_tensor(stats[u][:, :, 11:12], stats[u][:, :, 6:7], -1.0, stats[u][:, :, 9:10], ALU.mult, ALU.mult).then_inc(s["stats_done"], 1)

        def exponents(act, i, u):
            act.wait_ge(s["shifted"], i + 1)
            nc.scalar.activation(pr[u][:], pr[u][:], ACT.Exp).then_inc(s["exp_done"], 1)

        def take_turned(act, i, u):
            act.wait_ge(s["pr_turned"], i + 1)
            wait_later(act, s["o_done"], T2 * (i - 1))
            nc.scalar.activation(prT[u][:].rearrange("p t m r -> p (t m r)"), bank[2 + u][:], ACT.Copy).then_inc(s["prT_done"], 1)

        def normalise(act, i, u, half):
            act.wait_ge(s["stats_done"], i + 1)
            wait_later(act, stored[u], 16 * half)
            for j in range(T2):
                last = nc.scalar.activation(out[u][:, j, :], xr[u][:, j, :], ACT.Identity, bias=stats[u][:, j, 11:12], scale=stats[u][:, j, 9:10])
            last.then_inc(s["out_done"], 1)

        def softmax_shift(pool, i, u):
            pool.wait_ge(s["top_done"], i + 1)
            wait_later(pool, s["pr_turned"], i - 1)
            nc.gpsimd.tensor_tensor(pr[u][:].rearrange("p t (h q) -> p (t h) q", q=SLOTS), sc[u][:].rearrange("p t (h q) -> p (t h) q", q=SLOTS),
                                    broadcast(top[u][:].unsqueeze(2), [P, T2 * HEADS, SLOTS]), ALU.subtract).then_inc(s["shifted"], 1)

        def softmax_norm(pool, i, u):
            pool.wait_ge(s["rden_done"], i + 1)
            nc.gpsimd.tensor_tensor(pr[u][:].rearrange("p t (h q) -> p (t h) q", q=SLOTS), pr[u][:].rearrange("p t (h q) -> p (t h) q", q=SLOTS),
                                    broadcast(rden[u][:].unsqueeze(2), [P, T2 * HEADS, SLOTS]), ALU.mult).then_inc(s["normed"], 1)

        def steps(eng, body):
            def alone(*ts):
                for i in ts:
                    body(i, i % 2, i // 2, lambda d, i=i: (i + d) // PER_SEQ)

            def loop(first, end, b):
                with eng.Fori(first // 2, end // 2) as p:
                    for u in (0, 1):
                        body(2 * p + u, u, p, lambda d: b)
            alone(0, 1)
            loop(2, PER_SEQ - 2, 0)
            alone(PER_SEQ - 2, PER_SEQ - 1)
            loop(PER_SEQ, STEPS - 4, 1)
            alone(*range(STEPS - 4, STEPS))

        def before(i, n):
            return not isinstance(i, int) or i >= n

        def ahead(i, n):
            return not isinstance(i, int) or i + n <= LAST

        with nc.Block() as block:
            @block.sync
            def _(sp):
                load_turned(sp, 2, 0)

                def step(i, u, half, seq):
                    if ahead(i, 3):
                        load_turned(sp, i + 3, 1 - u)
                    if ahead(i, 1):
                        load_tokens(sp, i + 1, 1 - u)
                    if before(i, 1):
                        store(sp, i - 1, 1 - u)
                steps(sp, step)
                store(sp, LAST, 1)
                for u in range(2):
                    sp.wait_ge(stored[u], 16 * STEPS // 2)

            @block.tensor
            def _(pe):
                score(pe, 0, 0, 0, 0)
                score(pe, 1, 1, 0, 0)
                turn(pe, 0, 0)

                def step(i, u, half, seq):
                    if ahead(i, 2):
                        score(pe, i + 2, u, half + 1, seq(2))
                    project_out(pe, i, u, seq(0))
                    if ahead(i, 1):
                        turn(pe, i + 1, 1 - u)
                steps(pe, step)

            @block.scalar
            def _(act):
                exponents(act, 0, 0)
                exponents(act, 1, 1)
                take_turned(act, 0, 0)

                def step(i, u, half, seq):
                    if ahead(i, 2):
                        exponents(act, i + 2, u)
                    if ahead(i, 1):
                        take_turned(act, i + 1, 1 - u)
                    normalise(act, i, u, half)
                steps(act, step)

            @block.vector
            def _(dve):
                for i in (0, 1):
                    take_scores(dve, i, i, 0)
                    denominators(dve, i, i)

                def step(i, u, half, seq):
                    if ahead(i, 2):
                        take_scores(dve, i + 2, u, seq(2))
                    residual(dve, i, u, half)
                    if ahead(i, 2):
                        denominators(dve, i + 2, u)
                steps(dve, step)

            @block.gpsimd
            def _(pool):
                for i in (0, 1):
                    softmax_shift(pool, i, i)
                    softmax_norm(pool, i, i)

                def step(i, u, half, seq):
                    if ahead(i, 2):
                        softmax_shift(pool, i + 2, u)
                        softmax_norm(pool, i + 2, u)
                steps(pool, step)


def decoder_layer(nc, io):
    with Stage(nc, "all") as keep:
        ring = keep.sb("ring", [P, UNITS, UNIT])
        ring_in = [nc.alloc_semaphore(f"ring_in{i}") for i in range(UNITS)]
        hold = dict(
            arena=ring[:].rearrange("p u n -> p (u n)"),
            ident=keep.sb("ident", [P, P]),
            tri=keep.sb("tri", [P, P]),
            kbias=keep.sb("kbias", [P, SM]),
            top=keep.sb("top", [P, BATCH, SM]),
            sum=keep.sb("sum", [P, BATCH, SM]),
            z=keep.sb("z", [P, BATCH, SM, D]),
            dwv=keep.sb("dwv", [P, KC, D]),
            dwo=keep.sb("dwo", [P, KC, D]),
            slot_w_in=nc.alloc_semaphore("slot_w_in"),
        )
        with Stage(nc, "att") as att:
            hold["mask"] = att.sb("mask", [P, CTX])
            hold["kbd"] = att.sb("kbd", [P, BATCH, GROUPS, HG, CTX])
            hold["vbd"] = att.sb("vbd", [PIECE, BATCH, 3, GROUPS, P])
            hold["m1"] = att.sb("m1", [P, KC, SROWS])
            hold["q_w"] = att.sb("q_w", [P, KC, D])
            hold["o_w"] = att.sb("o_w", [P, KC, D])
            hold["qbias"] = att.sb("qbias", [P, GROUPS])
            hold["cross_in"] = att.sem("cross_in")
            with Stage(nc, "mxw") as mxw:
                hold["win"] = mxw.sb("win", [P, KC, CONV])
                hold["wout"] = mxw.sb("wout", [P, KC, D])
                hold["taps"] = mxw.sb("taps", [P, CT, TAPS])
                hold["convb"] = mxw.sb("convb", [P, CT])
                hold["decay"] = mxw.sb("decay", [P, CHUNKS, HEADS])
                hold["rate"] = mxw.sb("rate", [P, BATCH, CHUNKS, HEADS])
                hold["conv"] = [shaped(hold["arena"][:, RESERVED + i * CT * P:RESERVED + (i + 1) * CT * P], [P, CT, P]) for i in range(2)]
                hold["product"] = [mxw.sb(f"product{i}", [P, 4, P]) for i in range(2)]
                hold["proj"] = [shaped(w[:].rearrange("p k n -> p (k n)")[:, 0:CT * (HALO + P)], [P, CT, HALO + P]) for w in (hold["dwv"], hold["dwo"])]
                hold["mixer_in"] = mxw.sem("mixer_in")
                hold["mix"] = mxw.sems(*MIXER_SEMS)
                tables_stage(nc, io, hold)
                mixer_stage(nc, io, hold)
            cross_stage(nc, io, hold, ring, ring_in)
        with Stage(nc, "slt") as slt:
            late = slt.sb("late", [P, UNIT])
            n = BATCH * KC * SROWS
            hold["late"] = late
            hold["m2"] = shaped(late[:, 0:n], [P, BATCH, KC, SROWS])
            hold["vo"] = shaped(late[:, n:n + BATCH * SM * D], [P, BATCH, SM, D])
            hold["kb2"] = slt.sb("kb2", [P, BATCH, GROUPS, HG * SLOTS])
            free = ring[:, 0, :]
            n = T2 * D
            hold["x2T"] = [shaped(free[:, i * n:(i + 1) * n], [P, T2, KC, P]) for i in range(2)]
            hold["x2"] = [shaped(free[:, (2 + i) * n:(3 + i) * n], [P, T2, D]) for i in range(2)]
            hold["x2T_in"], hold["x2_in"] = slt.pair("x2T_in"), slt.pair("x2_in")
            experts_stage(nc, io, hold, ring, ring_in)
            combine_stage(nc, io, hold)


INPUTS = {"conv_w": "L0_attn_conv_w", "conv_b": "L0_attn_conv_b", "A_param": "L0_attn_A_param", "dt_bias": "L0_attn_dt_bias",
          "q_w": "L0_xattn_q_w", "q_b": "L0_xattn_q_b", "k_w": "L0_xattn_k_w", "k_b": "L0_xattn_k_b", "v_w": "L0_xattn_v_w",
          "v_b": "L0_xattn_v_b", "o_w": "L0_xattn_o_w", "o_b": "L0_xattn_o_b"}
for _n in ("d_Wq", "d_Wv", "d_Wo", "d_bq", "d_bk", "d_bv", "d_bo", "c_Wk", "c_Wv", "c_Wo", "c_bq", "c_bk", "c_bv", "c_bo",
           "e_ln_g", "e_ln_b", "e_W1", "e_b1", "e_Wg", "e_bg", "e_W2", "e_b2"):
    INPUTS[_n] = "L0_ffn_" + _n


def kernel(**inputs):
    import concourse.bacc as bacc
    import numpy as np
    from concourse.bass_utils import run_bass_kernel_spmd

    x = np.asarray(inputs["x"]).reshape(TOKENS, D)
    arrays = {name: np.ascontiguousarray(inputs[of]) for name, of in INPUTS.items()}
    arrays["x"] = np.ascontiguousarray(x)
    arrays["xT"] = np.ascontiguousarray(x.T)
    arrays["ctxT"] = np.ascontiguousarray(np.asarray(inputs["ctx_1024"]).reshape(BATCH * CTX, D).T)
    arrays["WinT"] = np.ascontiguousarray(np.asarray(inputs["L0_attn_W_in"]).T)
    arrays["WoutT"] = np.ascontiguousarray(np.asarray(inputs["L0_attn_W_out"]).T)
    slot = np.asarray(inputs["L0_ffn_slot_query"]).reshape(SLOTS, D)
    arrays["slot"] = np.ascontiguousarray(slot)
    arrays["slotT"] = np.ascontiguousarray(slot.T)
    arrays["d_WkT"] = np.ascontiguousarray(np.asarray(inputs["L0_ffn_d_Wk"]).T)
    arrays["c_WqT"] = np.ascontiguousarray(np.asarray(inputs["L0_ffn_c_Wq"]).T)

    arrays["conv_w"] = np.ascontiguousarray(arrays["conv_w"].reshape(CT, P, TAPS).transpose(1, 0, 2))
    for name in ("conv_b", "q_b", "k_b", "d_bq", "d_bk", "d_bv", "c_bq", "c_bk", "c_bv"):
        arrays[name] = np.ascontiguousarray(arrays[name].reshape(-1, P).T)

    nc = bacc.Bacc("TRN2", target_bir_lowering=False, num_devices=1)
    io = {name: nc.dram_tensor(f"in_{name}", a.shape, F32, kind="ExternalInput").ap() for name, a in arrays.items()}
    io["out"] = nc.dram_tensor("out", [TOKENS, D], F32, kind="ExternalOutput").ap()
    io["x1"] = nc.dram_tensor("scratch_x1", [TOKENS, D], F32).ap()
    io["x2"] = nc.dram_tensor("scratch_x2", [TOKENS, D], F32).ap()
    io["x2T"] = nc.dram_tensor("scratch_x2T", [TOKENS, D], F32).ap()
    decoder_layer(nc, io)
    got = run_bass_kernel_spmd(nc, [{f"in_{name}": a for name, a in arrays.items()}], core_ids=[0])
    return got.results[0]["out"].reshape(BATCH, SEQ, D)
```
